# Optimizing a Trainium2 kernel written in Bass

```python
import numpy as np
import jax
import jax.numpy as jnp

def _softmax(x, axis=-1):
    return jax.nn.softmax(x, axis=axis)

def _gelu(x):
    return jax.nn.gelu(x, approximate=True)

def _silu(x):
    return jax.nn.silu(x)

def _sigmoid(x):
    return jax.nn.sigmoid(x)

def _layernorm(x, axis=-1, eps=1e-05):
    m = jnp.mean(x, axis=axis, keepdims=True)
    v = jnp.var(x, axis=axis, keepdims=True)
    return (x - m) / jnp.sqrt(v + eps)

def _scatter_add(tgt, idx, src, axis=0):
    return tgt.at[idx].add(src)

def _segment_sum(src, seg, n):
    return jax.ops.segment_sum(src, seg, n)
kernel_name = 'mk_xattn_ffn_d2_seqx_r4_04dcb5'

def setup_inputs(seed: int=0):
    np.random.seed(seed)
    _w = jnp.asarray

    def _rec_inputs():
        import jax
        import jax.numpy as jnp
        _rk = jax.random.key(seed)
        x = 7.22e-05 + 1 * jax.random.normal(jax.random.fold_in(_rk, 1), (1, 2048, 256), jnp.float32)
        _lenS = 2048 - jax.random.randint(jax.random.fold_in(_rk, 7), (1,), 0, max(1, 2048 // 4) + 1, jnp.int32)
        _lenS2 = 1601 - jax.random.randint(jax.random.fold_in(_rk, 8), (1,), 0, max(1, 1601 // 4) + 1, jnp.int32)
        _ctx_768P = jax.random.normal(jax.random.fold_in(_rk, 11), (1, 16, 192), jnp.float32)
        _ctx_768c = jax.random.dirichlet(jax.random.fold_in(_rk, 511), 0.3 * jnp.ones((16,), jnp.float32), (1, 1601))
        _ctx_768t = jnp.einsum('bsk,bkd->bsd', _ctx_768c, _ctx_768P)
        _ctx_768t = _ctx_768t * jax.lax.rsqrt(jnp.mean(jnp.square(_ctx_768t)) + 1e-12) * 0.953939
        ctx_768 = -0.000191848 + 0.999787 * (_ctx_768t + 0.3 * jax.random.normal(jax.random.fold_in(_rk, 611), (1, 1601, 192), jnp.float32))
        return (x, ctx_768)
    x, ctx_768 = _rec_inputs()

    def _L0_xattn_setup():
        import jax, jax.numpy as jnp
        import numpy as np
        HEADS = 8
        DIM_HEAD = 64
        SCALE = DIM_HEAD ** (-0.5)
        key = jax.random.key(seed)
        ks = jax.random.split(key, 7)
        B, Nq, Nc = (4, 512, 512)
        Dq, Dc = (256, 192)
        inner = HEADS * DIM_HEAD
        x = jax.random.normal(ks[0], (B, Nq, Dq), dtype=jnp.float32)
        context = jax.random.normal(ks[1], (B, Nc, Dc), dtype=jnp.float32)
        Wq = jax.random.normal(ks[2], (Dq, inner), dtype=jnp.float32) * Dq ** (-0.5)
        Wk = jax.random.normal(ks[3], (Dc, inner), dtype=jnp.float32) * Dc ** (-0.5)
        Wv = jax.random.normal(ks[4], (Dc, inner), dtype=jnp.float32) * Dc ** (-0.5)
        Wo = jax.random.normal(ks[5], (inner, Dq), dtype=jnp.float32) * inner ** (-0.5)
        bo = jax.random.normal(ks[6], (Dq,), dtype=jnp.float32) * 0.01
        return {'x': x, 'context': context, 'Wq': Wq, 'Wk': Wk, 'Wv': Wv, 'Wo': Wo, 'bo': bo}
    _L0_xattn_all = _L0_xattn_setup()
    _L0_xattn_in = {k: v for k, v in _L0_xattn_all.items() if k in ('Wq', 'Wk', 'Wv', 'Wo', 'bo')}
    del _L0_xattn_all

    def _L0_ffn_setup():
        import jax, jax.numpy as jnp
        import numpy as np
        D_MODEL = 256
        EXPANSION = 4
        D_HIDDEN = D_MODEL * EXPANSION
        NUM_STAGES = int(np.log2(D_HIDDEN))

        def butterfly(y, weights, dim):
            lead = y.shape[:-1]
            for stage in range(weights.shape[0]):
                s = 2 ** stage
                nb = dim // (2 * s)
                yr = y.reshape(*lead, nb, 2, s)
                a = yr[..., 0, :]
                b = yr[..., 1, :]
                w = weights[stage].reshape(nb, s, 2, 2)
                na = w[..., 0, 0] * a + w[..., 0, 1] * b
                nb2 = w[..., 1, 0] * a + w[..., 1, 1] * b
                y = jnp.stack([na, nb2], axis=-2).reshape(*lead, dim)
            return y
        key = jax.random.key(seed)
        ks = jax.random.split(key, 6)
        B, S = (4, 512)
        x = jax.random.normal(ks[0], (B, S, D_MODEL), jnp.float32)
        W_exp = jax.random.normal(ks[1], (D_MODEL, D_HIDDEN), jnp.float32) * 0.02
        b_exp = jnp.zeros((D_HIDDEN,), jnp.float32)
        up_weights = jax.random.normal(ks[2], (NUM_STAGES, D_HIDDEN // 2, 2, 2), jnp.float32) * 0.02
        up_bias = jnp.zeros((D_HIDDEN,), jnp.float32)
        down_weights = jax.random.normal(ks[3], (NUM_STAGES, D_HIDDEN // 2, 2, 2), jnp.float32) * 0.02
        W_con = jax.random.normal(ks[4], (D_HIDDEN, D_MODEL), jnp.float32) * 0.02
        b_con = jnp.zeros((D_MODEL,), jnp.float32)
        down_bias = jnp.zeros((D_MODEL,), jnp.float32)
        return dict(x=x, W_exp=W_exp, b_exp=b_exp, up_weights=up_weights, up_bias=up_bias, down_weights=down_weights, W_con=W_con, b_con=b_con, down_bias=down_bias)
    _L0_ffn_all = _L0_ffn_setup()
    _L0_ffn_in = {k: v for k, v in _L0_ffn_all.items() if k in ('W_exp', 'b_exp', 'up_weights', 'up_bias', 'down_weights', 'W_con', 'b_con', 'down_bias')}
    del _L0_ffn_all

    def _L1_xattn_setup():
        import jax, jax.numpy as jnp
        import numpy as np
        HEADS = 8
        DIM_HEAD = 64
        SCALE = DIM_HEAD ** (-0.5)
        key = jax.random.key(seed)
        ks = jax.random.split(key, 7)
        b, n, m = (4, 512, 256)
        qd, cd, inner = (256, 192, HEADS * DIM_HEAD)
        s = lambda fan_in: 1.0 / np.sqrt(fan_in)
        return {'x': jax.random.normal(ks[0], (b, n, qd), jnp.float32), 'context': jax.random.normal(ks[1], (b, m, cd), jnp.float32), 'Wq': jax.random.normal(ks[2], (qd, inner), jnp.float32) * s(qd), 'Wk': jax.random.normal(ks[3], (cd, inner), jnp.float32) * s(cd), 'Wv': jax.random.normal(ks[4], (cd, inner), jnp.float32) * s(cd), 'Wout': jax.random.normal(ks[5], (inner, qd), jnp.float32) * s(inner), 'bout': jax.random.normal(ks[6], (qd,), jnp.float32) * 0.01}
    _L1_xattn_all = _L1_xattn_setup()
    _L1_xattn_in = {k: v for k, v in _L1_xattn_all.items() if k in ('Wq', 'Wk', 'Wv', 'Wout', 'bout')}
    del _L1_xattn_all

    def _L1_ffn_setup():
        import jax, jax.numpy as jnp
        import numpy as np
        DIM = 256
        DEPTH = 2
        HEADS = 8
        DIM_HEAD = 64
        WINDOW = 128
        INNER = HEADS * DIM_HEAD
        HID = int(DIM * 4 * 2 / 3)
        B, N = (2, 2048)
        QK_SCALE = 8.0

        def shift_token(t):
            t1, t2 = jnp.split(t, 2, axis=-1)
            t2 = jnp.pad(t2, ((0, 0), (1, 0), (0, 0)))[:, :-1]
            return jnp.concatenate([t1, t2], axis=-1)

        def l2norm(t):
            return t / jnp.clip(jnp.linalg.norm(t, axis=-1, keepdims=True), 1e-12)

        def rotate_half(x):
            x1, x2 = jnp.split(x, 2, axis=-1)
            return jnp.concatenate([-x2, x1], axis=-1)

        def rotary_xpos(q, k):
            n = q.shape[-2]
            half_idx = jnp.arange(0, DIM_HEAD, 2, dtype=jnp.float32)
            inv_freq = 1.0 / 10000.0 ** (half_idx / DIM_HEAD)
            t = jnp.arange(n, dtype=jnp.float32)
            freqs = t[:, None] * inv_freq[None, :]
            freqs = jnp.concatenate([freqs, freqs], axis=-1)
            base = (half_idx + 0.4 * DIM_HEAD) / (1.4 * DIM_HEAD)
            power = (t - n // 2) / float(WINDOW // 2)
            scale = base[None, :] ** power[:, None]
            scale = jnp.concatenate([scale, scale], axis=-1)
            cos, sin = (jnp.cos(freqs), jnp.sin(freqs))
            q = q * cos * scale + rotate_half(q) * sin * scale
            k = k * cos / scale + rotate_half(k) * sin / scale
            return (q, k)

        def local_attention(q, k, v):
            b, h, n, d = q.shape
            w = n // WINDOW
            bq = q.reshape(b, h, w, WINDOW, d) * QK_SCALE
            bk = k.reshape(b, h, w, WINDOW, d)
            bv = v.reshape(b, h, w, WINDOW, d)

            def look_around(t):
                p = jnp.pad(t, ((0, 0), (0, 0), (1, 0), (0, 0), (0, 0)))
                return jnp.concatenate([p[:, :, :w], p[:, :, 1:]], axis=3)
            bk, bv = (look_around(bk), look_around(bv))
            bt = jnp.arange(n).reshape(w, WINDOW)
            btp = jnp.pad(bt, ((1, 0), (0, 0)), constant_values=-1)
            btk = jnp.concatenate([btp[:w], btp[1:]], axis=1)
            sim = jnp.einsum('bhwid,bhwjd->bhwij', bq, bk)
            i = bt[:, :, None]
            j = btk[:, None, :]
            mask = (i < j) | (i > j + WINDOW) | (j == -1)
            sim = jnp.where(mask, -jnp.finfo(sim.dtype).max, sim)
            attn = jax.nn.softmax(sim, axis=-1)
            out = jnp.einsum('bhwij,bhwjd->bhwid', attn, bv)
            return out.reshape(b, h, n, d)

        def _layer(x, wqkv, qs, ksc, wo, lg, lb, w1, b1, w2, b2):
            b, n, _ = x.shape
            h = shift_token(x)
            qkv = h @ wqkv
            q, k, v = jnp.split(qkv, 3, axis=-1)
            to_heads = lambda t: t.reshape(b, n, HEADS, DIM_HEAD).transpose(0, 2, 1, 3)
            q, k, v = (to_heads(q), to_heads(k), to_heads(v))
            q = l2norm(q) * qs
            k = l2norm(k) * ksc
            q, k = rotary_xpos(q, k)
            o = local_attention(q, k, v)
            o = o.transpose(0, 2, 1, 3).reshape(b, n, INNER)
            x = x + o @ wo
            h = shift_token(x)
            mu = h.mean(-1, keepdims=True)
            var = h.var(-1, keepdims=True)
            h = (h - mu) / jnp.sqrt(var + 1e-05) * lg + lb
            h = h @ w1 + b1
            a, g = jnp.split(h, 2, axis=-1)
            h = a * jax.nn.gelu(g, approximate=False)
            x = x + h @ w2 + b2
            return x
        key = jax.random.key(seed)
        ks = jax.random.split(key, 6)
        return {'x': jax.random.normal(ks[0], (B, N, DIM), jnp.float32), 'wqkv': jax.random.normal(ks[1], (DEPTH, DIM, 3 * INNER), jnp.float32) * 0.02, 'q_scale': jnp.ones((DEPTH, DIM_HEAD), jnp.float32), 'k_scale': jnp.ones((DEPTH, DIM_HEAD), jnp.float32), 'wo': jax.random.normal(ks[2], (DEPTH, INNER, DIM), jnp.float32) * 0.02, 'ln_g': jnp.ones((DEPTH, DIM), jnp.float32), 'ln_b': jnp.zeros((DEPTH, DIM), jnp.float32), 'w1': jax.random.normal(ks[3], (DEPTH, DIM, 2 * HID), jnp.float32) * 0.02, 'b1': jnp.zeros((DEPTH, 2 * HID), jnp.float32), 'w2': jax.random.normal(ks[4], (DEPTH, HID, DIM), jnp.float32) * 0.02, 'b2': jnp.zeros((DEPTH, DIM), jnp.float32)}
    _L1_ffn_all = _L1_ffn_setup()
    _L1_ffn_in = {k: v for k, v in _L1_ffn_all.items() if k in ('wqkv', 'q_scale', 'k_scale', 'wo', 'ln_g', 'ln_b', 'w1', 'b1', 'w2', 'b2')}
    del _L1_ffn_all
    return {'x': x, 'ctx_768': ctx_768, 'L0_xattn_Wq': _L0_xattn_in['Wq'], 'L0_xattn_Wk': _L0_xattn_in['Wk'], 'L0_xattn_Wv': _L0_xattn_in['Wv'], 'L0_xattn_Wo': _L0_xattn_in['Wo'], 'L0_xattn_bo': _L0_xattn_in['bo'], 'L0_ffn_W_exp': _L0_ffn_in['W_exp'], 'L0_ffn_b_exp': _L0_ffn_in['b_exp'], 'L0_ffn_up_weights': _L0_ffn_in['up_weights'], 'L0_ffn_up_bias': _L0_ffn_in['up_bias'], 'L0_ffn_down_weights': _L0_ffn_in['down_weights'], 'L0_ffn_W_con': _L0_ffn_in['W_con'], 'L0_ffn_b_con': _L0_ffn_in['b_con'], 'L0_ffn_down_bias': _L0_ffn_in['down_bias'], 'L1_xattn_Wq': _L1_xattn_in['Wq'], 'L1_xattn_Wk': _L1_xattn_in['Wk'], 'L1_xattn_Wv': _L1_xattn_in['Wv'], 'L1_xattn_Wout': _L1_xattn_in['Wout'], 'L1_xattn_bout': _L1_xattn_in['bout'], 'L1_ffn_wqkv': _L1_ffn_in['wqkv'], 'L1_ffn_q_scale': _L1_ffn_in['q_scale'], 'L1_ffn_k_scale': _L1_ffn_in['k_scale'], 'L1_ffn_wo': _L1_ffn_in['wo'], 'L1_ffn_ln_g': _L1_ffn_in['ln_g'], 'L1_ffn_ln_b': _L1_ffn_in['ln_b'], 'L1_ffn_w1': _L1_ffn_in['w1'], 'L1_ffn_b1': _L1_ffn_in['b1'], 'L1_ffn_w2': _L1_ffn_in['w2'], 'L1_ffn_b2': _L1_ffn_in['b2']}

def reference(x, ctx_768, L0_xattn_Wq, L0_xattn_Wk, L0_xattn_Wv, L0_xattn_Wo, L0_xattn_bo, L0_ffn_W_exp, L0_ffn_b_exp, L0_ffn_up_weights, L0_ffn_up_bias, L0_ffn_down_weights, L0_ffn_W_con, L0_ffn_b_con, L0_ffn_down_bias, L1_xattn_Wq, L1_xattn_Wk, L1_xattn_Wv, L1_xattn_Wout, L1_xattn_bout, L1_ffn_wqkv, L1_ffn_q_scale, L1_ffn_k_scale, L1_ffn_wo, L1_ffn_ln_g, L1_ffn_ln_b, L1_ffn_w1, L1_ffn_b1, L1_ffn_w2, L1_ffn_b2):
    import jax
    import jax.numpy as jnp

    def _L0_xattn_ref(x, context, Wq, Wk, Wv, Wo, bo):
        import jax, jax.numpy as jnp
        import numpy as np
        HEADS = 8
        DIM_HEAD = 64
        SCALE = DIM_HEAD ** (-0.5)
        B, Nq, _ = x.shape
        q = (x @ Wq).reshape(B, Nq, HEADS, DIM_HEAD)
        k = (context @ Wk).reshape(B, context.shape[1], HEADS, DIM_HEAD)
        v = (context @ Wv).reshape(B, context.shape[1], HEADS, DIM_HEAD)
        sim = jnp.einsum('bihd,bjhd->bhij', q, k) * SCALE
        attn = jax.nn.softmax(sim, axis=-1)
        out = jnp.einsum('bhij,bjhd->bihd', attn, v)
        out = out.reshape(B, Nq, HEADS * DIM_HEAD)
        return out @ Wo + bo

    def _L0_ffn_ref(x, W_exp, b_exp, up_weights, up_bias, down_weights, W_con, b_con, down_bias):
        import jax, jax.numpy as jnp
        import numpy as np
        D_MODEL = 256
        EXPANSION = 4
        D_HIDDEN = D_MODEL * EXPANSION
        NUM_STAGES = int(np.log2(D_HIDDEN))

        def butterfly(y, weights, dim):
            lead = y.shape[:-1]
            for stage in range(weights.shape[0]):
                s = 2 ** stage
                nb = dim // (2 * s)
                yr = y.reshape(*lead, nb, 2, s)
                a = yr[..., 0, :]
                b = yr[..., 1, :]
                w = weights[stage].reshape(nb, s, 2, 2)
                na = w[..., 0, 0] * a + w[..., 0, 1] * b
                nb2 = w[..., 1, 0] * a + w[..., 1, 1] * b
                y = jnp.stack([na, nb2], axis=-2).reshape(*lead, dim)
            return y
        h = jnp.einsum('bsd,dh->bsh', x, W_exp) + b_exp
        h = butterfly(h, up_weights, D_HIDDEN)
        h = jax.nn.gelu(h + up_bias, approximate=False)
        h = butterfly(h, down_weights, D_HIDDEN)
        y = jnp.einsum('bsh,hd->bsd', h, W_con) + b_con
        return y + down_bias

    def _L1_xattn_ref(x, context, Wq, Wk, Wv, Wout, bout):
        import jax, jax.numpy as jnp
        import numpy as np
        HEADS = 8
        DIM_HEAD = 64
        SCALE = DIM_HEAD ** (-0.5)
        b, n, _ = x.shape
        m = context.shape[1]
        q = (x @ Wq).reshape(b, n, HEADS, DIM_HEAD)
        k = (context @ Wk).reshape(b, m, HEADS, DIM_HEAD)
        v = (context @ Wv).reshape(b, m, HEADS, DIM_HEAD)
        sim = jnp.einsum('bihd,bjhd->bhij', q, k) * SCALE
        attn = jax.nn.softmax(sim, axis=-1)
        out = jnp.einsum('bhij,bjhd->bihd', attn, v).reshape(b, n, HEADS * DIM_HEAD)
        return out @ Wout + bout

    def _L1_ffn_ref(x, wqkv, q_scale, k_scale, wo, ln_g, ln_b, w1, b1, w2, b2):
        import jax, jax.numpy as jnp
        import numpy as np
        DIM = 256
        DEPTH = 2
        HEADS = 8
        DIM_HEAD = 64
        WINDOW = 128
        INNER = HEADS * DIM_HEAD
        HID = int(DIM * 4 * 2 / 3)
        B, N = (2, 2048)
        QK_SCALE = 8.0

        def shift_token(t):
            t1, t2 = jnp.split(t, 2, axis=-1)
            t2 = jnp.pad(t2, ((0, 0), (1, 0), (0, 0)))[:, :-1]
            return jnp.concatenate([t1, t2], axis=-1)

        def l2norm(t):
            return t / jnp.clip(jnp.linalg.norm(t, axis=-1, keepdims=True), 1e-12)

        def rotate_half(x):
            x1, x2 = jnp.split(x, 2, axis=-1)
            return jnp.concatenate([-x2, x1], axis=-1)

        def rotary_xpos(q, k):
            n = q.shape[-2]
            half_idx = jnp.arange(0, DIM_HEAD, 2, dtype=jnp.float32)
            inv_freq = 1.0 / 10000.0 ** (half_idx / DIM_HEAD)
            t = jnp.arange(n, dtype=jnp.float32)
            freqs = t[:, None] * inv_freq[None, :]
            freqs = jnp.concatenate([freqs, freqs], axis=-1)
            base = (half_idx + 0.4 * DIM_HEAD) / (1.4 * DIM_HEAD)
            power = (t - n // 2) / float(WINDOW // 2)
            scale = base[None, :] ** power[:, None]
            scale = jnp.concatenate([scale, scale], axis=-1)
            cos, sin = (jnp.cos(freqs), jnp.sin(freqs))
            q = q * cos * scale + rotate_half(q) * sin * scale
            k = k * cos / scale + rotate_half(k) * sin / scale
            return (q, k)

        def local_attention(q, k, v):
            b, h, n, d = q.shape
            w = n // WINDOW
            bq = q.reshape(b, h, w, WINDOW, d) * QK_SCALE
            bk = k.reshape(b, h, w, WINDOW, d)
            bv = v.reshape(b, h, w, WINDOW, d)

            def look_around(t):
                p = jnp.pad(t, ((0, 0), (0, 0), (1, 0), (0, 0), (0, 0)))
                return jnp.concatenate([p[:, :, :w], p[:, :, 1:]], axis=3)
            bk, bv = (look_around(bk), look_around(bv))
            bt = jnp.arange(n).reshape(w, WINDOW)
            btp = jnp.pad(bt, ((1, 0), (0, 0)), constant_values=-1)
            btk = jnp.concatenate([btp[:w], btp[1:]], axis=1)
            sim = jnp.einsum('bhwid,bhwjd->bhwij', bq, bk)
            i = bt[:, :, None]
            j = btk[:, None, :]
            mask = (i < j) | (i > j + WINDOW) | (j == -1)
            sim = jnp.where(mask, -jnp.finfo(sim.dtype).max, sim)
            attn = jax.nn.softmax(sim, axis=-1)
            out = jnp.einsum('bhwij,bhwjd->bhwid', attn, bv)
            return out.reshape(b, h, n, d)

        def _layer(x, wqkv, qs, ksc, wo, lg, lb, w1, b1, w2, b2):
            b, n, _ = x.shape
            h = shift_token(x)
            qkv = h @ wqkv
            q, k, v = jnp.split(qkv, 3, axis=-1)
            to_heads = lambda t: t.reshape(b, n, HEADS, DIM_HEAD).transpose(0, 2, 1, 3)
            q, k, v = (to_heads(q), to_heads(k), to_heads(v))
            q = l2norm(q) * qs
            k = l2norm(k) * ksc
            q, k = rotary_xpos(q, k)
            o = local_attention(q, k, v)
            o = o.transpose(0, 2, 1, 3).reshape(b, n, INNER)
            x = x + o @ wo
            h = shift_token(x)
            mu = h.mean(-1, keepdims=True)
            var = h.var(-1, keepdims=True)
            h = (h - mu) / jnp.sqrt(var + 1e-05) * lg + lb
            h = h @ w1 + b1
            a, g = jnp.split(h, 2, axis=-1)
            h = a * jax.nn.gelu(g, approximate=False)
            x = x + h @ w2 + b2
            return x
        for l in range(DEPTH):
            x = _layer(x, wqkv[l], q_scale[l], k_scale[l], wo[l], ln_g[l], ln_b[l], w1[l], b1[l], w2[l], b2[l])
        return x
    x = x + _L0_xattn_ref(_layernorm(x, axis=-1), ctx_768, L0_xattn_Wq, L0_xattn_Wk, L0_xattn_Wv, L0_xattn_Wo, L0_xattn_bo)
    x = x + _L0_ffn_ref(_layernorm(x, axis=-1), L0_ffn_W_exp, L0_ffn_b_exp, L0_ffn_up_weights, L0_ffn_up_bias, L0_ffn_down_weights, L0_ffn_W_con, L0_ffn_b_con, L0_ffn_down_bias)
    x = x + _L1_xattn_ref(_layernorm(x, axis=-1), ctx_768, L1_xattn_Wq, L1_xattn_Wk, L1_xattn_Wv, L1_xattn_Wout, L1_xattn_bout)
    x = x + _L1_ffn_ref(_layernorm(x, axis=-1), L1_ffn_wqkv, L1_ffn_q_scale, L1_ffn_k_scale, L1_ffn_wo, L1_ffn_ln_g, L1_ffn_ln_b, L1_ffn_w1, L1_ffn_b1, L1_ffn_w2, L1_ffn_b2)
    return x

_drawn_inputs = setup_inputs


def setup_inputs(seed=0):
    import zlib

    import numpy as np

    out = dict(_drawn_inputs(seed))
    spreads = {'L0_ffn_b_exp': (0.0, 0.1),
     'L0_ffn_up_bias': (0.0, 0.1),
     'L0_ffn_b_con': (0.0, 0.1),
     'L0_ffn_down_bias': (0.0, 0.1),
     'L1_ffn_q_scale': (1.0, 0.6),
     'L1_ffn_k_scale': (1.0, 0.6),
     'L1_ffn_ln_g': (1.0, 0.6),
     'L1_ffn_ln_b': (0.0, 0.8),
     'L1_ffn_b1': (0.0, 0.8),
     'L1_ffn_b2': (0.0, 0.1)}
    factors = {'L0_xattn_bo': 7.503, 'L1_xattn_bout': 7.797, 'L1_ffn_w1': 2.814, 'L1_ffn_w2': 2.809}
    for name, (base, spread) in spreads.items():
        noise = np.random.default_rng([zlib.crc32(name.encode()), seed]).standard_normal(out[name].shape)
        drawn = base * np.exp(spread * noise) if base else spread * noise
        out[name] = jnp.asarray(drawn.astype(out[name].dtype))
    for name, factor in factors.items():
        out[name] = (out[name] * factor).astype(out[name].dtype)
    return out
```

```python
import numpy as np
import concourse.bass as bass
from concourse import mybir
from contextlib import ExitStack

F32 = mybir.dt.float32
F32R = mybir.dt.float32r
BF16 = mybir.dt.bfloat16
ALU = mybir.AluOpType
ACT = mybir.ActivationFunctionType
AX = mybir.AxisListType

P = 128
NQ = 2048
D = 256
DT = D // P
NC_ = 1601
DC = 192
HEADS, DH = 8, 64
INNER = HEADS * DH
PAIRS = HEADS // 2
CH = 512
NCH = NQ // CH
KT = -(-NC_ // P)
LASTK = NC_ - (KT - 1) * P
EPS = 1e-5
HID0 = 4 * D
HT0 = HID0 // P
STAGES = 10
HID1 = D * 4 * 2 // 3
HT1 = -(-HID1 // P)
LASTH = HID1 - (HT1 - 1) * P
WIN = 128
NEG = -1e30


def key_rows(t):
    return P if t < KT - 1 else LASTK


def hid_rows(j):
    return P if j < HT1 - 1 else LASTH


class Scope:

    def __init__(self, nc, tag):
        self.nc, self.tag, self.stack, self.sems = nc, tag, ExitStack(), []

    def __enter__(self):
        return self

    def __exit__(self, *a):
        self.stack.close()
        if self.sems:
            self.nc.clear_and_free_semaphores(self.sems)
            self.nc.all_engine_barrier()

    def sb(self, name, shape, dt=F32):
        return self.stack.enter_context(self.nc.sbuf_tensor(f"{self.tag}_{name}", shape, dt))

    def ps(self, name, shape, dt=F32):
        return self.stack.enter_context(self.nc.psum_tensor(f"{self.tag}_{name}", shape, dt))

    def sem(self, name):
        self.sems.append(self.nc.alloc_semaphore(f"{self.tag}_{name}"))
        return self.sems[-1]

    def block(self):
        return self.stack.enter_context(self.nc.Block())



def load_phase(nc, x, ctx, ident, ones_mean, ones64, eps, resid, ctx_t):
    xv = x.rearrange("b (t p) d -> p (b t) d", p=P)
    TX = NQ // P
    with Scope(nc, "load") as s:
        xin = s.sb("xin", [P, TX, D])
        cin = s.sb("cin", [P, KT, DC])
        tp = s.ps("tp", [P, 4, 4, P])
        consts = s.sem("consts")
        ident_zero = s.sem("ident_zero")
        x_in = [s.sem(f"x_in{i}") for i in range(4)]
        c_in = s.sem("c_in")
        turned = s.sem("turned")
        taken = s.sem("taken")
        groups = []
        for g in range(TX // 4):
            for k in range(DT):
                groups.append(("x", k, P, [(4 * g + j, P) for j in range(4)]))
        for g in range(-(-KT // 4)):
            for k, rows in ((0, P), (1, DC - P)):
                groups.append(("c", k, rows, [(t, key_rows(t)) for t in range(4 * g, min(4 * g + 4, KT))]))
        block = s.block()

        @block.sync
        def _(sp):
            for i in range(4):
                sp.dma_start(xin[:, 4 * i:4 * i + 4, :], xv[:, 4 * i:4 * i + 4, :]).then_inc(x_in[i], 16)

        @block.gpsimd
        def _(pool):
            pool.memset(ident[:, :], 0.0).then_inc(ident_zero, 1)
            pool.memset(ones_mean[:, :], 1.0 / D).then_inc(consts, 1)
            pool.memset(ones64[:, :], 1.0).then_inc(consts, 1)
            pool.memset(eps[:, :], EPS).then_inc(consts, 1)
            pool.wait_ge(ident_zero, 1)
            pool.affine_select(out=ident[:, :], in_=ident[:, :], compare_op=ALU.not_equal, fill=1.0,
                               base=0, pattern=[[-1, P]], channel_multiplier=1).then_inc(consts, 1)

        @block.tensor
        def _(pe):
            pe.wait_ge(consts, 4)
            for n, (src, k, rows, tiles) in enumerate(groups):
                if src == "x":
                    pe.wait_ge(x_in[tiles[0][0] // 4], 16)
                else:
                    pe.wait_ge(c_in, 32)
                if n >= 4:
                    pe.wait_ge(taken, n - 3)
                for j, (t, toks) in enumerate(tiles):
                    a = xin[:, t, k * P:k * P + rows] if src == "x" else cin[0:toks, t, k * P:k * P + rows]
                    last = pe.transpose(tp[0:rows, n % 4, j, 0:toks], a, ident[0:toks, 0:toks])
                last.then_inc(turned, 1)

        @block.scalar
        def _(act):
            act.dma_start(cin[:, 0:KT - 1, :], ctx[0, 0:(KT - 1) * P, :].rearrange("(t p) d -> p t d", p=P)).then_inc(c_in, 16)
            act.dma_start(cin[0:LASTK, KT - 1, :], ctx[0, (KT - 1) * P:NC_, :]).then_inc(c_in, 16)

        @block.vector
        def _(dve):
            for n, (src, k, rows, tiles) in enumerate(groups):
                dve.wait_ge(turned, n + 1)
                t0, toks = tiles[0][0] * P, sum(m for _, m in tiles)
                dst = resid if src == "x" else ctx_t
                dve.tensor_copy(dst[0:rows, k, t0:t0 + toks],
                                tp[0:rows, n % 4, :, :].rearrange("p j q -> p (j q)")[:, 0:toks]).then_inc(taken, 1)



def norm_phase(nc, tag, src, dst, ones_mean, eps, also=None):
    with Scope(nc, tag) as s:
        sq = s.sb("sq", [P, 2, DT, CH])
        std = s.sb("std", [P, 2, CH])
        rstd = s.sb("rstd", [P, 2, CH])
        mean = s.ps("mean", [P, 2, CH])
        var = s.ps("var", [P, 2, CH])
        mean_done = s.sem("mean_done")
        centred = s.sem("centred")
        squared = s.sem("squared")
        var_done = s.sem("var_done")
        std_done = s.sem("std_done")
        rstd_done = s.sem("rstd_done")
        normed = s.sem("normed")
        block = s.block()

        def chunk(c):
            return slice(c * CH, (c + 1) * CH)

        @block.tensor
        def _(pe):
            def means(c):
                if c >= 2:
                    pe.wait_ge(centred, c - 1)
                for k in range(DT):
                    last = pe.matmul(mean[:, c % 2, :], ones_mean[:, :], src[:, k, chunk(c)],
                                     start=k == 0, stop=k == DT - 1)
                last.then_inc(mean_done, 1)

            def variances(c):
                pe.wait_ge(squared, c + 1)
                if c >= 2:
                    pe.wait_ge(std_done, c - 1)
                for k in range(DT):
                    last = pe.matmul(var[:, c % 2, :], ones_mean[:, :], sq[:, c % 2, k, :],
                                     start=k == 0, stop=k == DT - 1)
                last.then_inc(var_done, 1)

            means(0)
            for c in range(1, NCH):
                means(c)
                variances(c - 1)
            variances(NCH - 1)

        @block.scalar
        def _(act):
            for c in range(NCH):
                act.wait_ge(centred, c + 1)
                if c >= 2:
                    act.wait_ge(var_done, c - 1)
                act.activation(sq[:, c % 2, :, :], dst[:, :, chunk(c)], ACT.Square).then_inc(squared, 1)
                act.wait_ge(var_done, c + 1)
                if c >= 2:
                    act.wait_ge(rstd_done, c - 1)
                act.activation(std[:, c % 2, :], var[:, c % 2, :], ACT.Sqrt, bias=eps[:, 0:1]).then_inc(std_done, 1)

        @block.vector
        def _(dve):
            def centre(c):
                dve.wait_ge(mean_done, c + 1)
                dve.tensor_tensor(dst[:, :, chunk(c)], src[:, :, chunk(c)],
                                  mean[:, c % 2:c % 2 + 1, :].broadcast_to([P, DT, CH]), ALU.subtract).then_inc(centred, 1)

            def scale(c):
                dve.wait_ge(std_done, c + 1)
                if c >= 2:
                    dve.wait_ge(normed, c - 1)
                dve.reciprocal(rstd[:, c % 2, :], std[:, c % 2, :]).then_inc(rstd_done, 1)
                dve.wait_ge(rstd_done, c + 1)
                dve.wait_ge(squared, c + 1)
                dve.tensor_tensor(dst[:, :, chunk(c)], dst[:, :, chunk(c)],
                                  rstd[:, c % 2:c % 2 + 1, :].broadcast_to([P, DT, CH]), ALU.mult).then_inc(normed, 1)

            centre(0)
            for c in range(1, NCH):
                centre(c)
                scale(c - 1)
            scale(NCH - 1)



def values_phase(nc, tag, ctx_t, wv, v_dram):
    with Scope(nc, tag) as s:
        w = s.sb("w", [P, 2, INNER])
        v = s.sb("v", [P, KT, INNER])
        ps = s.ps("ps", [P, 4, INNER])
        w_in = s.sem("w_in")
        made = s.sem("made")
        copied = s.sem("copied")
        stored = s.sem("stored")
        block = s.block()

        @block.sync
        def _(sp):
            sp.dma_start(w[:, 0, :], wv[0:P, :]).then_inc(w_in, 16)
            sp.dma_start(w[0:DC - P, 1, :], wv[P:DC, :]).then_inc(w_in, 16)
            sp.wait_ge(copied, KT)
            full = (KT - 1) * P
            sp.dma_start(v_dram[0:full, :].rearrange("(t p) d -> p t d", p=P), v[:, 0:KT - 1, :]).then_inc(stored, 16)
            sp.dma_start(v_dram[full:NC_, :], v[0:LASTK, KT - 1, :]).then_inc(stored, 16)
            sp.wait_ge(stored, 32)

        @block.tensor
        def _(pe):
            pe.wait_ge(w_in, 32)
            for t in range(KT):
                n = key_rows(t)
                if t >= 4:
                    pe.wait_ge(copied, t - 3)
                pe.matmul(ps[0:n, t % 4, :], ctx_t[:, 0, t * P:t * P + n], w[:, 0, :], start=True, stop=False)
                pe.matmul(ps[0:n, t % 4, :], ctx_t[0:DC - P, 1, t * P:t * P + n], w[0:DC - P, 1, :],
                          start=False, stop=True).then_inc(made, 1)

        @block.scalar
        def _(act):
            for t in range(KT):
                n = key_rows(t)
                act.wait_ge(made, t + 1)
                act.activation(v[0:n, t, :], ps[0:n, t % 4, :], ACT.Copy).then_inc(copied, 1)


KCOLS = [(0, CH), (CH, CH), (2 * CH, CH), (3 * CH, NC_ - 3 * CH)]
MCOLS = [(0, CH), (CH, CH), (2 * CH, CH), (3 * CH - 1, NC_ - 3 * CH + 1)]
QT = NQ // P


def attention_order(now, nxt):
    side = []
    if nxt is not None:
        side = [("project", nxt, u, 0) for u in range(8)]
        for h in range(2):
            side += [("max", nxt, h, qt) for qt in range(QT)]
            side += [("shift", nxt, h, 0)]
    if now is None:
        return side
    out, steps = [], NCH * KT
    for i in range(steps + 2):
        if i < steps:
            out.append(("scores", now, i, 0))
        if i >= 2:
            out.append(("values", now, i - 2, 0))
            if (i - 2) % KT == KT - 1:
                out.append(("sums", now, (i - 2) // KT, 0))
        if side and i < 8:
            out.append(side.pop(0))
        elif side and i >= 9 and len(side) > (steps - 2 - i) * 34 // 42:
            out.append(side.pop(0))
    return out + side


def attention_phase(nc, tag, hn, ctx_t, wq, wk, v_dram, o_dram, ident, ones64):
    with Scope(nc, tag) as s:
        w = s.sb("w", [P, 2, 2, P])
        hi = s.sb("hi", [P, 2, CH], F32R)
        lo = s.sb("lo", [P, 2, CH], F32R)
        q_dup = [[s.sb(f"q_dup{b}{h}", [P, NQ], F32R) for h in range(2)] for b in range(2)]
        q_low = [[s.sb(f"q_low{b}{h}", [DH + 1, NQ], F32R) for h in range(2)] for b in range(2)]
        k_both = [[s.sb(f"k_both{b}{h}", [P, NC_ + 1], F32R) for h in range(2)] for b in range(2)]
        k_one = [[s.sb(f"k_one{b}{h}", [DH + 1, NC_ + 1], F32R) for h in range(2)] for b in range(2)]
        v = s.sb("v", [P, 2, KT, P])
        probs = s.sb("probs", [P, 3, 2, CH])
        psum_p = s.sb("psum_p", [P, 2, CH])
        rden = s.sb("rden", [P, CH])
        onorm = s.sb("onorm", [P, CH])
        mx = s.sb("mx", [P, QT, 4])
        negmax = s.sb("negmax", [P, QT])
        negmax_t = s.sb("negmax_t", [QT, P], F32R)
        st = s.ps("st", [P, 2, 2, CH])
        av = s.ps("av", [P, 2, CH])
        ring = s.ps("ring", [P, 2, CH])
        w_in = s.sem("w_in")
        v_in = [s.sem(f"v_in{i}") for i in range(2)]
        hi_done = s.sem("hi_done")
        spread = [s.sem(f"spread{i}") for i in range(2)]
        ring_full = s.sem("ring_full")
        ring_read = s.sem("ring_read")
        neg_done = s.sem("neg_done")
        shift_in = s.sem("shift_in")
        scored = s.sem("scored")
        exped = s.sem("exped")
        weighed = s.sem("weighed")
        summed = s.sem("summed")
        outed = s.sem("outed")
        stored = s.sem("stored")
        ones_set = s.sem("ones_set")
        block = s.block()

        stages = [(None, 0)] + [(p, p + 1 if p + 1 < PAIRS else None) for p in range(PAIRS)]
        order = [op for now, nxt in stages for op in attention_order(now, nxt)]
        STEPS = NCH * KT
        ring_at, n = {}, 0
        for op in order:
            ring_at[op] = n
            n += {"project": 1, "max": 4, "shift": 1, "sums": 1}.get(op[0], 0)

        def step(p, i):
            return p * STEPS + i, i // KT, i % KT

        def adds_through(p, i):
            return (p * NCH + i // KT) * (KT - 1) + max(i % KT, 1)

        @block.sync
        def _(sp):
            for kind, p, u, _ in order:
                r = ring_at[(kind, p, u, 0)] if kind != "max" else None
                if kind == "shift":
                    sp.wait_ge(ring_read, r + 1)
                    sp.dma_start(q_low[p % 2][u][DH:DH + 1, :].bitcast(F32).rearrange("a (t q) -> a t q", q=P),
                                 negmax_t[:, :].bitcast(F32)).then_inc(shift_in, 16)
                if kind == "sums":
                    sp.wait_ge(outed, p * NCH + u + 1)
                    sp.dma_start(o_dram[p * P:(p + 1) * P, u * CH:(u + 1) * CH], onorm[:, :]).then_inc(stored, 16)
                if kind == "project":
                    b, n = p % 2, 8 * p + u
                    if u == 0:
                        if p:
                            sp.wait_ge(ring_full, ring_at[("project", p - 1, 7, 0)] + 1)
                        cols = slice(p * P, (p + 1) * P)
                        sp.dma_start(w[:, 0, 0, :], wk[0:P, cols]).then_inc(w_in, 16)
                        sp.dma_start(w[0:DC - P, 1, 0, :], wk[P:DC, cols]).then_inc(w_in, 16)
                        sp.dma_start(w[:, :, 1, :], wq[:, cols].rearrange("(k p) d -> p k d", p=P)).then_inc(w_in, 16)
                        if p >= 2:
                            sp.wait_ge(weighed, STEPS * (p - 1))
                        full = (KT - 1) * P
                        sp.dma_start(v[:, b, 0:KT - 1, :], v_dram[0:full, cols].rearrange("(t p) d -> p t d", p=P)).then_inc(v_in[b], 16)
                        sp.dma_start(v[0:LASTK, b, KT - 1, :], v_dram[full:NC_, cols]).then_inc(v_in[b], 16)
                    sp.wait_ge(ring_read, r + 1)
                    c0, m = KCOLS[u] if u < 4 else ((u - 4) * CH, CH)
                    for h in range(2):
                        h_hi, h_lo = hi[h * DH:(h + 1) * DH, n % 2, 0:m], lo[h * DH:(h + 1) * DH, n % 2, 0:m]
                        if u < 4:
                            to = ((k_both[b][h][0:DH], h_hi), (k_both[b][h][DH:P], h_lo), (k_one[b][h][0:DH], h_hi))
                        else:
                            to = ((q_dup[b][h][0:DH], h_hi), (q_dup[b][h][DH:P], h_hi), (q_low[b][h][0:DH], h_lo))
                        for dst, src in to:
                            sp.dma_start(dst[:, c0:c0 + m].bitcast(F32), src.bitcast(F32)).then_inc(spread[n % 2], 16)
            sp.wait_ge(stored, 16 * PAIRS * NCH)

        @block.gpsimd
        def _(pool):
            for b in range(2):
                for h in range(2):
                    pool.memset(k_one[b][h][DH:DH + 1, :].bitcast(F32), 1.0).then_inc(ones_set, 1)
            for kind, p, u, _ in order:
                if kind == "scores":
                    n, c, t = step(p, u)
                    if t == 0:
                        continue
                    rows = key_rows(t)
                    pool.wait_ge(exped, n + 1)
                    if t == 1:
                        if p or c:
                            pool.wait_ge(ring_full, ring_at[("sums", *divmod(p * NCH + c - 1, NCH), 0)] + 1)
                        a = probs[:, (n - 1) % 3, :, :]
                    else:
                        pool.wait_ge(summed, adds_through(p, u) - 1)
                        a = psum_p[0:rows, :, :]
                    pool.tensor_tensor(psum_p[0:rows, :, :], probs[0:rows, n % 3, :, :], a[0:rows], ALU.add).then_inc(summed, 1)

        @block.scalar
        def _(act):
            for kind, p, u, _ in order:
                if kind == "scores":
                    n, c, t = step(p, u)
                    rows = key_rows(t)
                    act.wait_ge(scored, n + 1)
                    if n >= 3:
                        act.wait_ge(weighed, n - 2)
                        act.wait_ge(summed, adds_through(*divmod(n - 3, STEPS)))
                    act.activation(probs[0:rows, n % 3, :, :], st[0:rows, n % 2, :, :], ACT.Exp,
                                   scale=DH ** -0.5).then_inc(exped, 1)

        @block.vector
        def _(dve):
            for kind, p, u, t in order:
                op, b = (kind, p, u, t), p % 2
                r = ring_at[op]
                if kind == "project":
                    n, m = 8 * p + u, KCOLS[u][1] if u < 4 else CH
                    dve.wait_ge(ring_full, r + 1)
                    if n >= 2:
                        dve.wait_ge(spread[n % 2], 96 * (n // 2))
                    dve.tensor_copy(hi[:, n % 2, 0:m], ring[:, r % 2, 0:m]).then_inc(hi_done, 1)
                    dve.wait_ge(hi_done, n + 1)
                    dve.tensor_tensor(lo[:, n % 2, 0:m], ring[:, r % 2, 0:m], hi[:, n % 2, 0:m].bitcast(F32),
                                      ALU.subtract).then_inc(ring_read, 1)
                if kind == "max":
                    if t == 0 and (p or u):
                        dve.wait_ge(neg_done, 2 * (2 * p + u))
                    for j in range(4):
                        dve.wait_ge(ring_full, r + j + 1)
                        dve.reduce_max(mx[:, t, j:j + 1], ring[:, (r + j) % 2, 0:MCOLS[j][1]], AX.X).then_inc(ring_read, 1)
                if kind == "shift":
                    k = 2 * p + u
                    dve.wait_ge(ring_read, r)
                    if k:
                        dve.wait_ge(ring_full, ring_at[("shift", *divmod(k - 1, 2), 0)] + 1)
                    dve.reduce_max(negmax[:, :], mx[:, :, :], AX.X).then_inc(neg_done, 1)
                    dve.wait_ge(neg_done, 2 * k + 1)
                    dve.tensor_scalar(negmax[:, :], negmax[:, :], -1.0, None, ALU.mult).then_inc(neg_done, 1)
                    dve.wait_ge(ring_full, r + 1)
                    if k:
                        dve.wait_ge(shift_in, 16 * k)
                    dve.tensor_copy(negmax_t[:, :], ring[0:QT, r % 2, 0:P]).then_inc(ring_read, 1)
                if kind == "sums":
                    n = p * NCH + u
                    dve.wait_ge(ring_full, r + 1)
                    if n:
                        dve.wait_ge(outed, n)
                    dve.reciprocal(rden[:, :], ring[:, r % 2, :]).then_inc(ring_read, 1)
                    dve.wait_ge(ring_read, r + 1)
                    dve.wait_ge(weighed, p * STEPS + (u + 1) * KT)
                    if n:
                        dve.wait_ge(stored, 16 * n)
                    dve.tensor_tensor(onorm[:, :], av[:, n % 2, :], rden[:, :], ALU.mult).then_inc(outed, 1)

        @block.tensor
        def _(pe):
            pe.wait_ge(ones_set, 4)
            for kind, p, u, t in order:
                op, b = (kind, p, u, t), p % 2
                r = ring_at[op]

                def free(n):
                    if n >= 2:
                        pe.wait_ge(ring_read, n - 1)
                if kind == "project":
                    if u == 0:
                        pe.wait_ge(w_in, 48 * (p + 1))
                    free(r)
                    if u < 4:
                        c0, m = KCOLS[u]
                        pe.matmul(ring[:, r % 2, 0:m], w[:, 0, 0, :], ctx_t[:, 0, c0:c0 + m], start=True, stop=False)
                        last = pe.matmul(ring[:, r % 2, 0:m], w[0:DC - P, 1, 0, :], ctx_t[0:DC - P, 1, c0:c0 + m],
                                         start=False, stop=True)
                    else:
                        c0 = (u - 4) * CH
                        for k in range(DT):
                            last = pe.matmul(ring[:, r % 2, :], w[:, k, 1, :], hn[:, k, c0:c0 + CH],
                                             start=k == 0, stop=k == DT - 1)
                    last.then_inc(ring_full, 1)
                if kind == "max":
                    if u == 0 and t == 0:
                        for i in range(2):
                            pe.wait_ge(spread[i], 96 * 4 * (p + 1))
                    for j, (c0, m) in enumerate(MCOLS):
                        free(r + j)
                        pe.matmul(ring[:, (r + j) % 2, 0:m], q_dup[b][u][:, t * P:(t + 1) * P],
                                  k_both[b][u][:, c0:c0 + m], start=True, stop=True).then_inc(ring_full, 1)
                if kind == "shift":
                    free(r)
                    pe.wait_ge(neg_done, 2 * (2 * p + u + 1))
                    pe.transpose(ring[0:QT, r % 2, 0:P], negmax[:, :], ident[:, :]).then_inc(ring_full, 1)
                if kind == "scores":
                    n, c, kt = step(p, u)
                    rows, keys, qs = key_rows(kt), slice(kt * P, kt * P + key_rows(kt)), slice(c * CH, (c + 1) * CH)
                    if u == 0:
                        pe.wait_ge(shift_in, 32 * (p + 1))
                    if n >= 2:
                        pe.wait_ge(exped, n - 1)
                    for h in range(2):
                        pe.matmul(st[0:rows, n % 2, h, :], k_both[b][h][:, keys], q_dup[b][h][:, qs], start=True, stop=False)
                        last = pe.matmul(st[0:rows, n % 2, h, :], k_one[b][h][:, keys], q_low[b][h][:, qs],
                                         start=False, stop=True)
                    last.then_inc(scored, 1)
                if kind == "values":
                    n, c, kt = step(p, u)
                    rows, m = key_rows(kt), p * NCH + c
                    if u == 0:
                        pe.wait_ge(v_in[b], 32 * (p // 2 + 1))
                    pe.wait_ge(exped, n + 1)
                    if kt == 0 and m >= 2:
                        pe.wait_ge(outed, m - 1)
                    for h in range(2):
                        last = pe.matmul(av[h * DH:(h + 1) * DH, m % 2, :], v[0:rows, b, kt, h * DH:(h + 1) * DH],
                                         probs[0:rows, n % 3, h, :], start=kt == 0, stop=kt == KT - 1)
                    last.then_inc(weighed, 1)
                if kind == "sums":
                    free(r)
                    pe.wait_ge(summed, (p * NCH + u + 1) * (KT - 1))
                    for h in range(2):
                        last = pe.matmul(ring[h * DH:(h + 1) * DH, r % 2, :], ones64[:, :], psum_p[:, h, :],
                                         start=True, stop=True)
                    last.then_inc(ring_full, 1)


def output_phase(nc, tag, o_dram, wo, bo, resid):
    with Scope(nc, tag) as s:
        w = s.sb("w", [P, PAIRS, D])
        bias = s.sb("bias", [P, DT])
        o = s.sb("o", [P, PAIRS, NQ])
        ps = s.ps("ps", [P, 4, CH])
        w_in = s.sem("w_in")
        o_in = [s.sem(f"o_in{c}") for c in range(NCH)]
        made = s.sem("made")
        added = s.sem("added")
        block = s.block()

        @block.sync
        def _(sp):
            sp.dma_start(w[:, :, :], wo.rearrange("(k p) d -> p k d", p=P)).then_inc(w_in, 16)
            sp.dma_start(bias[:, :], bo.rearrange("(k p) -> p k", p=P), allow_slow_non_contiguous=True).then_inc(w_in, 16)
            for c in range(NCH):
                sp.dma_start(o[:, :, c * CH:(c + 1) * CH],
                             o_dram[:, c * CH:(c + 1) * CH].rearrange("(k p) q -> p k q", p=P)).then_inc(o_in[c], 16)

        @block.tensor
        def _(pe):
            pe.wait_ge(w_in, 32)
            for c in range(NCH):
                pe.wait_ge(o_in[c], 16)
                for m in range(DT):
                    n = DT * c + m
                    if n >= 4:
                        pe.wait_ge(added, n - 3)
                    for k in range(PAIRS):
                        last = pe.matmul(ps[:, n % 4, :], w[:, k, m * P:(m + 1) * P], o[:, k, c * CH:(c + 1) * CH],
                                         start=k == 0, stop=k == PAIRS - 1)
                    last.then_inc(made, 1)

        @block.vector
        def _(dve):
            for n in range(NCH * DT):
                c, m = divmod(n, DT)
                dve.wait_ge(made, n + 1)
                part = resid[:, m, c * CH:(c + 1) * CH]
                dve.scalar_tensor_tensor(part, ps[:, n % 4, :], bias[:, m:m + 1], part, ALU.add, ALU.add).then_inc(added, 1)



def butterfly_phase(nc, w_exp, b_exp, up_w, up_b, down_w, w_con, b_con, down_b, ident, w_up, b_up, w_down, b_out):
    HALF = HID0 // 2
    with Scope(nc, "fold") as s:
        up = [s.sb(f"up{i}", [P, DT, HID0]) for i in range(2)]
        down = [s.sb(f"down{i}", [P, DT, HID0]) for i in range(2)]
        row = [s.sb(f"row{i}", [1, HID0]) for i in range(2)]
        wb = [s.sb(f"wb{i}", [P, HALF * 4]) for i in range(4)]
        t_dve = s.sb("t_dve", [P, 2, HALF])
        t_pool = s.sb("t_pool", [P, 2, HALF])
        con = s.sb("con", [P, HT0, D])
        biases = s.sb("biases", [P, DT, 2])
        upb = s.sb("upb", [P, HT0])
        tp = s.ps("tp", [P, 4, 4, P])
        w_in = s.sem("w_in")
        con_in = s.sem("con_in")
        stage_in = [s.sem(f"stage_in{i}") for i in range(4)]
        turned = s.sem("turned")
        taken = s.sem("taken")
        dve_step = s.sem("dve_step")
        pool_step = s.sem("pool_step")
        dve_stage = s.sem("dve_stage")
        pool_stage = s.sem("pool_stage")
        back = s.sem("back")
        row_t = s.sem("row_t")
        block = s.block()

        @block.sync
        def _(sp):
            sp.dma_start(con[:, :, :], w_con.rearrange("(t p) d -> p t d", p=P)).then_inc(con_in, 16)
            sp.dma_start(up[0][:, :, :], w_exp.rearrange("(k p) h -> p k h", p=P)).then_inc(w_in, 16)
            sp.dma_start(row[0][:, :], b_exp.rearrange("(a h) -> a h", a=1)).then_inc(w_in, 16)
            sp.dma_start(upb[:, :], up_b.rearrange("(t p) -> p t", p=P), allow_slow_non_contiguous=True).then_inc(w_in, 16)
            sp.dma_start(biases[:, :, 0], b_con.rearrange("(t p) -> p t", p=P), allow_slow_non_contiguous=True).then_inc(w_in, 16)
            sp.dma_start(biases[:, :, 1], down_b.rearrange("(t p) -> p t", p=P), allow_slow_non_contiguous=True).then_inc(w_in, 16)
            for i in range(STAGES):
                if i >= 2:
                    sp.wait_ge(dve_stage, i - 1)
                sp.dma_start(wb[i % 2][:, :], down_w[STAGES - 1 - i].rearrange("(a n) i j -> a (n i j)", a=1).broadcast_to([P, HALF * 4])).then_inc(stage_in[i % 2], 16)
                if i >= 2:
                    sp.wait_ge(pool_stage, i - 1)
                sp.dma_start(wb[2 + i % 2][:, :], up_w[i].rearrange("(a n) i j -> a (n i j)", a=1).broadcast_to([P, HALF * 4])).then_inc(stage_in[2 + i % 2], 16)

        def stage(eng, step, count, src, dst, tmp, weights, stride, swap, rows):
            def halves(t):
                v = t.rearrange("p (n h s) -> p n h s", h=2, s=stride)
                return v[:, :, 0, :], v[:, :, 1, :]
            a, b = halves(src)
            oa, ob = halves(dst)
            wv = weights.rearrange("p (n s i j) -> p n s i j", s=stride, i=2, j=2)
            shape = lambda t: t.rearrange("p (n s) -> p n s", s=stride)
            for n, (o, i0, i1) in enumerate(((oa, (0, 0), (0, 1)), (ob, (1, 0), (1, 1)))):
                if swap:
                    i0, i1 = i0[::-1], i1[::-1]
                t = shape(tmp[0:rows, n, :])
                eng.tensor_tensor(o, a, wv[0:rows, :, :, i0[0], i0[1]], ALU.mult).then_inc(step, 1)
                eng.tensor_tensor(t, b, wv[0:rows, :, :, i1[0], i1[1]], ALU.mult).then_inc(step, 1)
                count += 2
                eng.wait_ge(step, count)
                eng.tensor_tensor(o, o, t, ALU.add).then_inc(step, 1)
                count += 1
            eng.wait_ge(step, count)
            return count

        @block.gpsimd
        def _(pool):
            pool.wait_ge(w_in, 80)
            count = 0
            for i in range(STAGES):
                pool.wait_ge(stage_in[2 + i % 2], 16 * (i // 2 + 1))
                for k in range(DT):
                    count = stage(pool, pool_step, count, up[i % 2][:, k, :], up[(i + 1) % 2][:, k, :], t_pool,
                                  wb[2 + i % 2], 2 ** i, False, P)
                count = stage(pool, pool_step, count, row[i % 2][:, :], row[(i + 1) % 2][:, :], t_pool,
                              wb[2 + i % 2][0:1, :], 2 ** i, False, 1)
                pool.sem_inc(pool_stage, 1)
            for k in range(DT):
                pool.tensor_copy(w_up[:, k, :], up[0][:, k, :]).then_inc(pool_step, 1)
            pool.tensor_tensor(b_out[:, :], biases[:, :, 0], biases[:, :, 1], ALU.add).then_inc(pool_step, 1)

        @block.vector
        def _(dve):
            for n in range(4):
                k, g = divmod(n, 2)
                dve.wait_ge(turned, n + 1)
                dve.tensor_copy(down[0][:, k, g * CH:(g + 1) * CH], tp[:, n, :, :].rearrange("p j q -> p (j q)")).then_inc(taken, 1)
            dve.wait_ge(taken, 4)
            count = 0
            for i in range(STAGES):
                dve.wait_ge(stage_in[i % 2], 16 * (i // 2 + 1))
                for k in range(DT):
                    count = stage(dve, dve_step, count, down[i % 2][:, k, :], down[(i + 1) % 2][:, k, :], t_dve,
                                  wb[i % 2], 2 ** (STAGES - 1 - i), True, P)
                dve.engine_nop().then_inc(dve_stage, 1)
            for n in range(4):
                dve.wait_ge(back, n + 1)
                dve.tensor_copy(w_down[:, 2 * n:2 * n + 2, :].rearrange("p t d -> p (t d)"),
                                tp[:, n, :, :].rearrange("p j q -> p (j q)")).then_inc(taken, 1)
            dve.wait_ge(row_t, 1)
            dve.wait_ge(w_in, 80)
            dve.tensor_tensor(b_up[:, :], tp[:, 0, 0, 0:HT0], upb[:, :], ALU.add).then_inc(taken, 1)

        @block.tensor
        def _(pe):
            pe.wait_ge(con_in, 16)
            for n in range(4):
                k, g = divmod(n, 2)
                for j in range(4):
                    last = pe.transpose(tp[:, n, j, :], con[:, 4 * g + j, k * P:(k + 1) * P], ident[:, :])
                last.then_inc(turned, 1)
            pe.wait_ge(dve_stage, STAGES)
            for n in range(4):
                for j in range(4):
                    t, k = divmod(4 * n + j, DT)
                    last = pe.transpose(tp[:, n, j, :], down[0][:, k, t * P:(t + 1) * P], ident[:, :])
                last.then_inc(back, 1)
            pe.wait_ge(taken, 5)
            pe.wait_ge(pool_stage, STAGES)
            for t in range(HT0):
                last = pe.matmul(tp[:, 0, 0, t:t + 1], row[0][:, t * P:(t + 1) * P], ident[0:1, 0:1], start=True, stop=True)
            last.then_inc(row_t, 1)


def butterfly_ffn_phase(nc, hn, w_up, b_up, w_down, b_out, resid):
    with Scope(nc, "ffn0") as s:
        g = s.sb("g", [P, 2, HT0, CH])
        hid = s.ps("hid", [P, 4, CH])
        ps = s.ps("ps", [P, 2, CH])
        made = s.sem("made")
        gelued = s.sem("gelued")
        out_done = s.sem("out_done")
        added = s.sem("added")
        block = s.block()

        @block.tensor
        def _(pe):
            def up(c):
                for j in range(HT0):
                    n = c * HT0 + j
                    if n >= 4:
                        pe.wait_ge(gelued, n - 3)
                    for k in range(DT):
                        last = pe.matmul(hid[:, n % 4, :], w_up[:, k, j * P:(j + 1) * P], hn[:, k, c * CH:(c + 1) * CH],
                                         start=k == 0, stop=k == DT - 1)
                    last.then_inc(made, 1)

            def down(c):
                pe.wait_ge(gelued, (c + 1) * HT0)
                for m in range(DT):
                    n = c * DT + m
                    if n >= 2:
                        pe.wait_ge(added, n - 1)
                    for j in range(HT0):
                        last = pe.matmul(ps[:, m, :], w_down[:, j, m * P:(m + 1) * P], g[:, c % 2, j, :],
                                         start=j == 0, stop=j == HT0 - 1)
                    last.then_inc(out_done, 1)

            up(0)
            for c in range(1, NCH):
                up(c)
                down(c - 1)
            down(NCH - 1)

        @block.scalar
        def _(act):
            for n in range(NCH * HT0):
                c, j = divmod(n, HT0)
                act.wait_ge(made, n + 1)
                if c >= 2:
                    act.wait_ge(out_done, DT * (c - 1))
                act.activation(g[:, c % 2, j, :], hid[:, n % 4, :], ACT.Gelu, bias=b_up[:, j:j + 1]).then_inc(gelued, 1)

        @block.vector
        def _(dve):
            for n in range(NCH * DT):
                c, m = divmod(n, DT)
                dve.wait_ge(out_done, n + 1)
                part = resid[:, m, c * CH:(c + 1) * CH]
                dve.scalar_tensor_tensor(part, ps[:, m, :], b_out[:, m:m + 1], part, ALU.add, ALU.add).then_inc(added, 1)



UNITS = 2 * PAIRS
QK_SCALE = 8.0
NLOADS = 24
WPC = CH // WIN
SLOTS = WPC * PAIRS
KW = CH + WIN
RING_V = UNITS
RING_ROT = RING_V + WPC
RING_OUT = RING_ROT + 2 * UNITS
RING = RING_OUT + DT
BACK_AG = 2
BACK_Y = BACK_AG + 2 * HT1
BACK = BACK_Y + DT


def layer_phase(nc, tag, a, l, y, y_mid, cst, ident, ones_mean, eps):
    with Scope(nc, tag) as s:
        wqkv = s.sb("wqkv", [P, DT, 3 * INNER])
        wo = s.sb("wo", [P, PAIRS, D])
        w1 = s.sb("w1", [P, DT, 2 * HID1])
        w2 = s.sb("w2", [P, HT1, D])
        b1 = s.sb("b1", [P, 2, HT1])
        b2 = s.sb("b2", [P, DT])
        ln_g = s.sb("ln_g", [P, DT])
        ln_b = s.sb("ln_b", [P, DT])
        scales = s.sb("scales", [P, 2, 2])
        table = s.sb("table", [P, 4, CH])
        raw = s.sb("raw", [P, UNITS, CH])
        sq = s.sb("sq", [P, 2, CH])
        norm = s.sb("norm", [2 * UNITS, CH])
        t_cos = s.sb("t_cos", [P, 2, CH])
        t_sin = s.sb("t_sin", [P, 2, CH])
        qr = s.sb("qr", [P, PAIRS, 2, CH])
        kr = s.sb("kr", [P, PAIRS, KW])
        v = s.sb("v", [P, WPC + 1, INNER])
        y_stage = s.sb("y_stage", [P, DT, CH])
        mx = s.sb("mx", [P, 4, 2])
        neg = s.sb("neg", [P, 4, 2])
        den = s.sb("den", [P, 4, 2])
        rden = s.sb("rden", [P, 4, 2])
        probs = s.sb("probs", [P, 2, 2, 2 * WIN])
        probs_t = s.sb("probs_t", [P, 2, 4, WIN])
        o = s.sb("o", [P, PAIRS, CH])
        hn = s.sb("hn", [P, DT, CH])
        std = s.sb("std", [P, CH])
        rstd = s.sb("rstd", [P, CH])
        gel = s.sb("gel", [P, 2, CH])
        hid = s.sb("hid", [P, HT1, CH])
        ring = s.ps("ring", [P, 2, CH])
        st = s.ps("st", [P, 2, 2, 2 * WIN])
        tp = s.ps("tp", [P, 4, WIN])
        ov = s.ps("ov", [P, PAIRS, WIN])
        back = s.ps("back", [P, 2, CH])
        sem = s.sem
        w_in, v_zero, table_in = sem("w_in"), sem("v_zero"), sem("table_in")
        ring_full, n2_full, st_full, tp_full, av_done = sem("ring_full"), sem("n2_full"), sem("st_full"), sem("tp_full"), sem("av_done")
        n2_part = sem("n2_part")
        raw_copied, squared, v_copied, norm_done = sem("raw_copied"), sem("squared"), sem("v_copied"), sem("norm_done")
        exped, pt_copied, o_copied = sem("exped"), sem("pt_copied"), sem("o_copied")
        clipped, rnormed, sin_done, qk_done = sem("clipped"), sem("rnormed"), sem("sin_done"), sem("qk_done")
        maxed, negged, inverted, p_normed, mid_done = sem("maxed"), sem("negged"), sem("inverted"), sem("p_normed"), sem("mid_done")
        cos_done, rotated, kv_moved, staged, table_scaled = sem("cos_done"), sem("rotated"), sem("kv_moved"), sem("staged"), sem("table_scaled")
        back_full, hsquared, std_done, gelued = sem("back_full"), sem("hsquared"), sem("std_done"), sem("gelued")
        centred, inv_std, scaled, affined, gated, y_done = sem("centred"), sem("inv_std"), sem("scaled"), sem("affined"), sem("gated"), sem("y_done")
        block = s.block()

        def iterations(eng, body):
            body(0, None)
            with eng.Fori(1, NCH) as c:
                body(c, c - 1)
            body(None, NCH - 1)

        def ring_free(pe, c, pos):
            if pos < 2:
                if isinstance(c, int) and c == 0:
                    return
                pe.wait_ge(mid_done, DT * c + pos - 1)
            elif pos - 2 < RING_V:
                pe.wait_ge(squared, UNITS * c + pos - 1)
            elif pos - 2 < RING_ROT:
                pe.wait_ge(v_copied, WPC * c + pos - 1 - RING_V)
            elif pos - 2 < RING_OUT:
                j, bc = divmod(pos - 2 - RING_ROT, 2)
                pe.wait_ge(qk_done if bc else sin_done, UNITS * c + j + 1)

        def back_free(pe, c, pos):
            if pos < 2:
                pe.wait_ge(y_done, DT * c + pos + 1)
            elif pos == 2:
                pe.wait_ge(centred, DT * (c + 1))
            elif pos == 3:
                pe.wait_ge(std_done, c + 1)
            else:
                j, g = divmod(pos - 2 - BACK_AG, 2)
                pe.wait_ge(gelued if g else gated, HT1 * c + j + 1)

        def toks(c, shifted):
            return bass.ds(c * CH + (0 if shifted else 1), CH)

        @block.sync
        def _(sp):
            slow = dict(allow_slow_non_contiguous=True)
            loads = [(wqkv[:, :, :], a["L1_ffn_wqkv"][l].rearrange("(k p) n -> p k n", p=P), {}),
                     (wo[:, :, :], a["L1_ffn_wo"][l].rearrange("(k p) n -> p k n", p=P), {}),
                     (w1[:, :, :], a["L1_ffn_w1"][l].rearrange("(k p) n -> p k n", p=P), {}),
                     (w2[:, 0:HT1 - 1, :], a["L1_ffn_w2"][l, 0:(HT1 - 1) * P, :].rearrange("(k p) n -> p k n", p=P), {}),
                     (w2[0:LASTH, HT1 - 1, :], a["L1_ffn_w2"][l, (HT1 - 1) * P:HID1, :], {})]
            for i in range(2):
                bv = a["L1_ffn_b1"][l, i * HID1:(i + 1) * HID1]
                loads += [(b1[:, i, 0:HT1 - 1], bv[0:(HT1 - 1) * P].rearrange("(k p) -> p k", p=P), slow),
                          (b1[0:LASTH, i, HT1 - 1:HT1], bv[(HT1 - 1) * P:HID1].rearrange("(p a) -> p a", a=1), {})]
            for t, n in ((b2, "b2"), (ln_g, "ln_g"), (ln_b, "ln_b")):
                loads.append((t[:, :], a["L1_ffn_" + n][l].rearrange("(k p) -> p k", p=P), slow))
            for i, n in enumerate(("L1_ffn_q_scale", "L1_ffn_k_scale")):
                sv = a[n][l].rearrange("(p a) -> p a", a=1)
                for h in range(2):
                    r = h * DH
                    loads += [(scales[r:r + DH, i, 0:1], sv, {}),
                              (scales[r:r + DH // 2, i, 1:2], sv[DH // 2:DH], {}),
                              (scales[r + DH // 2:r + DH, i, 1:2], sv[0:DH // 2], {})]
            for dst, src, kw in loads:
                sp.dma_start(dst, src, **kw).then_inc(w_in, 16)
            assert len(loads) == NLOADS
            for c in range(NCH):
                if c:
                    sp.wait_ge(qk_done, UNITS * c)
                sp.dma_start(table[:, :, :], cst["tables"][:, :, c * CH:(c + 1) * CH]).then_inc(table_in, 16)

        @block.tensor
        def _(pe):
            def project(c, j):
                ring_free(pe, c, j)
                for k in range(DT):
                    last = pe.matmul(ring[:, j % 2, :], wqkv[:, k, j * P:(j + 1) * P], y[:, k, toks(c, k)],
                                     start=k == 0, stop=k == DT - 1)
                last.then_inc(ring_full, 1)

            def norm_sum(c, j):
                pe.wait_ge(squared, UNITS * c + j + 1)
                if j == 0 and not (isinstance(c, int) and c == 0):
                    pe.wait_ge(o_copied, WPC * c)
                last = pe.matmul(ov[0:2 * UNITS, :, :].rearrange("p m q -> p (m q)"), cst["sel"][:, j, :], sq[:, j % 2, :],
                                 start=j == 0, stop=j == UNITS - 1)
                last.then_inc(n2_part, 1)

            def values(c, t):
                ring_free(pe, c, RING_V + t)
                for k in range(DT):
                    pe_in = y_stage[:, k, t * P:(t + 1) * P]
                    last = pe.matmul(ring[:, t % 2, :], pe_in, wqkv[:, k, 2 * INNER:3 * INNER],
                                     start=k == 0, stop=k == DT - 1)
                last.then_inc(ring_full, 1)

            def rotate(c, j):
                ring_free(pe, c, RING_ROT + 2 * j)
                pe.matmul(ring[:, 0, :], cst["rot"][:, :], raw[:, j, :], start=True, stop=True).then_inc(ring_full, 1)
                ring_free(pe, c, RING_ROT + 2 * j + 1)
                if j == 0:
                    pe.wait_ge(rnormed, c + 1)
                pe.matmul(ring[:, 1, :], cst["sel_t"][:, j, :], norm[:, :], start=True, stop=True).then_inc(ring_full, 1)

            def scores(c, u):
                w, m = divmod(u, PAIRS)
                first = isinstance(c, int) and c == 0
                if u == 0:
                    pe.wait_ge(qk_done, UNITS * (c + 1))
                    pe.wait_ge(rotated, UNITS * (c + 1))
                if u >= 2 or not first:
                    pe.wait_ge(exped, SLOTS * c + u - 1)
                mask = cst["mask_first"] if first and w == 0 else cst["mask"]
                bank = st[:, u % 2, :, :]
                pe.matmul(bank.rearrange("p h k -> p (h k)"), cst["ident_b"][:, :], mask[:, :], start=True, stop=True)
                for h in range(2):
                    last = pe.matmul(bank[:, h, :], qr[:, m, h, w * WIN:(w + 1) * WIN], kr[:, m, w * WIN:(w + 2) * WIN],
                                     start=False, stop=True, skip_group_check=True)
                last.then_inc(st_full, 1)

            def turn(c, u):
                pe.wait_ge(p_normed, SLOTS * c + u + 1)
                if u or not (isinstance(c, int) and c == 0):
                    pe.wait_ge(pt_copied, SLOTS * c + u)
                for i in range(4):
                    last = pe.transpose(tp[:, i, :], probs[:, u % 2, i // 2, (i % 2) * WIN:(i % 2 + 1) * WIN], ident[:, :])
                last.then_inc(tp_full, 1)

            def weigh(c, u):
                w, m = divmod(u, PAIRS)
                pe.wait_ge(pt_copied, SLOTS * c + u + 1)
                if u == 0:
                    pe.wait_ge(v_copied, WPC * (c + 1))
                    pe.wait_ge(norm_done, c + 1)
                elif m == 0:
                    pe.wait_ge(o_copied, WPC * c + w)
                for h in range(2):
                    for i in range(2):
                        last = pe.matmul(ov[h * DH:(h + 1) * DH, m, :], v[:, w + i, (2 * m + h) * DH:(2 * m + h + 1) * DH],
                                         probs_t[:, u % 2, 2 * h + i, :], start=i == 0, stop=i == 1)
                last.then_inc(av_done, 1)

            def output(c, m):
                pos = RING_OUT + m
                ring_free(pe, c, pos)
                pe.wait_ge(o_copied, WPC * (c + 1))
                for k in range(PAIRS):
                    last = pe.matmul(ring[:, pos % 2, :], wo[:, k, m * P:(m + 1) * P], o[:, k, :], start=k == 0, stop=k == PAIRS - 1)
                last.then_inc(ring_full, 1)

            def mean(c):
                pe.wait_ge(mid_done, DT * (c + 1))
                back_free(pe, c, 0)
                for k in range(DT):
                    last = pe.matmul(back[:, 0, :], ones_mean[:, :], y_mid[:, k, toks(c, k)], start=k == 0, stop=k == DT - 1)
                last.then_inc(back_full, 1)

            def variance(c):
                pe.wait_ge(hsquared, c + 1)
                back_free(pe, c, 1)
                for k in range(DT):
                    last = pe.matmul(back[:, 1, :], ones_mean[:, :], gel[:, k, :], start=k == 0, stop=k == DT - 1)
                last.then_inc(back_full, 1)

            def expand(c, j):
                n = hid_rows(j)
                if j == 0:
                    pe.wait_ge(affined, DT * (c + 1))
                for g in range(2):
                    back_free(pe, c, BACK_AG + 2 * j + g)
                    col = g * HID1 + j * P
                    for k in range(DT):
                        last = pe.matmul(back[0:n, g, :], w1[:, k, col:col + n], hn[:, k, :], start=k == 0, stop=k == DT - 1)
                    last.then_inc(back_full, 1)

            def contract(c, m):
                back_free(pe, c, BACK_Y + m)
                pe.wait_ge(gated, HT1 * (c + 1))
                for j in range(HT1):
                    n = hid_rows(j)
                    last = pe.matmul(back[:, m, :], w2[0:n, j, m * P:(m + 1) * P], hid[0:n, j, :], start=j == 0, stop=j == HT1 - 1)
                last.then_inc(back_full, 1)

            def body(f, b):
                if f is None:
                    mean(b)
                if f is not None:
                    for j in range(UNITS):
                        project(f, j)
                        if j:
                            norm_sum(f, j - 1)
                        if j == 1 and b is not None:
                            mean(b)
                    norm_sum(f, UNITS - 1)
                    pe.wait_ge(staged, DT * (f + 1))
                if b is not None:
                    variance(b)
                if f is not None:
                    for t in range(WPC):
                        values(f, t)
                for j in range(UNITS):
                    if f is not None:
                        rotate(f, j)
                    if b is not None and j >= UNITS - HT1:
                        expand(b, j - (UNITS - HT1))
                if f is not None:
                    for u in range(SLOTS + 2):
                        if u < SLOTS:
                            scores(f, u)
                        if 1 <= u <= SLOTS:
                            turn(f, u - 1)
                        if u >= 2:
                            weigh(f, u - 2)
                        if b is not None and u in (1, 4):
                            contract(b, u // 4)
                    for m in range(DT):
                        output(f, m)
                else:
                    for m in range(DT):
                        contract(b, m)

            pe.wait_ge(w_in, 16 * NLOADS)
            iterations(pe, body)

        @block.scalar
        def _(act):
            def body(f, b):
                if f is not None:
                    act.wait_ge(table_in, 16 * (f + 1))
                    for i in range(2):
                        act.activation(table[:, 2 * i, :], table[:, 2 * i, :], ACT.Copy, scale=scales[:, i, 0:1]).then_inc(table_scaled, 1)
                    for j in range(UNITS):
                        act.wait_ge(ring_full, RING * f + j + 1)
                        if j == 0 and not (isinstance(f, int) and f == 0):
                            act.wait_ge(qk_done, UNITS * f)
                        act.activation(raw[:, j, :], ring[:, j % 2, :], ACT.Copy).then_inc(raw_copied, 1)
                        if j >= 2:
                            act.wait_ge(n2_part, UNITS * f + j - 1)
                        act.activation(sq[:, j % 2, :], ring[:, j % 2, :], ACT.Square).then_inc(squared, 1)
                        if b is not None and j == 4:
                            act.wait_ge(centred, DT * (b + 1))
                            act.activation(gel[:, :, :], hn[:, :, :], ACT.Square).then_inc(hsquared, 1)
                    act.wait_ge(n2_part, UNITS * (f + 1))
                    act.activation(norm[:, :], ov[0:2 * UNITS, :, :].rearrange("p m q -> p (m q)"), ACT.Sqrt).then_inc(norm_done, 1)
                else:
                    act.wait_ge(centred, DT * (b + 1))
                    act.activation(gel[:, :, :], hn[:, :, :], ACT.Square).then_inc(hsquared, 1)
                if b is not None:
                    act.wait_ge(back_full, BACK * b + 2)
                    act.activation(std[:, :], back[:, 1, :], ACT.Sqrt, bias=eps[:, 0:1]).then_inc(std_done, 1)
                if f is not None:
                    for t in range(WPC):
                        act.wait_ge(ring_full, RING * f + RING_V + t + 1)
                        if t == 0 and not (isinstance(f, int) and f == 0):
                            act.wait_ge(kv_moved, 2 * f)
                        act.activation(v[:, t + 1, :], ring[:, t % 2, :], ACT.Copy).then_inc(v_copied, 1)
                if b is not None:
                    for j in range(HT1):
                        n = hid_rows(j)
                        act.wait_ge(back_full, BACK * b + BACK_AG + 2 * j + 2)
                        if j >= 2:
                            act.wait_ge(gated, HT1 * b + j - 1)
                        act.activation(gel[0:n, j % 2, :], back[0:n, 1, :], ACT.Gelu, bias=b1[0:n, 1, j:j + 1]).then_inc(gelued, 1)
                if f is not None:
                    first = isinstance(f, int) and f == 0
                    for u in range(SLOTS + 2):
                        if u < SLOTS:
                            act.wait_ge(negged, SLOTS * f + u + 1)
                            if u >= 2 or not first:
                                act.wait_ge(tp_full, SLOTS * f + u - 1)
                            if u >= 4 or not first:
                                act.wait_ge(inverted, SLOTS * f + u - 3)
                            for h in range(2):
                                last = act.activation(probs[:, u % 2, h, :], st[:, u % 2, h, :], ACT.Exp, scale=QK_SCALE,
                                                      bias=neg[:, u % 4, h:h + 1], accum_out=den[:, u % 4, h:h + 1])
                            last.then_inc(exped, 1)
                        if u >= 1 and u <= SLOTS:
                            t = u - 1
                            act.wait_ge(tp_full, SLOTS * f + t + 1)
                            if t >= 2 or not first:
                                act.wait_ge(av_done, SLOTS * f + t - 1)
                            act.activation(probs_t[:, t % 2, :, :], tp[:, :, :], ACT.Copy).then_inc(pt_copied, 1)
                        if u >= 2 and (u - 2) % PAIRS == PAIRS - 1:
                            w = (u - 2) // PAIRS
                            act.wait_ge(av_done, SLOTS * f + u - 1)
                            act.activation(o[:, :, w * WIN:(w + 1) * WIN], ov[:, :, :], ACT.Copy).then_inc(o_copied, 1)
                    act.activation(kr[:, :, 0:WIN], kr[:, :, CH:KW], ACT.Copy).then_inc(kv_moved, 1)
                    act.activation(v[:, 0, :], v[:, WPC, :], ACT.Copy).then_inc(kv_moved, 1)

            act.wait_ge(w_in, 16 * NLOADS)
            iterations(act, body)

        @block.vector
        def _(dve):
            def body(f, b):
                if b is not None:
                    dve.wait_ge(back_full, BACK * b + 1)
                    for k in range(DT):
                        dve.tensor_tensor(hn[:, k, :], y_mid[:, k, toks(b, k)], back[:, 0, :], ALU.subtract).then_inc(centred, 1)
                if f is not None:
                    dve.wait_ge(norm_done, f + 1)
                    dve.tensor_scalar(norm[:, :], norm[:, :], 1e-12, None, ALU.max).then_inc(clipped, 1)
                    dve.wait_ge(clipped, f + 1)
                    dve.reciprocal(norm[:, :], norm[:, :]).then_inc(rnormed, 1)
                if b is not None:
                    dve.wait_ge(std_done, b + 1)
                    dve.reciprocal(rstd[:, :], std[:, :]).then_inc(inv_std, 1)
                    dve.wait_ge(inv_std, b + 1)
                    dve.wait_ge(hsquared, b + 1)
                    for k in range(DT):
                        dve.scalar_tensor_tensor(hn[:, k, :], hn[:, k, :], ln_g[:, k:k + 1], rstd[:, :], ALU.mult, ALU.mult).then_inc(scaled, 1)
                    for k in range(DT):
                        dve.wait_ge(scaled, DT * b + k + 1)
                        dve.tensor_scalar(hn[:, k, :], hn[:, k, :], ln_b[:, k:k + 1], None, ALU.add).then_inc(affined, 1)
                for j in range(UNITS):
                    if f is not None:
                        i = j // PAIRS
                        if j == 0:
                            dve.wait_ge(table_in, 16 * (f + 1))
                            if not (isinstance(f, int) and f == 0):
                                dve.wait_ge(kv_moved, 2 * f)
                        dve.wait_ge(ring_full, RING * f + RING_ROT + 2 * j + 1)
                        if j >= 2 or not (isinstance(f, int) and f == 0):
                            dve.wait_ge(rotated, UNITS * f + j - 1)
                        dve.scalar_tensor_tensor(t_sin[:, j % 2, :], ring[:, 0, :], scales[:, i, 1:2],
                                                 table[:, 2 * i + 1, :], ALU.mult, ALU.mult).then_inc(sin_done, 1)
                        dve.wait_ge(ring_full, RING * f + RING_ROT + 2 * j + 2)
                        dve.wait_ge(rotated, UNITS * f + j + 1)
                        if j < PAIRS:
                            for h in range(2):
                                rows = slice(h * DH, (h + 1) * DH)
                                last = dve.tensor_tensor(qr[rows, j, h, :], t_cos[rows, j % 2, :], ring[rows, 1, :], ALU.mult)
                        else:
                            last = dve.tensor_tensor(kr[:, j - PAIRS, WIN:KW], t_cos[:, j % 2, :], ring[:, 1, :], ALU.mult)
                        last.then_inc(qk_done, 1)
                    if b is not None and j >= UNITS - HT1:
                        jj = j - (UNITS - HT1)
                        n = hid_rows(jj)
                        dve.wait_ge(gelued, HT1 * b + jj + 1)
                        dve.scalar_tensor_tensor(hid[0:n, jj, :], back[0:n, 0, :], b1[0:n, 0, jj:jj + 1], gel[0:n, jj % 2, :],
                                                 ALU.add, ALU.mult).then_inc(gated, 1)

                def finish(m):
                    dve.wait_ge(back_full, BACK * b + BACK_Y + m + 1)
                    dve.scalar_tensor_tensor(y[:, m, toks(b, 0)], back[:, m, :], b2[:, m:m + 1], y_mid[:, m, toks(b, 0)],
                                             ALU.add, ALU.add).then_inc(y_done, 1)
                if f is not None:
                    for u in range(SLOTS + 1):
                        if u < SLOTS:
                            dve.wait_ge(st_full, SLOTS * f + u + 1)
                            dve.reduce_max(mx[:, u % 4, :], st[:, u % 2, :, :], AX.X).then_inc(maxed, 1)
                            dve.wait_ge(maxed, SLOTS * f + u + 1)
                            dve.tensor_scalar(neg[:, u % 4, :], mx[:, u % 4, :], -QK_SCALE, None, ALU.mult).then_inc(negged, 1)
                        if u >= 1:
                            t = u - 1
                            dve.wait_ge(exped, SLOTS * f + t + 1)
                            dve.reciprocal(rden[:, t % 4, :], den[:, t % 4, :]).then_inc(inverted, 1)
                            dve.wait_ge(inverted, SLOTS * f + t + 1)
                            dve.tensor_tensor(probs[:, t % 2, :, :], probs[:, t % 2, :, :],
                                              rden[:, t % 4, :].unsqueeze(2).broadcast_to([P, 2, 2 * WIN]), ALU.mult).then_inc(p_normed, 1)
                        if b is not None and u in (3, 6):
                            finish(u // 6)
                    for m in range(DT):
                        dve.wait_ge(ring_full, RING * f + RING_OUT + m + 1)
                        dve.tensor_tensor(y_mid[:, m, toks(f, 0)], ring[:, (RING_OUT + m) % 2, :], y[:, m, toks(f, 0)],
                                          ALU.add).then_inc(mid_done, 1)
                else:
                    for m in range(DT):
                        finish(m)

            dve.sem_inc(y_done, DT)
            for h in range(2):
                other = slice((1 - h) * DH, (2 - h) * DH)
                dve.memset(qr[other, :, h, :], 0.0)
            dve.wait_ge(w_in, 16 * NLOADS)
            iterations(dve, body)

        @block.gpsimd
        def _(pool):
            def body(f, b):
                if f is None:
                    return
                first = isinstance(f, int) and f == 0
                for k in range(DT):
                    pool.tensor_copy(y_stage[:, k, :], y[:, k, toks(f, k)]).then_inc(staged, 1)
                pool.wait_ge(table_scaled, 2 * (f + 1))
                for j in range(UNITS):
                    i = j // PAIRS
                    pool.wait_ge(raw_copied, UNITS * f + j + 1)
                    if j >= 2 or not first:
                        pool.wait_ge(qk_done, UNITS * f + j - 1)
                    pool.tensor_tensor(t_cos[:, j % 2, :], raw[:, j, :], table[:, 2 * i, :], ALU.mult).then_inc(cos_done, 1)
                    pool.wait_ge(cos_done, UNITS * f + j + 1)
                    pool.wait_ge(sin_done, UNITS * f + j + 1)
                    pool.tensor_tensor(t_cos[:, j % 2, :], t_cos[:, j % 2, :], t_sin[:, j % 2, :], ALU.add).then_inc(rotated, 1)

            pool.memset(kr[:, :, 0:WIN], 0.0).then_inc(v_zero, 1)
            pool.memset(v[:, 0, :], 0.0).then_inc(v_zero, 1)
            pool.wait_ge(w_in, 16 * NLOADS)
            pool.wait_ge(v_zero, 2)
            iterations(pool, body)


def tables():
    t = np.arange(NQ, dtype=np.float32)
    half = np.arange(0, DH, 2, dtype=np.float32)
    freqs = t[:, None] * (np.float32(1.0) / np.float32(10000.0) ** (half / np.float32(DH)))[None, :]
    base = (half + np.float32(0.4 * DH)) / np.float32(1.4 * DH)
    power = (t - NQ // 2) / np.float32(WIN // 2)
    xpos = base[None, :] ** power[:, None]
    four = [np.cos(freqs) * xpos, np.sin(freqs) * xpos, np.cos(freqs) / xpos, np.sin(freqs) / xpos]
    rotary = np.stack([np.tile(m.T, (4, 1)) for m in four], axis=1).astype(np.float32)
    i, j = np.arange(WIN)[:, None], np.arange(2 * WIN)[None, :] - WIN
    band = np.where((i < j) | (i > j + WIN), NEG, 0.0).astype(np.float32)
    first = np.where((i < j) | (j < 0), NEG, 0.0).astype(np.float32)
    masks = np.stack([np.tile(band, (1, 2)), np.tile(first, (1, 2))], axis=1)
    p = np.arange(P)
    rot = np.zeros((P, P), np.float32)
    low = p[p % DH < DH // 2]
    rot[low + DH // 2, low] = -1.0
    rot[low, low + DH // 2] = 1.0
    sel = np.zeros((P, UNITS, 2 * UNITS), np.float32)
    for u in range(UNITS):
        sel[p, u, 2 * u + p // DH] = 1.0
    sel_t = np.ascontiguousarray(sel.transpose(2, 1, 0))
    return {"c_rotary": rotary, "c_masks": masks, "c_rot": rot, "c_sel": sel, "c_sel_t": sel_t}


def constants_phase(nc, a, cst, y, y_mid):
    with Scope(nc, "cst") as s:
        masks = s.sb("masks", [P, 2, 4 * WIN])
        loaded, masks_in, zeroed = s.sem("loaded"), s.sem("masks_in"), s.sem("zeroed")
        block = s.block()

        @block.sync
        def _(sp):
            sp.dma_start(masks[:, :, :], a["c_masks"]).then_inc(masks_in, 16)
            sp.dma_start(cst["rot"][:, :], a["c_rot"]).then_inc(loaded, 16)
            sp.dma_start(cst["sel"][:, :, :], a["c_sel"]).then_inc(loaded, 16)
            sp.dma_start(cst["sel_t"][:, :, :], a["c_sel_t"]).then_inc(loaded, 16)
            sp.wait_ge(loaded, 48)

        @block.gpsimd
        def _(pool):
            pool.memset(y[:, :, 0:1], 0.0).then_inc(zeroed, 1)
            pool.memset(y_mid[:, :, 0:1], 0.0).then_inc(zeroed, 1)
            pool.wait_ge(masks_in, 16)
            pool.tensor_copy(cst["mask"][:, :], masks[:, 0, :]).then_inc(zeroed, 1)
            pool.tensor_copy(cst["mask_first"][:, :], masks[:, 1, :]).then_inc(zeroed, 1)
            pool.tensor_copy(cst["ident_b"][:, :], cst["ident"][:, :]).then_inc(zeroed, 1)


def gated_layers(nc, s, a, resid, ident, ones_mean, eps):
    y = s.sb("y", [P, DT, NQ + 1])
    y_mid = s.sb("y_mid", [P, DT, NQ + 1])
    cst = {"rot": s.sb("rot", [P, P]), "sel": s.sb("sel", [P, UNITS, 2 * UNITS]),
           "sel_t": s.sb("sel_t", [2 * UNITS, UNITS, P]), "mask": s.sb("mask", [P, 4 * WIN], BF16),
           "mask_first": s.sb("mask_first", [P, 4 * WIN], BF16), "ident_b": s.sb("ident_b", [P, P], BF16),
           "ident": ident, "tables": a["c_rotary"]}
    constants_phase(nc, a, cst, y, y_mid)
    norm_phase(nc, "ln3", resid, y[:, :, 1:NQ + 1], ones_mean, eps)
    for l in range(2):
        layer_phase(nc, f"l{l}", a, l, y, y_mid, cst, ident, ones_mean, eps)
    return y[:, :, 1:NQ + 1]


def store_phase(nc, a, b, ident, out):
    TX = NQ // P
    with Scope(nc, "store") as s:
        y = s.sb("y", [P, DT, NQ])
        o = s.sb("o", [P, TX, D])
        tp = s.ps("tp", [P, 8, 2, DT, P])
        summed = s.sem("summed")
        turned = s.sem("turned")
        copied = s.sem("copied")
        stored = s.sem("stored")
        block = s.block()

        @block.gpsimd
        def _(pool):
            for c in range(NCH):
                part = slice(c * CH, (c + 1) * CH)
                if b is None:
                    pool.tensor_copy(y[:, :, part], a[:, :, part]).then_inc(summed, 1)
                else:
                    pool.tensor_tensor(y[:, :, part], a[:, :, part], b[:, :, part], ALU.add).then_inc(summed, 1)

        @block.tensor
        def _(pe):
            for n in range(TX // 2):
                pe.wait_ge(summed, n // 2 + 1)
                for j in range(2):
                    for k in range(DT):
                        t = 2 * n + j
                        last = pe.transpose(tp[:, n, j, k, :], y[:, k, t * P:(t + 1) * P], ident[:, :])
                last.then_inc(turned, 1)

        @block.vector
        def _(dve):
            for n in range(TX // 2):
                dve.wait_ge(turned, n + 1)
                dve.tensor_copy(o[:, 2 * n:2 * n + 2, :].rearrange("p j d -> p (j d)"),
                                tp[:, n, :, :, :].rearrange("p j k q -> p (j k q)")).then_inc(copied, 1)

        @block.sync
        def _(sp):
            ov = out.rearrange("b (t p) d -> p (b t) d", p=P)
            for n in range(4):
                sp.wait_ge(copied, 2 * (n + 1))
                sp.dma_start(ov[:, 4 * n:4 * n + 4, :], o[:, 4 * n:4 * n + 4, :]).then_inc(stored, 16)
            sp.wait_ge(stored, 64)


def transformer_kernel(nc, a, out, upto=99):
    with Scope(nc, "all") as s:
        ident = s.sb("ident", [P, P])
        ones_mean = s.sb("ones_mean", [P, P])
        ones64 = s.sb("ones64", [P, DH])
        eps = s.sb("eps", [P, 1])
        resid = s.sb("resid", [P, DT, NQ])
        v_dram = nc.dram_tensor("v_scratch", (NC_, INNER), F32, kind="Internal").ap()
        o_dram = nc.dram_tensor("o_scratch", (INNER, NQ), F32, kind="Internal").ap()

        def cross(tag, ctx_t, wq, wk, wv, wo, bo):
            values_phase(nc, tag + "v", ctx_t, wv, v_dram)
            with Scope(nc, tag + "h") as s2:
                hn = s2.sb("hn", [P, DT, NQ])
                norm_phase(nc, tag + "n", resid, hn, ones_mean, eps)
                attention_phase(nc, tag, hn, ctx_t, wq, wk, v_dram, o_dram, ident, ones64)
            output_phase(nc, tag + "o", o_dram, wo, bo, resid)

        def butterfly_ffn():
            with Scope(nc, "bf") as s2:
                w_up = s2.sb("w_up", [P, DT, HID0])
                w_down = s2.sb("w_down", [P, HT0, D])
                b_up = s2.sb("b_up", [P, HT0])
                b_out = s2.sb("b_out", [P, DT])
                butterfly_phase(nc, a["L0_ffn_W_exp"], a["L0_ffn_b_exp"], a["L0_ffn_up_weights"], a["L0_ffn_up_bias"],
                                a["L0_ffn_down_weights"], a["L0_ffn_W_con"], a["L0_ffn_b_con"], a["L0_ffn_down_bias"],
                                ident, w_up, b_up, w_down, b_out)
                with Scope(nc, "bfh") as s3:
                    hn = s3.sb("hn", [P, DT, NQ])
                    norm_phase(nc, "ln1", resid, hn, ones_mean, eps)
                    butterfly_ffn_phase(nc, hn, w_up, b_up, w_down, b_out, resid)

        with Scope(nc, "ctx") as s1:
            ctx_t = s1.sb("ctx_t", [P, 2, NC_ + 1])
            load_phase(nc, a["x"], a["ctx_768"], ident, ones_mean, ones64, eps, resid, ctx_t)
            if upto >= 1:
                cross("xa0", ctx_t, a["L0_xattn_Wq"], a["L0_xattn_Wk"], a["L0_xattn_Wv"], a["L0_xattn_Wo"], a["L0_xattn_bo"])
            if upto >= 2:
                butterfly_ffn()
            if upto >= 3:
                cross("xa1", ctx_t, a["L1_xattn_Wq"], a["L1_xattn_Wk"], a["L1_xattn_Wv"], a["L1_xattn_Wout"], a["L1_xattn_bout"])
        if upto >= 4:
            y = gated_layers(nc, s, a, resid, ident, ones_mean, eps)
            store_phase(nc, resid, y, ident, out)
        else:
            store_phase(nc, resid, None, ident, out)


_INS = ["x", "ctx_768", "L0_xattn_Wq", "L0_xattn_Wk", "L0_xattn_Wv", "L0_xattn_Wo", "L0_xattn_bo",
        "L0_ffn_W_exp", "L0_ffn_b_exp", "L0_ffn_up_weights", "L0_ffn_up_bias", "L0_ffn_down_weights",
        "L0_ffn_W_con", "L0_ffn_b_con", "L0_ffn_down_bias",
        "L1_xattn_Wq", "L1_xattn_Wk", "L1_xattn_Wv", "L1_xattn_Wout", "L1_xattn_bout",
        "L1_ffn_wqkv", "L1_ffn_q_scale", "L1_ffn_k_scale", "L1_ffn_wo", "L1_ffn_ln_g", "L1_ffn_ln_b",
        "L1_ffn_w1", "L1_ffn_b1", "L1_ffn_w2", "L1_ffn_b2"]
_CONSTS = ["c_rotary", "c_masks", "c_rot", "c_sel", "c_sel_t"]


def kernel(**inputs):
    import numpy as _np
    import concourse.bacc as _bacc
    from concourse import mybir as _mybir
    from concourse.bass_utils import run_bass_kernel_spmd as _run

    nc = _bacc.Bacc("TRN2", target_bir_lowering=False, num_devices=1)
    arrays, args = {}, {}
    given = {name: _np.ascontiguousarray(inputs[name]) for name in _INS}
    for name, value in {**given, **tables()}.items():
        arrays[f"in_{name}_dram"] = value
        args[name] = nc.dram_tensor(f"in_{name}_dram", value.shape, _mybir.dt.from_np(value.dtype), kind="ExternalInput").ap()
    out = nc.dram_tensor("out_dram", (1, NQ, D), _mybir.dt.float32, kind="ExternalOutput").ap()
    transformer_kernel(nc, args, out)
    return _run(nc, [arrays], core_ids=[0]).results[0]["out_dram"]
```

```python
import numpy as np
import concourse.bass as bass
from concourse import mybir
from contextlib import ExitStack

F32 = mybir.dt.float32
F32R = mybir.dt.float32r
BF16 = mybir.dt.bfloat16
ALU = mybir.AluOpType
ACT = mybir.ActivationFunctionType
AX = mybir.AxisListType

P = 128
NQ = 2048
D = 256
DT = D // P
NC_ = 1601
DC = 192
HEADS, DH = 8, 64
INNER = HEADS * DH
PAIRS = HEADS // 2
CH = 512
NCH = NQ // CH
KT = -(-NC_ // P)
LASTK = NC_ - (KT - 1) * P
EPS = 1e-5
HID0 = 4 * D
HT0 = HID0 // P
STAGES = 10
HID1 = D * 4 * 2 // 3
HT1 = -(-HID1 // P)
LASTH = HID1 - (HT1 - 1) * P
WIN = 128
NEG = -1e30


def key_rows(t):
    return P if t < KT - 1 else LASTK


def hid_rows(j):
    return P if j < HT1 - 1 else LASTH


class Scope:

    def __init__(self, nc, tag):
        self.nc, self.tag, self.stack, self.sems = nc, tag, ExitStack(), []

    def __enter__(self):
        return self

    def __exit__(self, *a):
        self.stack.close()
        if self.sems:
            self.nc.clear_and_free_semaphores(self.sems)
            self.nc.all_engine_barrier()

    def sb(self, name, shape, dt=F32):
        return self.stack.enter_context(self.nc.sbuf_tensor(f"{self.tag}_{name}", shape, dt))

    def ps(self, name, shape, dt=F32):
        return self.stack.enter_context(self.nc.psum_tensor(f"{self.tag}_{name}", shape, dt))

    def sem(self, name):
        self.sems.append(self.nc.alloc_semaphore(f"{self.tag}_{name}"))
        return self.sems[-1]

    def block(self):
        return self.stack.enter_context(self.nc.Block())



def load_phase(nc, x, ctx, ident, ones_mean, ones64, eps, resid, ctx_t):
    xv = x.rearrange("b (t p) d -> p (b t) d", p=P)
    TX = NQ // P
    with Scope(nc, "load") as s:
        xin = s.sb("xin", [P, TX, D])
        cin = s.sb("cin", [P, KT, DC])
        tp = s.ps("tp", [P, 4, 4, P])
        consts = s.sem("consts")
        ident_zero = s.sem("ident_zero")
        x_in = [s.sem(f"x_in{i}") for i in range(4)]
        c_in = s.sem("c_in")
        turned = s.sem("turned")
        taken = s.sem("taken")
        groups = []
        for g in range(TX // 4):
            for k in range(DT):
                groups.append(("x", k, P, [(4 * g + j, P) for j in range(4)]))
        for g in range(-(-KT // 4)):
            for k, rows in ((0, P), (1, DC - P)):
                groups.append(("c", k, rows, [(t, key_rows(t)) for t in range(4 * g, min(4 * g + 4, KT))]))
        block = s.block()

        @block.sync
        def _(sp):
            for i in range(4):
                sp.dma_start(xin[:, 4 * i:4 * i + 4, :], xv[:, 4 * i:4 * i + 4, :]).then_inc(x_in[i], 16)

        @block.gpsimd
        def _(pool):
            pool.memset(ident[:, :], 0.0).then_inc(ident_zero, 1)
            pool.memset(ones_mean[:, :], 1.0 / D).then_inc(consts, 1)
            pool.memset(ones64[:, :], 1.0).then_inc(consts, 1)
            pool.memset(eps[:, :], EPS).then_inc(consts, 1)
            pool.wait_ge(ident_zero, 1)
            pool.affine_select(out=ident[:, :], in_=ident[:, :], compare_op=ALU.not_equal, fill=1.0,
                               base=0, pattern=[[-1, P]], channel_multiplier=1).then_inc(consts, 1)

        @block.tensor
        def _(pe):
            pe.wait_ge(consts, 4)
            for n, (src, k, rows, tiles) in enumerate(groups):
                if src == "x":
                    pe.wait_ge(x_in[tiles[0][0] // 4], 16)
                else:
                    pe.wait_ge(c_in, 32)
                if n >= 4:
                    pe.wait_ge(taken, n - 3)
                for j, (t, toks) in enumerate(tiles):
                    a = xin[:, t, k * P:k * P + rows] if src == "x" else cin[0:toks, t, k * P:k * P + rows]
                    last = pe.transpose(tp[0:rows, n % 4, j, 0:toks], a, ident[0:toks, 0:toks])
                last.then_inc(turned, 1)

        @block.scalar
        def _(act):
            act.dma_start(cin[:, 0:KT - 1, :], ctx[0, 0:(KT - 1) * P, :].rearrange("(t p) d -> p t d", p=P)).then_inc(c_in, 16)
            act.dma_start(cin[0:LASTK, KT - 1, :], ctx[0, (KT - 1) * P:NC_, :]).then_inc(c_in, 16)

        @block.vector
        def _(dve):
            for n, (src, k, rows, tiles) in enumerate(groups):
                dve.wait_ge(turned, n + 1)
                t0, toks = tiles[0][0] * P, sum(m for _, m in tiles)
                dst = resid if src == "x" else ctx_t
                dve.tensor_copy(dst[0:rows, k, t0:t0 + toks],
                                tp[0:rows, n % 4, :, :].rearrange("p j q -> p (j q)")[:, 0:toks]).then_inc(taken, 1)



def norm_phase(nc, tag, src, dst, ones_mean, eps, also=None):
    with Scope(nc, tag) as s:
        sq = s.sb("sq", [P, 2, DT, CH])
        std = s.sb("std", [P, 2, CH])
        rstd = s.sb("rstd", [P, 2, CH])
        mean = s.ps("mean", [P, 2, CH])
        var = s.ps("var", [P, 2, CH])
        mean_done = s.sem("mean_done")
        centred = s.sem("centred")
        squared = s.sem("squared")
        var_done = s.sem("var_done")
        std_done = s.sem("std_done")
        rstd_done = s.sem("rstd_done")
        normed = s.sem("normed")
        block = s.block()

        def chunk(c):
            return slice(c * CH, (c + 1) * CH)

        @block.tensor
        def _(pe):
            def means(c):
                if c >= 2:
                    pe.wait_ge(centred, c - 1)
                for k in range(DT):
                    last = pe.matmul(mean[:, c % 2, :], ones_mean[:, :], src[:, k, chunk(c)],
                                     start=k == 0, stop=k == DT - 1)
                last.then_inc(mean_done, 1)

            def variances(c):
                pe.wait_ge(squared, c + 1)
                if c >= 2:
                    pe.wait_ge(std_done, c - 1)
                for k in range(DT):
                    last = pe.matmul(var[:, c % 2, :], ones_mean[:, :], sq[:, c % 2, k, :],
                                     start=k == 0, stop=k == DT - 1)
                last.then_inc(var_done, 1)

            means(0)
            for c in range(1, NCH):
                means(c)
                variances(c - 1)
            variances(NCH - 1)

        @block.scalar
        def _(act):
            for c in range(NCH):
                act.wait_ge(centred, c + 1)
                if c >= 2:
                    act.wait_ge(var_done, c - 1)
                act.activation(sq[:, c % 2, :, :], dst[:, :, chunk(c)], ACT.Square).then_inc(squared, 1)
                act.wait_ge(var_done, c + 1)
                if c >= 2:
                    act.wait_ge(rstd_done, c - 1)
                act.activation(std[:, c % 2, :], var[:, c % 2, :], ACT.Sqrt, bias=eps[:, 0:1]).then_inc(std_done, 1)

        @block.vector
        def _(dve):
            def centre(c):
                dve.wait_ge(mean_done, c + 1)
                dve.tensor_tensor(dst[:, :, chunk(c)], src[:, :, chunk(c)],
                                  mean[:, c % 2:c % 2 + 1, :].broadcast_to([P, DT, CH]), ALU.subtract).then_inc(centred, 1)

            def scale(c):
                dve.wait_ge(std_done, c + 1)
                if c >= 2:
                    dve.wait_ge(normed, c - 1)
                dve.reciprocal(rstd[:, c % 2, :], std[:, c % 2, :]).then_inc(rstd_done, 1)
                dve.wait_ge(rstd_done, c + 1)
                dve.wait_ge(squared, c + 1)
                dve.tensor_tensor(dst[:, :, chunk(c)], dst[:, :, chunk(c)],
                                  rstd[:, c % 2:c % 2 + 1, :].broadcast_to([P, DT, CH]), ALU.mult).then_inc(normed, 1)

            centre(0)
            for c in range(1, NCH):
                centre(c)
                scale(c - 1)
            scale(NCH - 1)



def values_phase(nc, tag, ctx_t, wv, v_dram):
    with Scope(nc, tag) as s:
        w = s.sb("w", [P, 2, INNER])
        v = s.sb("v", [P, KT, INNER])
        ps = s.ps("ps", [P, 4, INNER])
        w_in = s.sem("w_in")
        made = s.sem("made")
        copied = s.sem("copied")
        stored = s.sem("stored")
        block = s.block()

        @block.sync
        def _(sp):
            sp.dma_start(w[:, 0, :], wv[0:P, :]).then_inc(w_in, 16)
            sp.dma_start(w[0:DC - P, 1, :], wv[P:DC, :]).then_inc(w_in, 16)
            sp.wait_ge(copied, KT)
            full = (KT - 1) * P
            sp.dma_start(v_dram[0:full, :].rearrange("(t p) d -> p t d", p=P), v[:, 0:KT - 1, :]).then_inc(stored, 16)
            sp.dma_start(v_dram[full:NC_, :], v[0:LASTK, KT - 1, :]).then_inc(stored, 16)
            sp.wait_ge(stored, 32)

        @block.tensor
        def _(pe):
            pe.wait_ge(w_in, 32)
            for t in range(KT):
                n = key_rows(t)
                if t >= 4:
                    pe.wait_ge(copied, t - 3)
                pe.matmul(ps[0:n, t % 4, :], ctx_t[:, 0, t * P:t * P + n], w[:, 0, :], start=True, stop=False)
                pe.matmul(ps[0:n, t % 4, :], ctx_t[0:DC - P, 1, t * P:t * P + n], w[0:DC - P, 1, :],
                          start=False, stop=True).then_inc(made, 1)

        @block.scalar
        def _(act):
            for t in range(KT):
                n = key_rows(t)
                act.wait_ge(made, t + 1)
                act.activation(v[0:n, t, :], ps[0:n, t % 4, :], ACT.Copy).then_inc(copied, 1)


KCOLS = [(0, CH), (CH, CH), (2 * CH, CH), (3 * CH, NC_ - 3 * CH)]
MCOLS = [(0, CH), (CH, CH), (2 * CH, CH), (3 * CH - 1, NC_ - 3 * CH + 1)]
QT = NQ // P


SLOTS_PC = 3 * KT
LEAD = 6


def attention_order():
    chunks = PAIRS * NCH

    def project(g):
        if g >= chunks:
            return []
        p, c = divmod(g, NCH)
        return [("project", p, u, 0) for u in ([0, 1, 2, 3] if c == 0 else []) + [4 + c]]

    def maxima(g):
        if g >= chunks:
            return []
        p, c = divmod(g, NCH)
        return [("max", p, h * QT + qt, j) for h in range(2) for qt in range(4 * c, 4 * c + 4) for j in range(4)] \
            + [("shift", p, c, 0)]

    steps = NCH * KT
    out = project(0) + project(1) + maxima(0)
    for g in range(chunks):
        side = project(g + 2) + maxima(g + 1)
        total, slot = len(side), 0

        def fill():
            while side and total - len(side) < (slot + 1) * total / (SLOTS_PC - LEAD):
                out.append(side.pop(0))
        for n in range(g * KT, (g + 1) * KT):
            for h in range(2):
                out.append(("scores", n // steps, n % steps, h))
                fill()
                slot += 1
            if n >= 2:
                out.append(("values", (n - 2) // steps, (n - 2) % steps, 0))
                if (n - 2) % KT == KT - 1:
                    out.append(("sums", (n - 2) // steps, (n - 2) % steps // KT, 0))
            fill()
            slot += 1
    for n in range(PAIRS * steps - 2, PAIRS * steps):
        out.append(("values", n // steps, n % steps, 0))
    return out + [("sums", PAIRS - 1, NCH - 1, 0)]


def attention_phase(nc, tag, hn, ctx_t, wq, wk, v_dram, o_dram, s_dram, ident, ones64):
    with Scope(nc, tag) as s:
        w = s.sb("w", [P, 2, 2, P])
        hi = s.sb("hi", [P, 2, CH], F32R)
        lo = s.sb("lo", [P, 2, CH], F32R)
        q_dup = [[s.sb(f"q_dup{b}{h}", [P, NQ], F32R) for h in range(2)] for b in range(2)]
        q_low = [[s.sb(f"q_low{b}{h}", [DH + 1, NQ], F32R) for h in range(2)] for b in range(2)]
        k_both = [[s.sb(f"k_both{b}{h}", [P, NC_ + 1], F32R) for h in range(2)] for b in range(2)]
        k_one = [[s.sb(f"k_one{b}{h}", [DH + 1, NC_ + 1], F32R) for h in range(2)] for b in range(2)]
        v = s.sb("v", [P, 2, KT, P])
        probs = s.sb("probs", [P, 3, 2, CH])
        psum_p = s.sb("psum_p", [P, 2, CH])
        o_sb = s.sb("o_sb", [P, CH])
        s_sb = s.sb("s_sb", [P, CH])
        mx = s.sb("mx", [P, 2, 8, 4])
        negmax = s.sb("negmax", [P, 8])
        negmax_t = s.sb("negmax_t", [8, P], F32R)
        st = s.ps("st", [P, 2, 2, CH])
        av = s.ps("av", [P, 2, CH])
        ring = s.ps("ring", [P, 2, CH])
        w_in = s.sem("w_in")
        v_in = [s.sem(f"v_in{i}") for i in range(2)]
        hi_done = s.sem("hi_done")
        spread = [s.sem(f"spread{i}") for i in range(2)]
        ring_full = s.sem("ring_full")
        ring_read = s.sem("ring_read")
        neg_done = s.sem("neg_done")
        shift_in = s.sem("shift_in")
        scored = s.sem("scored")
        exped = s.sem("exped")
        weighed = s.sem("weighed")
        summed = s.sem("summed")
        outed = s.sem("outed")
        o_stored = s.sem("o_stored")
        s_stored = s.sem("s_stored")
        ones_set = s.sem("ones_set")
        block = s.block()

        order = attention_order()
        STEPS = NCH * KT
        RINGED = ("project", "max", "shift", "sums")
        ring_at = {op: n for n, op in enumerate(op for op in order if op[0] in RINGED)}

        def step(p, i):
            return p * STEPS + i, i // KT, i % KT

        def adds_through(p, i):
            return (p * NCH + i // KT) * (KT - 1) + max(i % KT, 1)

        def ring_of(kind, g):
            return ring_at[(kind, g // NCH, g % NCH, 0)]

        def spread_through(p, c, i):
            last = 8 * p + 4 + c
            return 96 * ((last - i) // 2 + 1)

        @block.sync
        def _(sp):
            for op in order:
                kind, p, u, _ = op
                r = ring_at.get(op)
                if kind == "shift":
                    sp.wait_ge(ring_read, r + 1)
                    for h in range(2):
                        sp.dma_start(q_low[p % 2][h][DH:DH + 1, u * CH:(u + 1) * CH].bitcast(F32).rearrange("a (t q) -> a t q", q=P),
                                     negmax_t[4 * h:4 * h + 4, :].bitcast(F32)).then_inc(shift_in, 16)
                if kind == "sums":
                    sp.wait_ge(ring_read, r + 1)
                    for h in range(2):
                        sp.dma_start(s_dram[2 * p + h:2 * p + h + 1, u * CH:(u + 1) * CH], s_sb[h * DH:h * DH + 1, :]).then_inc(s_stored, 16)
                    sp.wait_ge(outed, p * NCH + u + 1)
                    sp.dma_start(o_dram[p * P:(p + 1) * P, u * CH:(u + 1) * CH], o_sb[:, :]).then_inc(o_stored, 16)
                if kind == "project":
                    b, n = p % 2, 8 * p + u
                    if u == 0:
                        if p:
                            sp.wait_ge(ring_full, ring_at[("project", p - 1, 7, 0)] + 1)
                        cols = slice(p * P, (p + 1) * P)
                        sp.dma_start(w[:, 0, 0, :], wk[0:P, cols]).then_inc(w_in, 16)
                        sp.dma_start(w[0:DC - P, 1, 0, :], wk[P:DC, cols]).then_inc(w_in, 16)
                        sp.dma_start(w[:, :, 1, :], wq[:, cols].rearrange("(k p) d -> p k d", p=P)).then_inc(w_in, 16)
                        if p >= 2:
                            sp.wait_ge(weighed, STEPS * (p - 1))
                        full = (KT - 1) * P
                        sp.dma_start(v[:, b, 0:KT - 1, :], v_dram[0:full, cols].rearrange("(t p) d -> p t d", p=P)).then_inc(v_in[b], 16)
                        sp.dma_start(v[0:LASTK, b, KT - 1, :], v_dram[full:NC_, cols]).then_inc(v_in[b], 16)
                    sp.wait_ge(ring_read, r + 1)
                    c0, m = KCOLS[u] if u < 4 else ((u - 4) * CH, CH)
                    for h in range(2):
                        h_hi, h_lo = hi[h * DH:(h + 1) * DH, n % 2, 0:m], lo[h * DH:(h + 1) * DH, n % 2, 0:m]
                        if u < 4:
                            to = ((k_both[b][h][0:DH], h_hi), (k_both[b][h][DH:P], h_lo), (k_one[b][h][0:DH], h_hi))
                        else:
                            to = ((q_dup[b][h][0:DH], h_hi), (q_dup[b][h][DH:P], h_hi), (q_low[b][h][0:DH], h_lo))
                        for dst, src in to:
                            sp.dma_start(dst[:, c0:c0 + m].bitcast(F32), src.bitcast(F32)).then_inc(spread[n % 2], 16)
            sp.wait_ge(o_stored, 16 * PAIRS * NCH)
            sp.wait_ge(s_stored, 32 * PAIRS * NCH)

        @block.gpsimd
        def _(pool):
            for b in range(2):
                for h in range(2):
                    pool.memset(k_one[b][h][DH:DH + 1, :].bitcast(F32), 1.0).then_inc(ones_set, 1)
            for kind, p, u, h in order:
                if kind == "scores" and h == 1:
                    n, c, t = step(p, u)
                    if t == 0:
                        continue
                    rows = key_rows(t)
                    pool.wait_ge(exped, n + 1)
                    if t == 1:
                        if p or c:
                            pool.wait_ge(ring_full, ring_of("sums", p * NCH + c - 1) + 1)
                        a = probs[:, (n - 1) % 3, :, :]
                    else:
                        pool.wait_ge(summed, adds_through(p, u) - 1)
                        a = psum_p[0:rows, :, :]
                    pool.tensor_tensor(psum_p[0:rows, :, :], probs[0:rows, n % 3, :, :], a[0:rows], ALU.add).then_inc(summed, 1)

        @block.scalar
        def _(act):
            for kind, p, u, h in order:
                if kind == "scores" and h == 1:
                    n, c, t = step(p, u)
                    rows = key_rows(t)
                    act.wait_ge(scored, n + 1)
                    if n >= 3:
                        act.wait_ge(weighed, n - 2)
                        act.wait_ge(summed, adds_through(*divmod(n - 3, STEPS)))
                    act.activation(probs[0:rows, n % 3, :, :], st[0:rows, n % 2, :, :], ACT.Exp,
                                   scale=DH ** -0.5).then_inc(exped, 1)
                if kind == "sums":
                    g = p * NCH + u
                    act.wait_ge(weighed, (g + 1) * KT)
                    if g:
                        act.wait_ge(o_stored, 16 * g)
                    act.activation(o_sb[:, :], av[:, g % 2, :], ACT.Copy).then_inc(outed, 1)

        @block.vector
        def _(dve):
            for op in order:
                kind, p, u, t = op
                b, r = p % 2, ring_at.get(op)
                if kind == "project":
                    n, m = 8 * p + u, KCOLS[u][1] if u < 4 else CH
                    dve.wait_ge(ring_full, r + 1)
                    if n >= 2:
                        dve.wait_ge(spread[n % 2], 96 * (n // 2))
                    dve.tensor_copy(hi[:, n % 2, 0:m], ring[:, r % 2, 0:m]).then_inc(hi_done, 1)
                    dve.wait_ge(hi_done, n + 1)
                    dve.tensor_tensor(lo[:, n % 2, 0:m], ring[:, r % 2, 0:m], hi[:, n % 2, 0:m].bitcast(F32),
                                      ALU.subtract).then_inc(ring_read, 1)
                if kind == "max":
                    h, qt = divmod(u, QT)
                    g = p * NCH + qt // 4
                    if h == 0 and qt % 4 == 0 and t == 0 and g >= 2:
                        dve.wait_ge(neg_done, 2 * (g - 1))
                    dve.wait_ge(ring_full, r + 1)
                    dve.reduce_max(mx[:, g % 2, 4 * h + qt % 4, t:t + 1], ring[:, r % 2, 0:MCOLS[t][1]], AX.X).then_inc(ring_read, 1)
                if kind == "shift":
                    g = p * NCH + u
                    dve.wait_ge(ring_read, r)
                    if g:
                        dve.wait_ge(ring_full, ring_of("shift", g - 1) + 1)
                    dve.reduce_max(negmax[:, :], mx[:, g % 2, :, :], AX.X).then_inc(neg_done, 1)
                    dve.wait_ge(neg_done, 2 * g + 1)
                    dve.tensor_scalar(negmax[:, :], negmax[:, :], -1.0, None, ALU.mult).then_inc(neg_done, 1)
                    dve.wait_ge(ring_full, r + 1)
                    if g:
                        dve.wait_ge(shift_in, 32 * g)
                    dve.tensor_copy(negmax_t[:, :], ring[0:8, r % 2, 0:P]).then_inc(ring_read, 1)
                if kind == "sums":
                    g = p * NCH + u
                    dve.wait_ge(ring_full, r + 1)
                    if g:
                        dve.wait_ge(s_stored, 32 * g)
                    dve.tensor_copy(s_sb[:, :], ring[:, r % 2, :]).then_inc(ring_read, 1)

        @block.tensor
        def _(pe):
            pe.wait_ge(ones_set, 4)
            for op in order:
                kind, p, u, t = op
                b, r = p % 2, ring_at.get(op)
                if r is not None and r >= 2:
                    pe.wait_ge(ring_read, r - 1)
                if kind == "project":
                    if u == 0:
                        pe.wait_ge(w_in, 48 * (p + 1))
                    if u < 4:
                        c0, m = KCOLS[u]
                        pe.matmul(ring[:, r % 2, 0:m], w[:, 0, 0, :], ctx_t[:, 0, c0:c0 + m], start=True, stop=False)
                        last = pe.matmul(ring[:, r % 2, 0:m], w[0:DC - P, 1, 0, :], ctx_t[0:DC - P, 1, c0:c0 + m],
                                         start=False, stop=True)
                    else:
                        c0 = (u - 4) * CH
                        for k in range(DT):
                            last = pe.matmul(ring[:, r % 2, :], w[:, k, 1, :], hn[:, k, c0:c0 + CH],
                                             start=k == 0, stop=k == DT - 1)
                    last.then_inc(ring_full, 1)
                if kind == "max":
                    h, qt = divmod(u, QT)
                    if h == 0 and qt % 4 == 0 and t == 0:
                        for i in range(2):
                            pe.wait_ge(spread[i], spread_through(p, qt // 4, i))
                    c0, m = MCOLS[t]
                    pe.matmul(ring[:, r % 2, 0:m], q_dup[b][h][:, qt * P:(qt + 1) * P],
                              k_both[b][h][:, c0:c0 + m], start=True, stop=True).then_inc(ring_full, 1)
                if kind == "shift":
                    pe.wait_ge(neg_done, 2 * (p * NCH + u + 1))
                    pe.transpose(ring[0:8, r % 2, 0:P], negmax[:, :], ident[:, :]).then_inc(ring_full, 1)
                if kind == "scores":
                    n, c, kt = step(p, u)
                    h = t
                    rows, keys, qs = key_rows(kt), slice(kt * P, kt * P + key_rows(kt)), slice(c * CH, (c + 1) * CH)
                    if kt == 0 and h == 0:
                        pe.wait_ge(shift_in, 32 * (p * NCH + c + 1))
                    if n >= 2 and h == 0:
                        pe.wait_ge(exped, n - 1)
                    pe.matmul(st[0:rows, n % 2, h, :], k_both[b][h][:, keys], q_dup[b][h][:, qs], start=True, stop=False)
                    last = pe.matmul(st[0:rows, n % 2, h, :], k_one[b][h][:, keys], q_low[b][h][:, qs],
                                     start=False, stop=True)
                    if h == 1:
                        last.then_inc(scored, 1)
                if kind == "values":
                    n, c, kt = step(p, u)
                    rows, m = key_rows(kt), p * NCH + c
                    if u == 0:
                        pe.wait_ge(v_in[b], 32 * (p // 2 + 1))
                    pe.wait_ge(exped, n + 1)
                    if kt == 0 and m >= 2:
                        pe.wait_ge(outed, m - 1)
                    for h in range(2):
                        last = pe.matmul(av[h * DH:(h + 1) * DH, m % 2, :], v[0:rows, b, kt, h * DH:(h + 1) * DH],
                                         probs[0:rows, n % 3, h, :], start=kt == 0, stop=kt == KT - 1)
                    last.then_inc(weighed, 1)
                if kind == "sums":
                    pe.wait_ge(summed, (p * NCH + u + 1) * (KT - 1))
                    for h in range(2):
                        last = pe.matmul(ring[h * DH:(h + 1) * DH, r % 2, :], ones64[:, :], psum_p[:, h, :],
                                         start=True, stop=True)
                    last.then_inc(ring_full, 1)


def output_phase(nc, tag, o_dram, s_dram, r_dram, wo, bo, resid):
    with Scope(nc, tag) as s:
        w = s.sb("w", [P, PAIRS, D])
        bias = s.sb("bias", [P, DT])
        o = s.sb("o", [P, PAIRS, NQ])
        inv = s.sb("inv", [P, PAIRS, NQ])
        compact = s.sb("compact", [P, HEADS * NQ // P])
        s_in, r_stored, inverted, divided = s.sem("s_in"), s.sem("r_stored"), s.sem("inverted"), s.sem("divided")
        r_in = [s.sem(f"r_in{c}") for c in range(NCH)]
        ps = s.ps("ps", [P, 4, CH])
        w_in = s.sem("w_in")
        o_in = [s.sem(f"o_in{c}") for c in range(NCH)]
        made = s.sem("made")
        added = s.sem("added")
        block = s.block()

        @block.sync
        def _(sp):
            rows = "h (r q) -> (h r) q"
            sp.dma_start(compact[:, :], s_dram.rearrange(rows, q=P)).then_inc(s_in, 16)
            sp.dma_start(w[:, :, :], wo.rearrange("(k p) d -> p k d", p=P)).then_inc(w_in, 16)
            sp.dma_start(bias[:, :], bo.rearrange("(k p) -> p k", p=P), allow_slow_non_contiguous=True).then_inc(w_in, 16)
            for c in range(NCH):
                sp.dma_start(o[:, :, c * CH:(c + 1) * CH],
                             o_dram[:, c * CH:(c + 1) * CH].rearrange("(k p) q -> p k q", p=P)).then_inc(o_in[c], 16)
            sp.wait_ge(inverted, 1)
            sp.dma_start(r_dram.rearrange(rows, q=P), compact[:, :]).then_inc(r_stored, 16)
            sp.wait_ge(r_stored, 16)
            for c in range(NCH):
                for h in range(2):
                    src = r_dram[:, c * CH:(c + 1) * CH].rearrange("(m a h) q -> h a m q", a=1, h=2)[h]
                    sp.dma_start(inv[h * DH:(h + 1) * DH, :, c * CH:(c + 1) * CH],
                                 src.broadcast_to([DH, PAIRS, CH])).then_inc(r_in[c], 16)

        @block.tensor
        def _(pe):
            pe.wait_ge(w_in, 32)
            for c in range(NCH):
                pe.wait_ge(divided, c + 1)
                for m in range(DT):
                    n = DT * c + m
                    if n >= 4:
                        pe.wait_ge(added, n - 3)
                    for k in range(PAIRS):
                        last = pe.matmul(ps[:, n % 4, :], w[:, k, m * P:(m + 1) * P], o[:, k, c * CH:(c + 1) * CH],
                                         start=k == 0, stop=k == PAIRS - 1)
                    last.then_inc(made, 1)

        @block.vector
        def _(dve):
            dve.wait_ge(s_in, 16)
            dve.reciprocal(compact[:, :], compact[:, :]).then_inc(inverted, 1)

            def divide(c):
                dve.wait_ge(o_in[c], 16)
                dve.wait_ge(r_in[c], 32)
                part = slice(c * CH, (c + 1) * CH)
                dve.tensor_tensor(o[:, :, part], o[:, :, part], inv[:, :, part], ALU.mult).then_inc(divided, 1)

            divide(0)
            for n in range(NCH * DT):
                c, m = divmod(n, DT)
                if m == 0 and c + 1 < NCH:
                    divide(c + 1)
                dve.wait_ge(made, n + 1)
                part = resid[:, m, c * CH:(c + 1) * CH]
                dve.scalar_tensor_tensor(part, ps[:, n % 4, :], bias[:, m:m + 1], part, ALU.add, ALU.add).then_inc(added, 1)



def butterfly_phase(nc, w_exp, b_exp, up_w, up_b, down_w, w_con, b_con, down_b, ident, w_up, b_up, w_down, b_out):
    HALF = HID0 // 2
    with Scope(nc, "fold") as s:
        up = [s.sb(f"up{i}", [P, DT, HID0]) for i in range(2)]
        down = [s.sb(f"down{i}", [P, DT, HID0]) for i in range(2)]
        row = [s.sb(f"row{i}", [1, HID0]) for i in range(2)]
        wb = [s.sb(f"wb{i}", [P, HALF * 4]) for i in range(4)]
        t_dve = s.sb("t_dve", [P, 2, HALF])
        t_pool = s.sb("t_pool", [P, 2, HALF])
        con = s.sb("con", [P, HT0, D])
        biases = s.sb("biases", [P, DT, 2])
        upb = s.sb("upb", [P, HT0])
        tp = s.ps("tp", [P, 4, 4, P])
        w_in = s.sem("w_in")
        con_in = s.sem("con_in")
        stage_in = [s.sem(f"stage_in{i}") for i in range(4)]
        turned = s.sem("turned")
        taken = s.sem("taken")
        dve_step = s.sem("dve_step")
        pool_step = s.sem("pool_step")
        dve_stage = s.sem("dve_stage")
        pool_stage = s.sem("pool_stage")
        back = s.sem("back")
        row_t = s.sem("row_t")
        block = s.block()

        @block.sync
        def _(sp):
            sp.dma_start(con[:, :, :], w_con.rearrange("(t p) d -> p t d", p=P)).then_inc(con_in, 16)
            sp.dma_start(up[0][:, :, :], w_exp.rearrange("(k p) h -> p k h", p=P)).then_inc(w_in, 16)
            sp.dma_start(row[0][:, :], b_exp.rearrange("(a h) -> a h", a=1)).then_inc(w_in, 16)
            sp.dma_start(upb[:, :], up_b.rearrange("(t p) -> p t", p=P), allow_slow_non_contiguous=True).then_inc(w_in, 16)
            sp.dma_start(biases[:, :, 0], b_con.rearrange("(t p) -> p t", p=P), allow_slow_non_contiguous=True).then_inc(w_in, 16)
            sp.dma_start(biases[:, :, 1], down_b.rearrange("(t p) -> p t", p=P), allow_slow_non_contiguous=True).then_inc(w_in, 16)
            for i in range(STAGES):
                if i >= 2:
                    sp.wait_ge(dve_stage, i - 1)
                sp.dma_start(wb[i % 2][:, :], down_w[STAGES - 1 - i].rearrange("(a n) i j -> a (n i j)", a=1).broadcast_to([P, HALF * 4])).then_inc(stage_in[i % 2], 16)
                if i >= 2:
                    sp.wait_ge(pool_stage, i - 1)
                sp.dma_start(wb[2 + i % 2][:, :], up_w[i].rearrange("(a n) i j -> a (n i j)", a=1).broadcast_to([P, HALF * 4])).then_inc(stage_in[2 + i % 2], 16)

        def stage(eng, step, count, src, dst, tmp, weights, stride, swap, rows):
            def halves(t):
                v = t.rearrange("p (n h s) -> p n h s", h=2, s=stride)
                return v[:, :, 0, :], v[:, :, 1, :]
            a, b = halves(src)
            oa, ob = halves(dst)
            wv = weights.rearrange("p (n s i j) -> p n s i j", s=stride, i=2, j=2)
            shape = lambda t: t.rearrange("p (n s) -> p n s", s=stride)
            for n, (o, i0, i1) in enumerate(((oa, (0, 0), (0, 1)), (ob, (1, 0), (1, 1)))):
                if swap:
                    i0, i1 = i0[::-1], i1[::-1]
                t = shape(tmp[0:rows, n, :])
                eng.tensor_tensor(o, a, wv[0:rows, :, :, i0[0], i0[1]], ALU.mult).then_inc(step, 1)
                eng.tensor_tensor(t, b, wv[0:rows, :, :, i1[0], i1[1]], ALU.mult).then_inc(step, 1)
                count += 2
                eng.wait_ge(step, count)
                eng.tensor_tensor(o, o, t, ALU.add).then_inc(step, 1)
                count += 1
            eng.wait_ge(step, count)
            return count

        @block.gpsimd
        def _(pool):
            pool.wait_ge(w_in, 80)
            count = 0
            for i in range(STAGES):
                pool.wait_ge(stage_in[2 + i % 2], 16 * (i // 2 + 1))
                for k in range(DT):
                    count = stage(pool, pool_step, count, up[i % 2][:, k, :], up[(i + 1) % 2][:, k, :], t_pool,
                                  wb[2 + i % 2], 2 ** i, False, P)
                count = stage(pool, pool_step, count, row[i % 2][:, :], row[(i + 1) % 2][:, :], t_pool,
                              wb[2 + i % 2][0:1, :], 2 ** i, False, 1)
                pool.sem_inc(pool_stage, 1)
            for k in range(DT):
                pool.tensor_copy(w_up[:, k, :], up[0][:, k, :]).then_inc(pool_step, 1)
            pool.tensor_tensor(b_out[:, :], biases[:, :, 0], biases[:, :, 1], ALU.add).then_inc(pool_step, 1)

        @block.vector
        def _(dve):
            for n in range(4):
                k, g = divmod(n, 2)
                dve.wait_ge(turned, n + 1)
                dve.tensor_copy(down[0][:, k, g * CH:(g + 1) * CH], tp[:, n, :, :].rearrange("p j q -> p (j q)")).then_inc(taken, 1)
            dve.wait_ge(taken, 4)
            count = 0
            for i in range(STAGES):
                dve.wait_ge(stage_in[i % 2], 16 * (i // 2 + 1))
                for k in range(DT):
                    count = stage(dve, dve_step, count, down[i % 2][:, k, :], down[(i + 1) % 2][:, k, :], t_dve,
                                  wb[i % 2], 2 ** (STAGES - 1 - i), True, P)
                dve.engine_nop().then_inc(dve_stage, 1)
            for n in range(4):
                dve.wait_ge(back, n + 1)
                dve.tensor_copy(w_down[:, 2 * n:2 * n + 2, :].rearrange("p t d -> p (t d)"),
                                tp[:, n, :, :].rearrange("p j q -> p (j q)")).then_inc(taken, 1)
            dve.wait_ge(row_t, 1)
            dve.wait_ge(w_in, 80)
            dve.tensor_tensor(b_up[:, :], tp[:, 0, 0, 0:HT0], upb[:, :], ALU.add).then_inc(taken, 1)

        @block.tensor
        def _(pe):
            pe.wait_ge(con_in, 16)
            for n in range(4):
                k, g = divmod(n, 2)
                for j in range(4):
                    last = pe.transpose(tp[:, n, j, :], con[:, 4 * g + j, k * P:(k + 1) * P], ident[:, :])
                last.then_inc(turned, 1)
            pe.wait_ge(dve_stage, STAGES)
            for n in range(4):
                for j in range(4):
                    t, k = divmod(4 * n + j, DT)
                    last = pe.transpose(tp[:, n, j, :], down[0][:, k, t * P:(t + 1) * P], ident[:, :])
                last.then_inc(back, 1)
            pe.wait_ge(taken, 5)
            pe.wait_ge(pool_stage, STAGES)
            for t in range(HT0):
                last = pe.matmul(tp[:, 0, 0, t:t + 1], row[0][:, t * P:(t + 1) * P], ident[0:1, 0:1], start=True, stop=True)
            last.then_inc(row_t, 1)


def butterfly_ffn_phase(nc, hn, w_up, b_up, w_down, b_out, resid):
    with Scope(nc, "ffn0") as s:
        g = s.sb("g", [P, 2, HT0, CH])
        hid = s.ps("hid", [P, 4, CH])
        ps = s.ps("ps", [P, 2, CH])
        made = s.sem("made")
        gelued = s.sem("gelued")
        out_done = s.sem("out_done")
        added = s.sem("added")
        block = s.block()

        @block.tensor
        def _(pe):
            def up(c):
                for j in range(HT0):
                    n = c * HT0 + j
                    if n >= 4:
                        pe.wait_ge(gelued, n - 3)
                    for k in range(DT):
                        last = pe.matmul(hid[:, n % 4, :], w_up[:, k, j * P:(j + 1) * P], hn[:, k, c * CH:(c + 1) * CH],
                                         start=k == 0, stop=k == DT - 1)
                    last.then_inc(made, 1)

            def down(c):
                pe.wait_ge(gelued, (c + 1) * HT0)
                for m in range(DT):
                    n = c * DT + m
                    if n >= 2:
                        pe.wait_ge(added, n - 1)
                    for j in range(HT0):
                        last = pe.matmul(ps[:, m, :], w_down[:, j, m * P:(m + 1) * P], g[:, c % 2, j, :],
                                         start=j == 0, stop=j == HT0 - 1)
                    last.then_inc(out_done, 1)

            up(0)
            for c in range(1, NCH):
                up(c)
                down(c - 1)
            down(NCH - 1)

        @block.scalar
        def _(act):
            for n in range(NCH * HT0):
                c, j = divmod(n, HT0)
                act.wait_ge(made, n + 1)
                if c >= 2:
                    act.wait_ge(out_done, DT * (c - 1))
                act.activation(g[:, c % 2, j, :], hid[:, n % 4, :], ACT.Gelu, bias=b_up[:, j:j + 1]).then_inc(gelued, 1)

        @block.vector
        def _(dve):
            for n in range(NCH * DT):
                c, m = divmod(n, DT)
                dve.wait_ge(out_done, n + 1)
                part = resid[:, m, c * CH:(c + 1) * CH]
                dve.scalar_tensor_tensor(part, ps[:, m, :], b_out[:, m:m + 1], part, ALU.add, ALU.add).then_inc(added, 1)



UNITS = 2 * PAIRS
QK_SCALE = 8.0
HALF = DH // 2
INV_LOW = 32
INV_ROWS = INV_LOW + 2 * UNITS
NLOADS = 24
WPC = CH // WIN
SLOTS = WPC * PAIRS
KW = CH + WIN
RING_V = UNITS
RING_INV = RING_V + WPC
RING_OUT = RING_INV + UNITS
RING = RING_OUT + DT
BACK_AG = 2
BACK_Y = BACK_AG + 2 * HT1
BACK = BACK_Y + DT


def layer_phase(nc, tag, a, l, y, y_mid, cst, ident, ones_mean, eps):
    with Scope(nc, tag) as s:
        PB = 3
        wqkv = s.sb("wqkv", [P, DT, 3 * INNER])
        wo = s.sb("wo", [P, PAIRS, D])
        w1 = s.sb("w1", [P, DT, 2 * HID1])
        w2 = s.sb("w2", [P, HT1, D])
        b1 = s.sb("b1", [P, 2, HT1])
        b2 = s.sb("b2", [P, DT])
        ln_g = s.sb("ln_g", [P, DT])
        ln_b = s.sb("ln_b", [P, DT])
        scales = s.sb("scales", [P, 2, 2])
        table = s.sb("table", [P, 4, CH])
        raw = s.sb("raw", [P, UNITS, CH])
        sq = s.sb("sq", [P, 2, CH])
        norm = sq[0:2 * UNITS, 0, :]
        inv_parts = s.sb("inv_parts", [INV_ROWS, CH], F32R)
        t_cos = s.sb("t_cos", [P, 2, CH])
        t_sin = s.sb("t_sin", [P, 2, CH])
        qr = s.sb("qr", [P, PAIRS, 2, CH])
        kr = s.sb("kr", [P, PAIRS, KW])
        v = s.sb("v", [P, WPC + 1, INNER])
        y_stage = s.sb("y_stage", [P, DT, CH])
        mx = s.sb("mx", [P, 4, 2])
        neg = s.sb("neg", [P, 4, 2])
        den = s.sb("den", [P, 4, 2])
        rden = s.sb("rden", [P, 4, 2])
        probs = s.sb("probs", [P, PB, 2, 2 * WIN])
        probs_t = s.sb("probs_t", [P, 2, 4, WIN])
        o = s.sb("o", [P, PAIRS, CH])
        hn = s.sb("hn", [P, DT, CH])
        std = s.sb("std", [P, CH])
        gel = s.sb("gel", [P, 2, CH])
        hid = s.sb("hid", [P, HT1, CH])
        ring = s.ps("ring", [P, 2, CH])
        st = s.ps("st", [P, 2, 2, 2 * WIN])
        tp = s.ps("tp", [P, 4, WIN])
        ov = s.ps("ov", [P, PAIRS, WIN])
        back = s.ps("back", [P, 2, CH])
        sem = s.sem
        w_in, v_zero, table_in = sem("w_in"), sem("v_zero"), sem("table_in")
        ring_full, n2_full, st_full, tp_full, av_done = sem("ring_full"), sem("n2_full"), sem("st_full"), sem("tp_full"), sem("av_done")
        n2_part = sem("n2_part")
        raw_copied, squared, v_copied, norm_done = sem("raw_copied"), sem("squared"), sem("v_copied"), sem("norm_done")
        exped, pt_copied, o_copied = sem("exped"), sem("pt_copied"), sem("o_copied")
        clipped, rnormed, sin_done, qk_done = sem("clipped"), sem("rnormed"), sem("sin_done"), sem("qk_done")
        maxed, negged, inverted, p_normed, mid_done = sem("maxed"), sem("negged"), sem("inverted"), sem("p_normed"), sem("mid_done")
        turned_in = [sem(f"turned_in{i}") for i in range(2)]
        inv_split, inv_zero = sem("inv_split"), sem("inv_zero")
        cos_done, rotated, kv_moved, staged, table_scaled = sem("cos_done"), sem("rotated"), sem("kv_moved"), sem("staged"), sem("table_scaled")
        back_full, hsquared, std_done, gelued = sem("back_full"), sem("hsquared"), sem("std_done"), sem("gelued")
        centred, inv_std, scaled, affined, gated, y_done = sem("centred"), sem("inv_std"), sem("scaled"), sem("affined"), sem("gated"), sem("y_done")
        block = s.block()

        def iterations(eng, body):
            body(0, None)
            with eng.Fori(1, NCH) as c:
                body(c, c - 1)
            body(None, NCH - 1)

        def ring_free(pe, c, pos):
            if pos < 2:
                if isinstance(c, int) and c == 0:
                    return
                pe.wait_ge(mid_done, DT * c + pos - 1)
            elif pos - 2 < RING_V:
                pe.wait_ge(squared, UNITS * c + pos - 1)
            elif pos - 2 < RING_INV:
                pe.wait_ge(v_copied, WPC * c + pos - 1 - RING_V)
            elif pos - 2 < RING_OUT:
                pe.wait_ge(qk_done, UNITS * c + pos - 1 - RING_INV)

        def back_free(pe, c, pos):
            if pos < 2:
                pe.wait_ge(y_done, DT * c + pos + 1)
            elif pos == 2:
                pe.wait_ge(centred, DT * (c + 1))
            elif pos == 3:
                pe.wait_ge(std_done, c + 1)
            else:
                j, i = divmod(pos - 2 - BACK_AG, 2)
                pe.wait_ge(gated if i else gelued, HT1 * c + j + 1)

        def toks(c, shifted):
            return bass.ds(c * CH + (0 if shifted else 1), CH)

        @block.sync
        def _(sp):
            slow = dict(allow_slow_non_contiguous=True)
            loads = [(wqkv[:, :, :], a["L1_ffn_wqkv"][l].rearrange("(k p) n -> p k n", p=P), {}),
                     (wo[:, :, :], a["L1_ffn_wo"][l].rearrange("(k p) n -> p k n", p=P), {}),
                     (w1[:, :, :], a["L1_ffn_w1"][l].rearrange("(k p) n -> p k n", p=P), {}),
                     (w2[:, 0:HT1 - 1, :], a["L1_ffn_w2"][l, 0:(HT1 - 1) * P, :].rearrange("(k p) n -> p k n", p=P), {}),
                     (w2[0:LASTH, HT1 - 1, :], a["L1_ffn_w2"][l, (HT1 - 1) * P:HID1, :], {})]
            for i in range(2):
                bv = a["L1_ffn_b1"][l, i * HID1:(i + 1) * HID1]
                loads += [(b1[:, i, 0:HT1 - 1], bv[0:(HT1 - 1) * P].rearrange("(k p) -> p k", p=P), slow),
                          (b1[0:LASTH, i, HT1 - 1:HT1], bv[(HT1 - 1) * P:HID1].rearrange("(p a) -> p a", a=1), {})]
            for t, n in ((b2, "b2"), (ln_g, "ln_g"), (ln_b, "ln_b")):
                loads.append((t[:, :], a["L1_ffn_" + n][l].rearrange("(k p) -> p k", p=P), slow))
            for i, n in enumerate(("L1_ffn_q_scale", "L1_ffn_k_scale")):
                sv = a[n][l].rearrange("(p a) -> p a", a=1)
                for h in range(2):
                    r = h * DH
                    loads += [(scales[r:r + DH, i, 0:1], sv, {}),
                              (scales[r:r + DH // 2, i, 1:2], sv[DH // 2:DH], {}),
                              (scales[r + DH // 2:r + DH, i, 1:2], sv[0:DH // 2], {})]
            for dst, src, kw in loads:
                sp.dma_start(dst, src, **kw).then_inc(w_in, 16)
            assert len(loads) == NLOADS
            for c in range(NCH):
                if c:
                    sp.wait_ge(qk_done, UNITS * c)
                sp.dma_start(table[:, :, :], cst["tables"][:, :, c * CH:(c + 1) * CH]).then_inc(table_in, 16)
                for j in range(UNITS):
                    sp.wait_ge(raw_copied, UNITS * c + j + 1)
                    if j >= 2 or c:
                        sp.wait_ge(rotated, UNITS * c + j - 1)
                    for r in range(0, P, HALF):
                        src = r + HALF if r % DH == 0 else r - HALF
                        sp.dma_start(t_sin[r:r + HALF, j % 2, :], raw[src:src + HALF, j, :]).then_inc(turned_in[j % 2], 16)


        @block.tensor
        def _(pe):
            def project(c, j):
                ring_free(pe, c, j)
                for k in range(DT):
                    last = pe.matmul(ring[:, j % 2, :], wqkv[:, k, j * P:(j + 1) * P], y[:, k, toks(c, k)],
                                     start=k == 0, stop=k == DT - 1)
                last.then_inc(ring_full, 1)

            def norm_sum(c, j):
                pe.wait_ge(squared, UNITS * c + j + 1)
                if j == 0 and not (isinstance(c, int) and c == 0):
                    pe.wait_ge(o_copied, WPC * c)
                last = pe.matmul(ov[0:2 * UNITS, :, :].rearrange("p m q -> p (m q)"), cst["sel"][:, j, :], sq[:, j % 2, :],
                                 start=j == 0, stop=j == UNITS - 1)
                last.then_inc(n2_part, 1)

            def values(c, t):
                ring_free(pe, c, RING_V + t)
                for k in range(DT):
                    pe_in = y_stage[:, k, t * P:(t + 1) * P]
                    last = pe.matmul(ring[:, t % 2, :], pe_in, wqkv[:, k, 2 * INNER:3 * INNER],
                                     start=k == 0, stop=k == DT - 1)
                last.then_inc(ring_full, 1)

            def spread_inverse(c, j):
                ring_free(pe, c, RING_INV + j)
                if j == 0:
                    pe.wait_ge(inv_split, 2 * (c + 1))
                pe.matmul(ring[:, j % 2, :], cst["sel_t"][:, j, :], inv_parts[:, :], start=True, stop=True).then_inc(ring_full, 1)

            def scores(c, u):
                w, m = divmod(u, PAIRS)
                first = isinstance(c, int) and c == 0
                if u == 0:
                    pe.wait_ge(qk_done, UNITS * (c + 1))
                    pe.wait_ge(rotated, UNITS * (c + 1))
                if u >= 2 or not first:
                    pe.wait_ge(exped, SLOTS * c + u - 1)
                mask = cst["mask_first"] if first and w == 0 else cst["mask"]
                bank = st[:, u % 2, :, :]
                pe.matmul(bank.rearrange("p h k -> p (h k)"), cst["ident_b"][:, :], mask[:, :], start=True, stop=True)
                for h in range(2):
                    last = pe.matmul(bank[:, h, :], qr[:, m, h, w * WIN:(w + 1) * WIN], kr[:, m, w * WIN:(w + 2) * WIN],
                                     start=False, stop=True, skip_group_check=True)
                last.then_inc(st_full, 1)

            def turn(c, u):
                pe.wait_ge(p_normed, SLOTS * c + u + 1)
                if u or not (isinstance(c, int) and c == 0):
                    pe.wait_ge(pt_copied, SLOTS * c + u)
                for i in range(4):
                    last = pe.transpose(tp[:, i, :], probs[:, u % PB, i // 2, (i % 2) * WIN:(i % 2 + 1) * WIN], ident[:, :])
                last.then_inc(tp_full, 1)

            def weigh(c, u):
                w, m = divmod(u, PAIRS)
                pe.wait_ge(pt_copied, SLOTS * c + u + 1)
                if u == 0:
                    pe.wait_ge(v_copied, WPC * (c + 1))
                    pe.wait_ge(norm_done, c + 1)
                elif m == 0:
                    pe.wait_ge(o_copied, WPC * c + w)
                for h in range(2):
                    for i in range(2):
                        last = pe.matmul(ov[h * DH:(h + 1) * DH, m, :], v[:, w + i, (2 * m + h) * DH:(2 * m + h + 1) * DH],
                                         probs_t[:, u % 2, 2 * h + i, :], start=i == 0, stop=i == 1)
                last.then_inc(av_done, 1)

            def output(c, m):
                pos = RING_OUT + m
                ring_free(pe, c, pos)
                pe.wait_ge(o_copied, WPC * (c + 1))
                for k in range(PAIRS):
                    last = pe.matmul(ring[:, pos % 2, :], wo[:, k, m * P:(m + 1) * P], o[:, k, :], start=k == 0, stop=k == PAIRS - 1)
                last.then_inc(ring_full, 1)

            def mean(c):
                pe.wait_ge(mid_done, DT * (c + 1))
                back_free(pe, c, 0)
                for k in range(DT):
                    last = pe.matmul(back[:, 0, :], ones_mean[:, :], y_mid[:, k, toks(c, k)], start=k == 0, stop=k == DT - 1)
                last.then_inc(back_full, 1)

            def variance(c):
                pe.wait_ge(hsquared, c + 1)
                back_free(pe, c, 1)
                for k in range(DT):
                    last = pe.matmul(back[:, 1, :], ones_mean[:, :], gel[:, k, :], start=k == 0, stop=k == DT - 1)
                last.then_inc(back_full, 1)

            def expand(c, j):
                n = hid_rows(j)
                if j == 0:
                    pe.wait_ge(affined, DT * (c + 1))
                for i in range(2):
                    back_free(pe, c, BACK_AG + 2 * j + i)
                    col = (1 - i) * HID1 + j * P
                    for k in range(DT):
                        last = pe.matmul(back[0:n, i, :], w1[:, k, col:col + n], hn[:, k, :], start=k == 0, stop=k == DT - 1)
                    last.then_inc(back_full, 1)

            def contract(c, m):
                back_free(pe, c, BACK_Y + m)
                pe.wait_ge(gated, HT1 * (c + 1))
                for j in range(HT1):
                    n = hid_rows(j)
                    last = pe.matmul(back[:, m, :], w2[0:n, j, m * P:(m + 1) * P], hid[0:n, j, :], start=j == 0, stop=j == HT1 - 1)
                last.then_inc(back_full, 1)

            def body(f, b):
                if f is None:
                    mean(b)
                if f is not None:
                    for j in range(UNITS):
                        project(f, j)
                        if j:
                            norm_sum(f, j - 1)
                        if j == 1 and b is not None:
                            mean(b)
                        if j == 6 and b is not None:
                            variance(b)
                    norm_sum(f, UNITS - 1)
                    pe.wait_ge(staged, DT * (f + 1))
                if f is None:
                    variance(b)
                if f is not None:
                    for t in range(WPC):
                        values(f, t)
                for j in range(UNITS):
                    if f is not None:
                        spread_inverse(f, j)
                    if b is not None and j >= UNITS - HT1:
                        expand(b, j - (UNITS - HT1))
                if f is not None:
                    for u in range(SLOTS + 3):
                        if u < SLOTS:
                            scores(f, u)
                        if u >= 3:
                            weigh(f, u - 3)
                        if 2 <= u <= SLOTS + 1:
                            turn(f, u - 2)
                        if b is not None and u in (1, 4):
                            contract(b, u // 4)
                    for m in range(DT):
                        output(f, m)
                else:
                    for m in range(DT):
                        contract(b, m)

            pe.wait_ge(w_in, 16 * NLOADS)
            iterations(pe, body)

        @block.scalar
        def _(act):
            def root_variance(c):
                act.wait_ge(back_full, BACK * c + 2)
                act.activation(std[:, :], back[:, 1, :], ACT.Sqrt, bias=eps[:, 0:1]).then_inc(std_done, 1)

            def body(f, b):
                if f is not None:
                    act.wait_ge(table_in, 16 * (f + 1))
                    for i in range(2):
                        act.activation(table[:, 2 * i, :], table[:, 2 * i, :], ACT.Copy, scale=scales[:, i, 0:1]).then_inc(table_scaled, 1)
                    for j in range(UNITS):
                        act.wait_ge(ring_full, RING * f + j + 1)
                        if j == 0 and not (isinstance(f, int) and f == 0):
                            act.wait_ge(qk_done, UNITS * f)
                        act.activation(raw[:, j, :], ring[:, j % 2, :], ACT.Copy).then_inc(raw_copied, 1)
                        if j >= 2:
                            act.wait_ge(n2_part, UNITS * f + j - 1)
                        act.activation(sq[:, j % 2, :], ring[:, j % 2, :], ACT.Square).then_inc(squared, 1)
                        if b is not None and j == 4:
                            act.wait_ge(centred, DT * (b + 1))
                            act.activation(gel[:, :, :], hn[:, :, :], ACT.Square).then_inc(hsquared, 1)
                    if b is not None:
                        root_variance(b)
                    act.wait_ge(n2_part, UNITS * (f + 1))
                    act.activation(norm, ov[0:2 * UNITS, :, :].rearrange("p m q -> p (m q)"), ACT.Sqrt).then_inc(norm_done, 1)
                else:
                    act.wait_ge(centred, DT * (b + 1))
                    act.activation(gel[:, :, :], hn[:, :, :], ACT.Square).then_inc(hsquared, 1)
                    root_variance(b)
                if f is not None:
                    for t in range(WPC):
                        act.wait_ge(ring_full, RING * f + RING_V + t + 1)
                        if t == 0 and not (isinstance(f, int) and f == 0):
                            act.wait_ge(kv_moved, 2 * f)
                        act.activation(v[:, t + 1, :], ring[:, t % 2, :], ACT.Copy).then_inc(v_copied, 1)
                if b is not None:
                    for j in range(HT1):
                        n = hid_rows(j)
                        act.wait_ge(back_full, BACK * b + BACK_AG + 2 * j + 1)
                        if j >= 2:
                            act.wait_ge(gated, HT1 * b + j - 1)
                        act.activation(gel[0:n, j % 2, :], back[0:n, 0, :], ACT.Gelu, bias=b1[0:n, 1, j:j + 1]).then_inc(gelued, 1)
                if f is not None:
                    first = isinstance(f, int) and f == 0
                    for u in range(SLOTS + 3):
                        if u < SLOTS:
                            act.wait_ge(negged, SLOTS * f + u + 1)
                            if u >= PB or not first:
                                act.wait_ge(tp_full, SLOTS * f + max(u - PB + 1, 0))
                            if u >= 4 or not first:
                                act.wait_ge(inverted, SLOTS * f + u - 3)
                            for h in range(2):
                                last = act.activation(probs[:, u % PB, h, :], st[:, u % 2, h, :], ACT.Exp, scale=QK_SCALE,
                                                      bias=neg[:, u % 4, h:h + 1], accum_out=den[:, u % 4, h:h + 1])
                            last.then_inc(exped, 1)
                        if 2 <= u <= SLOTS + 1:
                            t = u - 2
                            act.wait_ge(tp_full, SLOTS * f + t + 1)
                            if t >= 2 or not first:
                                act.wait_ge(av_done, SLOTS * f + t - 1)
                            act.activation(probs_t[:, t % 2, :, :], tp[:, :, :], ACT.Copy).then_inc(pt_copied, 1)
                        if u >= 3 and (u - 3) % PAIRS == PAIRS - 1:
                            w = (u - 3) // PAIRS
                            act.wait_ge(av_done, SLOTS * f + u - 2)
                            act.activation(o[:, :, w * WIN:(w + 1) * WIN], ov[:, :, :], ACT.Copy).then_inc(o_copied, 1)
                    act.activation(kr[:, :, 0:WIN], kr[:, :, CH:KW], ACT.Copy).then_inc(kv_moved, 1)
                    act.activation(v[:, 0, :], v[:, WPC, :], ACT.Copy).then_inc(kv_moved, 1)

            act.wait_ge(w_in, 16 * NLOADS)
            iterations(act, body)

        @block.vector
        def _(dve):
            def sine(c, j):
                i = j // PAIRS
                dve.wait_ge(turned_in[j % 2], 64 * (UNITS // 2 * c + j // 2 + 1))
                dve.scalar_tensor_tensor(t_sin[:, j % 2, :], t_sin[:, j % 2, :], scales[:, i, 1:2],
                                         table[:, 2 * i + 1, :], ALU.mult, ALU.mult).then_inc(sin_done, 1)

            def body(f, b):
                if b is not None:
                    dve.wait_ge(back_full, BACK * b + 1)
                    for k in range(DT):
                        dve.tensor_tensor(hn[:, k, :], y_mid[:, k, toks(b, k)], back[:, 0, :], ALU.subtract).then_inc(centred, 1)
                if b is not None:
                    dve.wait_ge(std_done, b + 1)
                    dve.reciprocal(std[:, :], std[:, :]).then_inc(inv_std, 1)
                    dve.wait_ge(inv_std, b + 1)
                    dve.wait_ge(hsquared, b + 1)
                    for k in range(DT):
                        dve.scalar_tensor_tensor(hn[:, k, :], hn[:, k, :], ln_g[:, k:k + 1], std[:, :], ALU.mult, ALU.mult).then_inc(scaled, 1)
                    for k in range(DT):
                        dve.wait_ge(scaled, DT * b + k + 1)
                        dve.tensor_scalar(hn[:, k, :], hn[:, k, :], ln_b[:, k:k + 1], None, ALU.add).then_inc(affined, 1)
                if f is not None:
                    dve.wait_ge(norm_done, f + 1)
                    dve.tensor_scalar(norm, norm, 1e-12, None, ALU.max).then_inc(clipped, 1)
                    dve.wait_ge(clipped, f + 1)
                    dve.reciprocal(norm, norm).then_inc(rnormed, 1)
                    dve.wait_ge(rnormed, f + 1)
                    head = inv_parts[0:2 * UNITS, :]
                    dve.tensor_copy(head, norm).then_inc(inv_split, 1)
                    dve.wait_ge(inv_split, 2 * f + 1)
                    dve.tensor_tensor(inv_parts[INV_LOW:INV_ROWS, :], norm, head.bitcast(F32), ALU.subtract).then_inc(inv_split, 1)
                for j in range(UNITS):
                    if f is not None:
                        if j == 0:
                            dve.wait_ge(table_in, 16 * (f + 1))
                            if not (isinstance(f, int) and f == 0):
                                dve.wait_ge(kv_moved, 2 * f)
                            sine(f, 0)
                        if j + 1 < UNITS:
                            sine(f, j + 1)
                        dve.wait_ge(ring_full, RING * f + RING_INV + j + 1)
                        dve.wait_ge(rotated, UNITS * f + j + 1)
                        if j < PAIRS:
                            for h in range(2):
                                rows = slice(h * DH, (h + 1) * DH)
                                last = dve.tensor_tensor(qr[rows, j, h, :], t_cos[rows, j % 2, :], ring[rows, j % 2, :], ALU.mult)
                        else:
                            last = dve.tensor_tensor(kr[:, j - PAIRS, WIN:KW], t_cos[:, j % 2, :], ring[:, j % 2, :], ALU.mult)
                        last.then_inc(qk_done, 1)
                    if b is not None and j >= UNITS - HT1:
                        jj = j - (UNITS - HT1)
                        n = hid_rows(jj)
                        dve.wait_ge(gelued, HT1 * b + jj + 1)
                        dve.wait_ge(back_full, BACK * b + BACK_AG + 2 * jj + 2)
                        dve.scalar_tensor_tensor(hid[0:n, jj, :], back[0:n, 1, :], b1[0:n, 0, jj:jj + 1], gel[0:n, jj % 2, :],
                                                 ALU.add, ALU.mult).then_inc(gated, 1)

                def finish(m):
                    dve.wait_ge(back_full, BACK * b + BACK_Y + m + 1)
                    dve.scalar_tensor_tensor(y[:, m, toks(b, 0)], back[:, m, :], b2[:, m:m + 1], y_mid[:, m, toks(b, 0)],
                                             ALU.add, ALU.add).then_inc(y_done, 1)
                if f is not None:
                    for u in range(SLOTS + 1):
                        if u < SLOTS:
                            dve.wait_ge(st_full, SLOTS * f + u + 1)
                            dve.reduce_max(mx[:, u % 4, :], st[:, u % 2, :, :], AX.X).then_inc(maxed, 1)
                            dve.wait_ge(maxed, SLOTS * f + u + 1)
                            dve.tensor_scalar(neg[:, u % 4, :], mx[:, u % 4, :], -QK_SCALE, None, ALU.mult).then_inc(negged, 1)
                        if u >= 1:
                            t = u - 1
                            dve.wait_ge(exped, SLOTS * f + t + 1)
                            dve.reciprocal(rden[:, t % 4, :], den[:, t % 4, :]).then_inc(inverted, 1)
                            dve.wait_ge(inverted, SLOTS * f + t + 1)
                            dve.tensor_tensor(probs[:, t % PB, :, :], probs[:, t % PB, :, :],
                                              rden[:, t % 4, :].unsqueeze(2).broadcast_to([P, 2, 2 * WIN]), ALU.mult).then_inc(p_normed, 1)
                        if b is not None and u in (3, 6):
                            finish(u // 6)
                    for m in range(DT):
                        dve.wait_ge(ring_full, RING * f + RING_OUT + m + 1)
                        dve.tensor_tensor(y_mid[:, m, toks(f, 0)], ring[:, (RING_OUT + m) % 2, :], y[:, m, toks(f, 0)],
                                          ALU.add).then_inc(mid_done, 1)
                else:
                    for m in range(DT):
                        finish(m)

            dve.sem_inc(y_done, DT)
            for h in range(2):
                other = slice((1 - h) * DH, (2 - h) * DH)
                dve.memset(qr[other, :, h, :], 0.0)
            dve.memset(inv_parts[:, :].bitcast(F32), 0.0).then_inc(inv_zero, 1)
            dve.wait_ge(inv_zero, 1)
            dve.wait_ge(w_in, 16 * NLOADS)
            iterations(dve, body)

        @block.gpsimd
        def _(pool):
            def body(f, b):
                if f is None:
                    return
                first = isinstance(f, int) and f == 0
                for k in range(DT):
                    pool.tensor_copy(y_stage[:, k, :], y[:, k, toks(f, k)]).then_inc(staged, 1)
                pool.wait_ge(table_scaled, 2 * (f + 1))
                for j in range(UNITS):
                    i = j // PAIRS
                    pool.wait_ge(raw_copied, UNITS * f + j + 1)
                    if j >= 2 or not first:
                        pool.wait_ge(qk_done, UNITS * f + j - 1)
                    pool.tensor_tensor(t_cos[:, j % 2, :], raw[:, j, :], table[:, 2 * i, :], ALU.mult).then_inc(cos_done, 1)
                    pool.wait_ge(cos_done, UNITS * f + j + 1)
                    pool.wait_ge(sin_done, UNITS * f + j + 1)
                    pool.tensor_tensor(t_cos[:, j % 2, :], t_cos[:, j % 2, :], t_sin[:, j % 2, :], ALU.add).then_inc(rotated, 1)

            pool.memset(kr[:, :, 0:WIN], 0.0).then_inc(v_zero, 1)
            pool.memset(v[:, 0, :], 0.0).then_inc(v_zero, 1)
            pool.wait_ge(w_in, 16 * NLOADS)
            pool.wait_ge(v_zero, 2)
            iterations(pool, body)


def tables():
    t = np.arange(NQ, dtype=np.float32)
    half = np.arange(0, DH, 2, dtype=np.float32)
    freqs = t[:, None] * (np.float32(1.0) / np.float32(10000.0) ** (half / np.float32(DH)))[None, :]
    base = (half + np.float32(0.4 * DH)) / np.float32(1.4 * DH)
    power = (t - NQ // 2) / np.float32(WIN // 2)
    xpos = base[None, :] ** power[:, None]
    four = [np.cos(freqs) * xpos, np.sin(freqs) * xpos, np.cos(freqs) / xpos, np.sin(freqs) / xpos]
    rotary = np.stack([np.tile(m.T, (4, 1)) for m in four], axis=1).astype(np.float32)
    rotary[np.arange(P) % DH < HALF, 1::2] *= -1.0
    i, j = np.arange(WIN)[:, None], np.arange(2 * WIN)[None, :] - WIN
    band = np.where((i < j) | (i > j + WIN), NEG, 0.0).astype(np.float32)
    first = np.where((i < j) | (j < 0), NEG, 0.0).astype(np.float32)
    masks = np.stack([np.tile(band, (1, 2)), np.tile(first, (1, 2))], axis=1)
    p = np.arange(P)
    sel = np.zeros((P, UNITS, 2 * UNITS), np.float32)
    for u in range(UNITS):
        sel[p, u, 2 * u + p // DH] = 1.0
    sel_t = np.zeros((INV_ROWS, UNITS, P), np.float32)
    sel_t[0:2 * UNITS] = sel_t[INV_LOW:] = sel.transpose(2, 1, 0)
    return {"c_rotary": rotary, "c_masks": masks, "c_sel": sel, "c_sel_t": sel_t}


def constants_phase(nc, a, cst, y, y_mid):
    with Scope(nc, "cst") as s:
        masks = s.sb("masks", [P, 2, 4 * WIN])
        sel_t = s.sb("sel_t", [INV_ROWS, UNITS, P])
        loaded, masks_in, sel_in, zeroed = s.sem("loaded"), s.sem("masks_in"), s.sem("sel_in"), s.sem("zeroed")
        block = s.block()

        @block.sync
        def _(sp):
            sp.dma_start(masks[:, :, :], a["c_masks"]).then_inc(masks_in, 16)
            sp.dma_start(cst["sel"][:, :, :], a["c_sel"]).then_inc(loaded, 16)
            sp.dma_start(sel_t[:, :, :], a["c_sel_t"]).then_inc(sel_in, 16)
            sp.wait_ge(loaded, 16)

        @block.vector
        def _(dve):
            dve.wait_ge(sel_in, 16)
            dve.tensor_copy(cst["sel_t"][:, :, :], sel_t[:, :, :]).then_inc(zeroed, 1)

        @block.gpsimd
        def _(pool):
            pool.memset(y[:, :, 0:1], 0.0).then_inc(zeroed, 1)
            pool.memset(y_mid[:, :, 0:1], 0.0).then_inc(zeroed, 1)
            pool.wait_ge(masks_in, 16)
            pool.tensor_copy(cst["mask"][:, :], masks[:, 0, :]).then_inc(zeroed, 1)
            pool.tensor_copy(cst["mask_first"][:, :], masks[:, 1, :]).then_inc(zeroed, 1)
            pool.tensor_copy(cst["ident_b"][:, :], cst["ident"][:, :]).then_inc(zeroed, 1)


def gated_layers(nc, s, a, resid, ident, ones_mean, eps):
    y = s.sb("y", [P, DT, NQ + 1])
    y_mid = s.sb("y_mid", [P, DT, NQ + 1])
    cst = {"sel": s.sb("sel", [P, UNITS, 2 * UNITS]),
           "sel_t": s.sb("sel_t", [INV_ROWS, UNITS, P], F32R), "mask": s.sb("mask", [P, 4 * WIN], BF16),
           "mask_first": s.sb("mask_first", [P, 4 * WIN], BF16), "ident_b": s.sb("ident_b", [P, P], BF16),
           "ident": ident, "tables": a["c_rotary"]}
    constants_phase(nc, a, cst, y, y_mid)
    norm_phase(nc, "ln3", resid, y[:, :, 1:NQ + 1], ones_mean, eps)
    for l in range(2):
        layer_phase(nc, f"l{l}", a, l, y, y_mid, cst, ident, ones_mean, eps)
    return y[:, :, 1:NQ + 1]


def store_phase(nc, a, b, ident, out):
    TX = NQ // P
    with Scope(nc, "store") as s:
        y = s.sb("y", [P, DT, NQ])
        o = s.sb("o", [P, TX, D])
        tp = s.ps("tp", [P, 8, 2, DT, P])
        summed = s.sem("summed")
        turned = s.sem("turned")
        copied = s.sem("copied")
        stored = s.sem("stored")
        block = s.block()

        @block.gpsimd
        def _(pool):
            for c in range(NCH):
                part = slice(c * CH, (c + 1) * CH)
                if b is None:
                    pool.tensor_copy(y[:, :, part], a[:, :, part]).then_inc(summed, 1)
                else:
                    pool.tensor_tensor(y[:, :, part], a[:, :, part], b[:, :, part], ALU.add).then_inc(summed, 1)

        @block.tensor
        def _(pe):
            for n in range(TX // 2):
                pe.wait_ge(summed, n // 2 + 1)
                for j in range(2):
                    for k in range(DT):
                        t = 2 * n + j
                        last = pe.transpose(tp[:, n, j, k, :], y[:, k, t * P:(t + 1) * P], ident[:, :])
                last.then_inc(turned, 1)

        @block.vector
        def _(dve):
            for n in range(TX // 2):
                dve.wait_ge(turned, n + 1)
                dve.tensor_copy(o[:, 2 * n:2 * n + 2, :].rearrange("p j d -> p (j d)"),
                                tp[:, n, :, :, :].rearrange("p j k q -> p (j k q)")).then_inc(copied, 1)

        @block.sync
        def _(sp):
            ov = out.rearrange("b (t p) d -> p (b t) d", p=P)
            for n in range(4):
                sp.wait_ge(copied, 2 * (n + 1))
                sp.dma_start(ov[:, 4 * n:4 * n + 4, :], o[:, 4 * n:4 * n + 4, :]).then_inc(stored, 16)
            sp.wait_ge(stored, 64)


def transformer_kernel(nc, a, out, upto=99, skip_cross=False):
    with Scope(nc, "all") as s:
        ident = s.sb("ident", [P, P])
        ones_mean = s.sb("ones_mean", [P, P])
        ones64 = s.sb("ones64", [P, DH])
        eps = s.sb("eps", [P, 1])
        resid = s.sb("resid", [P, DT, NQ])
        v_dram = nc.dram_tensor("v_scratch", (NC_, INNER), F32, kind="Internal").ap()
        s_dram = nc.dram_tensor("sums_scratch", (HEADS, NQ), F32, kind="Internal").ap()
        r_dram = nc.dram_tensor("inverse_scratch", (HEADS, NQ), F32, kind="Internal").ap()
        o_dram = nc.dram_tensor("o_scratch", (INNER, NQ), F32, kind="Internal").ap()

        def cross(tag, ctx_t, wq, wk, wv, wo, bo):
            values_phase(nc, tag + "v", ctx_t, wv, v_dram)
            with Scope(nc, tag + "h") as s2:
                hn = s2.sb("hn", [P, DT, NQ])
                norm_phase(nc, tag + "n", resid, hn, ones_mean, eps)
                attention_phase(nc, tag, hn, ctx_t, wq, wk, v_dram, o_dram, s_dram, ident, ones64)
            output_phase(nc, tag + "o", o_dram, s_dram, r_dram, wo, bo, resid)

        def butterfly_ffn():
            with Scope(nc, "bf") as s2:
                w_up = s2.sb("w_up", [P, DT, HID0])
                w_down = s2.sb("w_down", [P, HT0, D])
                b_up = s2.sb("b_up", [P, HT0])
                b_out = s2.sb("b_out", [P, DT])
                butterfly_phase(nc, a["L0_ffn_W_exp"], a["L0_ffn_b_exp"], a["L0_ffn_up_weights"], a["L0_ffn_up_bias"],
                                a["L0_ffn_down_weights"], a["L0_ffn_W_con"], a["L0_ffn_b_con"], a["L0_ffn_down_bias"],
                                ident, w_up, b_up, w_down, b_out)
                with Scope(nc, "bfh") as s3:
                    hn = s3.sb("hn", [P, DT, NQ])
                    norm_phase(nc, "ln1", resid, hn, ones_mean, eps)
                    butterfly_ffn_phase(nc, hn, w_up, b_up, w_down, b_out, resid)

        with Scope(nc, "ctx") as s1:
            ctx_t = s1.sb("ctx_t", [P, 2, NC_ + 1])
            load_phase(nc, a["x"], a["ctx_768"], ident, ones_mean, ones64, eps, resid, ctx_t)
            if upto >= 1 and not skip_cross:
                cross("xa0", ctx_t, a["L0_xattn_Wq"], a["L0_xattn_Wk"], a["L0_xattn_Wv"], a["L0_xattn_Wo"], a["L0_xattn_bo"])
            if upto >= 2:
                butterfly_ffn()
            if upto >= 3 and not skip_cross:
                cross("xa1", ctx_t, a["L1_xattn_Wq"], a["L1_xattn_Wk"], a["L1_xattn_Wv"], a["L1_xattn_Wout"], a["L1_xattn_bout"])
        if upto >= 4:
            y = gated_layers(nc, s, a, resid, ident, ones_mean, eps)
            store_phase(nc, resid, y, ident, out)
        else:
            store_phase(nc, resid, None, ident, out)


_INS = ["x", "ctx_768", "L0_xattn_Wq", "L0_xattn_Wk", "L0_xattn_Wv", "L0_xattn_Wo", "L0_xattn_bo",
        "L0_ffn_W_exp", "L0_ffn_b_exp", "L0_ffn_up_weights", "L0_ffn_up_bias", "L0_ffn_down_weights",
        "L0_ffn_W_con", "L0_ffn_b_con", "L0_ffn_down_bias",
        "L1_xattn_Wq", "L1_xattn_Wk", "L1_xattn_Wv", "L1_xattn_Wout", "L1_xattn_bout",
        "L1_ffn_wqkv", "L1_ffn_q_scale", "L1_ffn_k_scale", "L1_ffn_wo", "L1_ffn_ln_g", "L1_ffn_ln_b",
        "L1_ffn_w1", "L1_ffn_b1", "L1_ffn_w2", "L1_ffn_b2"]
_CONSTS = ["c_rotary", "c_masks", "c_sel", "c_sel_t"]


def kernel(**inputs):
    import numpy as _np
    import concourse.bacc as _bacc
    from concourse import mybir as _mybir
    from concourse.bass_utils import run_bass_kernel_spmd as _run

    nc = _bacc.Bacc("TRN2", target_bir_lowering=False, num_devices=1)
    arrays, args = {}, {}
    given = {name: _np.ascontiguousarray(inputs[name]) for name in _INS}
    for name, value in {**given, **tables()}.items():
        arrays[f"in_{name}_dram"] = value
        args[name] = nc.dram_tensor(f"in_{name}_dram", value.shape, _mybir.dt.from_np(value.dtype), kind="ExternalInput").ap()
    out = nc.dram_tensor("out_dram", (1, NQ, D), _mybir.dt.float32, kind="ExternalOutput").ap()
    transformer_kernel(nc, args, out)
    return _run(nc, [arrays], core_ids=[0]).results[0]["out_dram"]
```

```python
import numpy as np
import concourse.bass as bass
from concourse import mybir
from contextlib import ExitStack

F32 = mybir.dt.float32
F32R = mybir.dt.float32r
BF16 = mybir.dt.bfloat16
ALU = mybir.AluOpType
ACT = mybir.ActivationFunctionType
AX = mybir.AxisListType

P = 128
NQ = 2048
D = 256
DT = D // P
NC_ = 1601
DC = 192
HEADS, DH = 8, 64
INNER = HEADS * DH
PAIRS = HEADS // 2
CH = 512
NCH = NQ // CH
KT = -(-NC_ // P)
LASTK = NC_ - (KT - 1) * P
EPS = 1e-5
HID0 = 4 * D
HT0 = HID0 // P
STAGES = 10
WITHIN = 7
HID1 = D * 4 * 2 // 3
HT1 = -(-HID1 // P)
LASTH = HID1 - (HT1 - 1) * P
WIN = 128
NEG = -1e30


def key_rows(t):
    return P if t < KT - 1 else LASTK


def hid_rows(j):
    return P if j < HT1 - 1 else LASTH


class Scope:

    def __init__(self, nc, tag):
        self.nc, self.tag, self.stack, self.sems = nc, tag, ExitStack(), []

    def __enter__(self):
        return self

    def __exit__(self, *a):
        self.stack.close()
        if self.sems:
            self.nc.clear_and_free_semaphores(self.sems)
            self.nc.all_engine_barrier()

    def sb(self, name, shape, dt=F32):
        return self.stack.enter_context(self.nc.sbuf_tensor(f"{self.tag}_{name}", shape, dt))

    def ps(self, name, shape, dt=F32):
        return self.stack.enter_context(self.nc.psum_tensor(f"{self.tag}_{name}", shape, dt))

    def sem(self, name):
        self.sems.append(self.nc.alloc_semaphore(f"{self.tag}_{name}"))
        return self.sems[-1]

    def block(self):
        return self.stack.enter_context(self.nc.Block())



class Norm:

    def __init__(self, s, src, dst, ones_mean, eps, banks, source_ready=None):
        self.src, self.dst, self.ones_mean, self.eps, self.banks = src, dst, ones_mean, eps, banks
        self.source_ready = source_ready
        self.sq = s.sb("sq", [P, 2, DT, CH])
        self.std = s.sb("std", [P, 2, CH])
        self.rstd = s.sb("rstd", [P, 2, CH])
        self.mean_ps = s.ps("mean", [P, banks, CH])
        self.var_ps = s.ps("var", [P, banks, CH])
        self.mean_done = s.sem("mean_done")
        self.centred = s.sem("centred")
        self.squared = s.sem("squared")
        self.var_done = s.sem("var_done")
        self.std_done = s.sem("std_done")
        self.rstd_done = s.sem("rstd_done")
        self.normed = s.sem("normed")

    def chunk(self, c):
        return slice(c * CH, (c + 1) * CH)

    def mean(self, pe, c):
        if self.source_ready:
            sem, count = self.source_ready
            pe.wait_ge(sem, count(c))
        if c >= self.banks:
            pe.wait_ge(self.centred, c - self.banks + 1)
        for k in range(DT):
            last = pe.matmul(self.mean_ps[:, c % self.banks, :], self.ones_mean[:, :], self.src[:, k, self.chunk(c)],
                             start=k == 0, stop=k == DT - 1)
        last.then_inc(self.mean_done, 1)

    def variance(self, pe, c):
        pe.wait_ge(self.squared, c + 1)
        if c >= self.banks:
            pe.wait_ge(self.std_done, c - self.banks + 1)
        for k in range(DT):
            last = pe.matmul(self.var_ps[:, c % self.banks, :], self.ones_mean[:, :], self.sq[:, c % 2, k, :],
                             start=k == 0, stop=k == DT - 1)
        last.then_inc(self.var_done, 1)

    def centre(self, dve, c):
        dve.wait_ge(self.mean_done, c + 1)
        b = c % self.banks
        dve.tensor_tensor(self.dst[:, :, self.chunk(c)], self.src[:, :, self.chunk(c)],
                          self.mean_ps[:, b:b + 1, :].broadcast_to([P, DT, CH]), ALU.subtract).then_inc(self.centred, 1)

    def square(self, act, c):
        act.wait_ge(self.centred, c + 1)
        if c >= 2:
            act.wait_ge(self.var_done, c - 1)
        act.activation(self.sq[:, c % 2, :, :], self.dst[:, :, self.chunk(c)], ACT.Square).then_inc(self.squared, 1)

    def root(self, act, c):
        act.wait_ge(self.var_done, c + 1)
        if c >= 2:
            act.wait_ge(self.rstd_done, c - 1)
        act.activation(self.std[:, c % 2, :], self.var_ps[:, c % self.banks, :], ACT.Sqrt,
                       bias=self.eps[:, 0:1]).then_inc(self.std_done, 1)

    def invert(self, dve, c):
        dve.wait_ge(self.std_done, c + 1)
        if c >= 2:
            dve.wait_ge(self.normed, c - 1)
        dve.reciprocal(self.rstd[:, c % 2, :], self.std[:, c % 2, :]).then_inc(self.rstd_done, 1)

    def scale_all(self, pool):
        for c in range(NCH):
            pool.wait_ge(self.rstd_done, c + 1)
            pool.wait_ge(self.squared, c + 1)
            part = self.dst[:, :, self.chunk(c)]
            pool.tensor_tensor(part, part, self.rstd[:, c % 2:c % 2 + 1, :].broadcast_to([P, DT, CH]),
                               ALU.mult).then_inc(self.normed, 1)


def norm_phase(nc, tag, src, dst, ones_mean, eps):
    with Scope(nc, tag) as s:
        norm = Norm(s, src, dst, ones_mean, eps, 2)
        block = s.block()

        @block.tensor
        def _(pe):
            norm.mean(pe, 0)
            for c in range(1, NCH):
                norm.mean(pe, c)
                norm.variance(pe, c - 1)
            norm.variance(pe, NCH - 1)

        @block.scalar
        def _(act):
            for c in range(NCH):
                norm.square(act, c)
                norm.root(act, c)

        @block.vector
        def _(dve):
            norm.centre(dve, 0)
            for c in range(1, NCH):
                norm.centre(dve, c)
                norm.invert(dve, c - 1)
            norm.invert(dve, NCH - 1)

        @block.gpsimd
        def _(pool):
            norm.scale_all(pool)



def load_phase(nc, x, ctx, ident, ones_mean, ones64, eps, resid, ctx_t, hn):
    xv = x.rearrange("b (t p) d -> p (b t) d", p=P)
    TX = NQ // P
    with Scope(nc, "load") as s:
        xin = s.sb("xin", [P, TX, D])
        cin = s.sb("cin", [P, KT, DC])
        tp = s.ps("tp", [P, 4, 4, P])
        consts = s.sem("consts")
        ident_zero = s.sem("ident_zero")
        x_in = [s.sem(f"x_in{i}") for i in range(4)]
        c_in = s.sem("c_in")
        turned = s.sem("turned")
        taken = s.sem("taken")
        groups = []
        for g in range(TX // 4):
            for k in range(DT):
                groups.append(("x", k, P, [(4 * g + j, P) for j in range(4)]))
        for g in range(-(-KT // 4)):
            for k, rows in ((0, P), (1, DC - P)):
                groups.append(("c", k, rows, [(t, key_rows(t)) for t in range(4 * g, min(4 * g + 4, KT))]))
        norm = Norm(s, resid, hn, ones_mean, eps, 2, (taken, lambda c: DT * (c + 1)))

        def due(n, lag):
            c, rest = divmod(n - lag, DT)
            return c if rest == 0 and 0 <= c < NCH else None
        block = s.block()

        @block.sync
        def _(sp):
            for i in range(4):
                sp.dma_start(xin[:, 4 * i:4 * i + 4, :], xv[:, 4 * i:4 * i + 4, :]).then_inc(x_in[i], 16)

        @block.gpsimd
        def _(pool):
            pool.memset(ident[:, :], 0.0).then_inc(ident_zero, 1)
            pool.memset(ones_mean[:, :], 1.0 / D).then_inc(consts, 1)
            pool.memset(ones64[:, :], 1.0).then_inc(consts, 1)
            pool.memset(eps[:, :], EPS).then_inc(consts, 1)
            pool.wait_ge(ident_zero, 1)
            pool.affine_select(out=ident[:, :], in_=ident[:, :], compare_op=ALU.not_equal, fill=1.0,
                               base=0, pattern=[[-1, P]], channel_multiplier=1).then_inc(consts, 1)
            norm.scale_all(pool)

        @block.tensor
        def _(pe):
            pe.wait_ge(consts, 4)
            for n, (src, k, rows, tiles) in enumerate(groups):
                if src == "x":
                    pe.wait_ge(x_in[tiles[0][0] // 4], 16)
                else:
                    pe.wait_ge(c_in, 32)
                if n >= 4:
                    pe.wait_ge(taken, n - 3)
                for j, (t, toks) in enumerate(tiles):
                    a = xin[:, t, k * P:k * P + rows] if src == "x" else cin[0:toks, t, k * P:k * P + rows]
                    last = pe.transpose(tp[0:rows, n % 4, j, 0:toks], a, ident[0:toks, 0:toks])
                last.then_inc(turned, 1)
                if due(n, 3) is not None:
                    norm.mean(pe, due(n, 3))
                if due(n, 5) is not None:
                    norm.variance(pe, due(n, 5))

        @block.scalar
        def _(act):
            act.dma_start(cin[:, 0:KT - 1, :], ctx[0, 0:(KT - 1) * P, :].rearrange("(t p) d -> p t d", p=P)).then_inc(c_in, 16)
            act.dma_start(cin[0:LASTK, KT - 1, :], ctx[0, (KT - 1) * P:NC_, :]).then_inc(c_in, 16)
            for c in range(NCH):
                norm.square(act, c)
                norm.root(act, c)

        @block.vector
        def _(dve):
            for n, (src, k, rows, tiles) in enumerate(groups):
                dve.wait_ge(turned, n + 1)
                t0, toks = tiles[0][0] * P, sum(m for _, m in tiles)
                dst = resid if src == "x" else ctx_t
                dve.tensor_copy(dst[0:rows, k, t0:t0 + toks],
                                tp[0:rows, n % 4, :, :].rearrange("p j q -> p (j q)")[:, 0:toks]).then_inc(taken, 1)
                if due(n, 3) is not None:
                    norm.centre(dve, due(n, 3))
                if due(n, 6) is not None:
                    norm.invert(dve, due(n, 6))



KCOLS = [(0, CH), (CH, CH), (2 * CH, CH), (3 * CH, NC_ - 3 * CH)]
MCOLS = [(0, CH), (CH, CH), (2 * CH, CH), (3 * CH - 1, NC_ - 3 * CH + 1)]
QT = NQ // P


SLOTS_PC = 3 * KT
DIVIDE_AT = (3, 5, 7, 9, 11)
LEAD = 6


def attention_order():
    chunks = PAIRS * NCH

    def project(g):
        if g >= chunks:
            return []
        p, c = divmod(g, NCH)
        return [("project", p, u, 0) for u in [4 + c] + ([0, 1, 2, 3] if c == 0 else [])]

    def maxima(g):
        if g >= chunks:
            return []
        p, c = divmod(g, NCH)
        return [("max", p, h * QT + qt, j) for h in range(2) for qt in range(4 * c, 4 * c + 4) for j in range(4)] \
            + [("shift", p, c, 0)]

    steps = NCH * KT

    def spread(few, many):
        out, left = [], list(few)
        for n, op in enumerate(many):
            while left and len(few) - len(left) <= n * len(few) / len(many):
                out.append(left.pop(0))
            out.append(op)
        return out + left

    def divide(g):
        return [("invert", g // NCH, g % NCH, i) for i in range(4)] + [("divide", g // NCH, g % NCH, 0)]

    context = [("context", 0, t, 0) for t in range(KT)]
    *first_max, first_shift = maxima(0)
    units = project(0)
    out = units[0:2] + context[0:2] + units[2:3] + context[2:4]
    for j, (more, made) in enumerate(((units[3:4], context[4:6]), (units[4:5], context[6:8]),
                                      (project(1), context[8:10]), ([], context[10:KT]))):
        out += spread(more + made, [op for op in first_max if op[3] == j])
    out.append(first_shift)
    for g in range(chunks):
        side = spread(project(g + 2), maxima(g + 1)) if g + 1 < chunks else []
        total, slot = len(side), 0

        def fill():
            while side and total - len(side) < (slot + 1) * total / (SLOTS_PC - LEAD):
                out.append(side.pop(0))
        for n in range(g * KT, (g + 1) * KT):
            for h in range(2):
                out.append(("scores", n // steps, n % steps, h))
                fill()
                slot += 1
            if n >= 2:
                out.append(("values", (n - 2) // steps, (n - 2) % steps, 0))
                if (n - 2) % KT == KT - 1:
                    out.append(("sums", (n - 2) // steps, (n - 2) % steps // KT, 0))
            if g and n - g * KT in DIVIDE_AT:
                out.append(divide(g - 1)[DIVIDE_AT.index(n - g * KT)])
            fill()
            slot += 1
    for n in range(PAIRS * steps - 2, PAIRS * steps):
        out.append(("values", n // steps, n % steps, 0))
    return out + [("sums", PAIRS - 1, NCH - 1, 0)] + divide(chunks - 1)


def attention_phase(nc, tag, hn, ctx_t, wq, wk, wv, v_dram, o_dram, ident, ones64):
    with Scope(nc, tag) as s:
        w = s.sb("w", [P, 2, 2, P])
        hi = s.sb("hi", [P, 2, CH], F32R)
        lo = s.sb("lo", [P, 2, CH], F32R)
        q_dup = [[s.sb(f"q_dup{b}{h}", [P, NQ], F32R) for h in range(2)] for b in range(2)]
        q_low = [[s.sb(f"q_low{b}{h}", [DH + 1, NQ], F32R) for h in range(2)] for b in range(2)]
        k_both = [[s.sb(f"k_both{b}{h}", [P, NC_ + 1], F32R) for h in range(2)] for b in range(2)]
        k_one = [[s.sb(f"k_one{b}{h}", [DH + 1, NC_ + 1], F32R) for h in range(2)] for b in range(2)]
        v = s.sb("v", [P, 2, KT, P])
        probs = s.sb("probs", [P, 3, 2, CH])
        psum_p = s.sb("psum_p", [P, 2, CH])
        o_sb = s.sb("o_sb", [P, CH])
        s_sb = s.sb("s_sb", [P, CH])
        mx = s.sb("mx", [P, 2, 8, 4])
        negmax = s.sb("negmax", [P, 8])
        negmax_t = s.sb("negmax_t", [8, P], F32R)
        st = s.ps("st", [P, 2, 2, CH])
        av = s.ps("av", [P, 2, CH])
        ring = s.ps("ring", [P, 2, CH])
        w_in = s.sem("w_in")
        v_in = [s.sem(f"v_in{i}") for i in range(2)]
        wv_in, v_made, v_copied, v_stored = s.sem("wv_in"), s.sem("v_made"), s.sem("v_copied"), s.sem("v_stored")
        hi_done = s.sem("hi_done")
        spread = [s.sem(f"spread{i}") for i in range(2)]
        ring_full = s.sem("ring_full")
        ring_read = s.sem("ring_read")
        neg_done = s.sem("neg_done")
        shift_in = s.sem("shift_in")
        scored = s.sem("scored")
        exped = s.sem("exped")
        weighed = s.sem("weighed")
        summed = s.sem("summed")
        outed = s.sem("outed")
        o_stored = s.sem("o_stored")
        inverted = s.sem("inverted")
        ones_set = s.sem("ones_set")
        wv_sb = psum_p
        v_bank = lambda t: st[:, (t // 2) % 2, t % 2, :]
        v_late = probs[:, :, :, :].rearrange("p a h q -> p (a h q)")
        LATE = INNER // 2
        block = s.block()

        def late_v(t):
            return (v_late[:, t * LATE:(t + 1) * LATE] if t < KT - 1 else o_sb[:, 0:LATE])[0:key_rows(t)]

        order = attention_order()
        STEPS = NCH * KT
        RINGED = ("project", "max", "shift", "sums")
        ring_at = {op: n for n, op in enumerate(op for op in order if op[0] in RINGED)}

        def step(p, i):
            return p * STEPS + i, i // KT, i % KT

        def adds_through(p, i):
            return (p * NCH + i // KT) * (KT - 1) + max(i % KT, 1)

        def ring_of(kind, g):
            return ring_at[(kind, g // NCH, g % NCH, 0)]

        unit_at = {op: n for n, op in enumerate(op for op in order if op[0] == "project")}

        def units_for(p, c, j):
            return max(unit_at[("project", p, u, 0)] for u in [4 + c] + list(range(j + 1)))

        def spread_through(n, i):
            return 96 * ((n - i) // 2 + 1)

        @block.sync
        def _(sp):
            for op in order:
                kind, p, u, _ = op
                r = ring_at.get(op)
                if kind == "context" and u == KT - 1:
                    full = (KT - 1) * P
                    sp.wait_ge(v_copied, 2 * KT)
                    sp.dma_start(v_dram[0:full, :].rearrange("(t p) d -> p t d", p=P),
                                 v_late.rearrange("p (t d) -> p t d", d=LATE)).then_inc(v_stored, 16)
                    sp.dma_start(v_dram[full:NC_, :], late_v(KT - 1)).then_inc(v_stored, 16)
                if kind == "shift":
                    sp.wait_ge(ring_read, r + 1)
                    for h in range(2):
                        sp.dma_start(q_low[p % 2][h][DH:DH + 1, u * CH:(u + 1) * CH].bitcast(F32).rearrange("a (t q) -> a t q", q=P),
                                     negmax_t[4 * h:4 * h + 4, :].bitcast(F32)).then_inc(shift_in, 16)
                if kind == "divide":
                    sp.wait_ge(outed, p * NCH + u + 1)
                    sp.dma_start(o_dram[p * P:(p + 1) * P, u * CH:(u + 1) * CH], o_sb[:, :]).then_inc(o_stored, 16)
                if kind == "project":
                    b, n = p % 2, unit_at[op]
                    if u == 4:
                        if p:
                            sp.wait_ge(ring_full, ring_at[("project", p - 1, 7, 0)] + 1)
                        cols = slice(p * P, (p + 1) * P)
                        sp.dma_start(w[:, 0, 0, :], wk[0:P, cols]).then_inc(w_in, 16)
                        sp.dma_start(w[0:DC - P, 1, 0, :], wk[P:DC, cols]).then_inc(w_in, 16)
                        sp.dma_start(w[:, :, 1, :], wq[:, cols].rearrange("(k p) d -> p k d", p=P)).then_inc(w_in, 16)
                        if p >= 2:
                            sp.wait_ge(weighed, STEPS * (p - 1))
                            sp.wait_ge(v_stored, 32)
                            full, late = (KT - 1) * P, slice((p - 2) * P, (p - 1) * P)
                            sp.dma_start(v[:, b, 0:KT - 1, :], v_dram[0:full, late].rearrange("(t p) d -> p t d", p=P)).then_inc(v_in[b], 16)
                            sp.dma_start(v[0:LASTK, b, KT - 1, :], v_dram[full:NC_, late]).then_inc(v_in[b], 16)
                    sp.wait_ge(ring_read, r + 1)
                    c0, m = KCOLS[u] if u < 4 else ((u - 4) * CH, CH)
                    for h in range(2):
                        h_hi, h_lo = hi[h * DH:(h + 1) * DH, n % 2, 0:m], lo[h * DH:(h + 1) * DH, n % 2, 0:m]
                        if u < 4:
                            to = ((k_both[b][h][0:DH], h_hi), (k_both[b][h][DH:P], h_lo), (k_one[b][h][0:DH], h_hi))
                        else:
                            to = ((q_dup[b][h][0:DH], h_hi), (q_dup[b][h][DH:P], h_hi), (q_low[b][h][0:DH], h_lo))
                        for dst, src in to:
                            sp.dma_start(dst[:, c0:c0 + m].bitcast(F32), src.bitcast(F32)).then_inc(spread[n % 2], 16)
            sp.wait_ge(o_stored, 16 * PAIRS * NCH)

        @block.gpsimd
        def _(pool):
            for b in range(2):
                for h in range(2):
                    pool.memset(k_one[b][h][DH:DH + 1, :].bitcast(F32), 1.0).then_inc(ones_set, 1)
            for kind, p, u, h in order:
                if kind == "scores" and h == 1:
                    n, c, t = step(p, u)
                    if t == 0:
                        continue
                    rows = key_rows(t)
                    pool.wait_ge(exped, n + 1)
                    if t == 1:
                        if p or c:
                            pool.wait_ge(ring_full, ring_of("sums", p * NCH + c - 1) + 1)
                        a = probs[:, (n - 1) % 3, :, :]
                    else:
                        pool.wait_ge(summed, adds_through(p, u) - 1)
                        a = psum_p[0:rows, :, :]
                    pool.tensor_tensor(psum_p[0:rows, :, :], probs[0:rows, n % 3, :, :], a[0:rows], ALU.add).then_inc(summed, 1)

        @block.scalar
        def _(act):
            act.dma_start(wv_sb[:, 0, :], wv[0:P, :]).then_inc(wv_in, 16)
            act.dma_start(wv_sb[0:DC - P, 1, :], wv[P:DC, :]).then_inc(wv_in, 16)
            for kind, p, u, h in order:
                if kind == "context":
                    rows = key_rows(u)
                    act.wait_ge(v_made, u + 1)
                    act.activation(v[0:rows, :, u, :], v_bank(u)[0:rows, 0:LATE].rearrange("p (b d) -> p b d", b=2), ACT.Copy).then_inc(v_copied, 1)
                    act.activation(late_v(u), v_bank(u)[0:rows, LATE:INNER], ACT.Copy).then_inc(v_copied, 1)
                if kind == "scores" and h == 1:
                    n, c, t = step(p, u)
                    rows = key_rows(t)
                    act.wait_ge(scored, n + 1)
                    if n == 0:
                        act.wait_ge(v_stored, 32)
                    if n >= 3:
                        act.wait_ge(weighed, n - 2)
                        act.wait_ge(summed, adds_through(*divmod(n - 3, STEPS)))
                    act.activation(probs[0:rows, n % 3, :, :], st[0:rows, n % 2, :, :], ACT.Exp,
                                   scale=DH ** -0.5).then_inc(exped, 1)

        @block.vector
        def _(dve):
            for op in order:
                kind, p, u, t = op
                b, r = p % 2, ring_at.get(op)
                if kind == "project":
                    n, m = unit_at[op], KCOLS[u][1] if u < 4 else CH
                    dve.wait_ge(ring_full, r + 1)
                    if n >= 2:
                        dve.wait_ge(spread[n % 2], 96 * (n // 2))
                    dve.tensor_copy(hi[:, n % 2, 0:m], ring[:, r % 2, 0:m]).then_inc(hi_done, 1)
                    dve.wait_ge(hi_done, n + 1)
                    dve.tensor_tensor(lo[:, n % 2, 0:m], ring[:, r % 2, 0:m], hi[:, n % 2, 0:m].bitcast(F32),
                                      ALU.subtract).then_inc(ring_read, 1)
                if kind == "max":
                    h, qt = divmod(u, QT)
                    g = p * NCH + qt // 4
                    if h == 0 and qt % 4 == 0 and t == 0 and g >= 2:
                        dve.wait_ge(neg_done, 2 * (g - 1))
                    dve.wait_ge(ring_full, r + 1)
                    dve.reduce_max(mx[:, g % 2, 4 * h + qt % 4, t:t + 1], ring[:, r % 2, 0:MCOLS[t][1]], AX.X).then_inc(ring_read, 1)
                if kind == "shift":
                    g = p * NCH + u
                    dve.wait_ge(ring_read, r)
                    if g:
                        dve.wait_ge(ring_full, ring_of("shift", g - 1) + 1)
                    dve.reduce_max(negmax[:, :], mx[:, g % 2, :, :], AX.X).then_inc(neg_done, 1)
                    dve.wait_ge(neg_done, 2 * g + 1)
                    dve.tensor_scalar(negmax[:, :], negmax[:, :], -1.0, None, ALU.mult).then_inc(neg_done, 1)
                    dve.wait_ge(ring_full, r + 1)
                    if g:
                        dve.wait_ge(shift_in, 32 * g)
                    dve.tensor_copy(negmax_t[:, :], ring[0:8, r % 2, 0:P]).then_inc(ring_read, 1)
                if kind == "sums":
                    g = p * NCH + u
                    dve.wait_ge(ring_full, r + 1)
                    if g:
                        dve.wait_ge(outed, g)
                    dve.tensor_copy(s_sb[:, :], ring[:, r % 2, :]).then_inc(ring_read, 1)
                if kind == "invert":
                    dve.wait_ge(ring_read, ring_of("sums", p * NCH + u) + 1)
                    part = s_sb[:, t * P:(t + 1) * P]
                    dve.reciprocal(part, part).then_inc(inverted, 1)
                if kind == "divide":
                    g = p * NCH + u
                    dve.wait_ge(inverted, 4 * (g + 1))
                    dve.wait_ge(weighed, (g + 1) * KT)
                    if g:
                        dve.wait_ge(o_stored, 16 * g)
                    dve.tensor_tensor(o_sb[:, :], av[:, g % 2, :], s_sb[:, :], ALU.mult).then_inc(outed, 1)

        @block.tensor
        def _(pe):
            pe.wait_ge(ones_set, 4)
            in_place = -1
            for op in order:
                kind, p, u, t = op
                b, r = p % 2, ring_at.get(op)
                if r is not None and r >= 2:
                    pe.wait_ge(ring_read, r - 1)
                if kind == "context":
                    rows = key_rows(u)
                    if u == 0:
                        pe.wait_ge(wv_in, 32)
                    if u >= 4:
                        pe.wait_ge(v_copied, 2 * (u - 3))
                    pe.matmul(v_bank(u)[0:rows], ctx_t[:, 0, u * P:u * P + rows], wv_sb[:, 0, :], start=True, stop=False)
                    pe.matmul(v_bank(u)[0:rows], ctx_t[0:DC - P, 1, u * P:u * P + rows], wv_sb[0:DC - P, 1, :],
                              start=False, stop=True).then_inc(v_made, 1)
                if kind == "project":
                    if u == 4:
                        pe.wait_ge(w_in, 48 * (p + 1))
                    if u < 4:
                        c0, m = KCOLS[u]
                        pe.matmul(ring[:, r % 2, 0:m], w[:, 0, 0, :], ctx_t[:, 0, c0:c0 + m], start=True, stop=False)
                        last = pe.matmul(ring[:, r % 2, 0:m], w[0:DC - P, 1, 0, :], ctx_t[0:DC - P, 1, c0:c0 + m],
                                         start=False, stop=True)
                    else:
                        c0 = (u - 4) * CH
                        for k in range(DT):
                            last = pe.matmul(ring[:, r % 2, :], w[:, k, 1, :], hn[:, k, c0:c0 + CH],
                                             start=k == 0, stop=k == DT - 1)
                    last.then_inc(ring_full, 1)
                if kind == "max":
                    h, qt = divmod(u, QT)
                    if units_for(p, qt // 4, t) > in_place:
                        in_place = units_for(p, qt // 4, t)
                        for i in range(2):
                            pe.wait_ge(spread[i], spread_through(in_place, i))
                    c0, m = MCOLS[t]
                    pe.matmul(ring[:, r % 2, 0:m], q_dup[b][h][:, qt * P:(qt + 1) * P],
                              k_both[b][h][:, c0:c0 + m], start=True, stop=True).then_inc(ring_full, 1)
                if kind == "shift":
                    pe.wait_ge(neg_done, 2 * (p * NCH + u + 1))
                    pe.transpose(ring[0:8, r % 2, 0:P], negmax[:, :], ident[:, :]).then_inc(ring_full, 1)
                if kind == "scores":
                    n, c, kt = step(p, u)
                    h = t
                    rows, keys, qs = key_rows(kt), slice(kt * P, kt * P + key_rows(kt)), slice(c * CH, (c + 1) * CH)
                    if n == 0 and h == 0:
                        pe.wait_ge(v_copied, 2 * KT)
                    if kt == 0 and h == 0:
                        pe.wait_ge(shift_in, 32 * (p * NCH + c + 1))
                    if n >= 2 and h == 0:
                        pe.wait_ge(exped, n - 1)
                    pe.matmul(st[0:rows, n % 2, h, :], k_both[b][h][:, keys], q_dup[b][h][:, qs], start=True, stop=False)
                    last = pe.matmul(st[0:rows, n % 2, h, :], k_one[b][h][:, keys], q_low[b][h][:, qs],
                                     start=False, stop=True)
                    if h == 1:
                        last.then_inc(scored, 1)
                if kind == "values":
                    n, c, kt = step(p, u)
                    rows, m = key_rows(kt), p * NCH + c
                    if u == 0 and p >= 2:
                        pe.wait_ge(v_in[b], 32)
                    pe.wait_ge(exped, n + 1)
                    if kt == 0 and m >= 2:
                        pe.wait_ge(outed, m - 1)
                    for h in range(2):
                        last = pe.matmul(av[h * DH:(h + 1) * DH, m % 2, :], v[0:rows, b, kt, h * DH:(h + 1) * DH],
                                         probs[0:rows, n % 3, h, :], start=kt == 0, stop=kt == KT - 1)
                    last.then_inc(weighed, 1)
                if kind == "sums":
                    pe.wait_ge(summed, (p * NCH + u + 1) * (KT - 1))
                    for h in range(2):
                        last = pe.matmul(ring[h * DH:(h + 1) * DH, r % 2, :], ones64[:, :], psum_p[:, h, :],
                                         start=True, stop=True)
                    last.then_inc(ring_full, 1)


class Output:

    def __init__(self, s, o_dram, wo, bo, resid, banks):
        self.o_dram, self.wo, self.bo, self.resid, self.banks = o_dram, wo, bo, resid, banks
        self.w = s.sb("o_w", [P, PAIRS, D])
        self.bias = s.sb("o_bias", [P, DT])
        self.o = s.sb("o", [P, PAIRS, NQ])
        self.ps = s.ps("o_ps", [P, banks, CH])
        self.w_in = s.sem("o_w_in")
        self.bias_in = s.sem("o_bias_in")
        self.o_in = [s.sem(f"o_in{c}") for c in range(NCH)]
        self.made = s.sem("o_made")
        self.added = s.sem("o_added")

    def load_chunk(self, sp, c):
        if c == 0:
            sp.dma_start(self.w[:, :, :], self.wo.rearrange("(k p) d -> p k d", p=P)).then_inc(self.w_in, 16)
        sp.dma_start(self.o[:, :, c * CH:(c + 1) * CH],
                     self.o_dram[:, c * CH:(c + 1) * CH].rearrange("(k p) q -> p k q", p=P)).then_inc(self.o_in[c], 16)
        if c == 0:
            sp.dma_start(self.bias[:, :], self.bo.rearrange("(k p) -> p k", p=P), allow_slow_non_contiguous=True).then_inc(self.bias_in, 16)

    def product(self, pe, i):
        n, k = divmod(i, PAIRS)
        c, m = divmod(n, DT)
        if i == 0:
            pe.wait_ge(self.w_in, 16)
        if k == 0 and m == 0:
            pe.wait_ge(self.o_in[c], 16)
        if k == 0 and n >= self.banks:
            pe.wait_ge(self.added, n - self.banks + 1)
        last = pe.matmul(self.ps[:, n % self.banks, :], self.w[:, k, m * P:(m + 1) * P], self.o[:, k, c * CH:(c + 1) * CH],
                         start=k == 0, stop=k == PAIRS - 1)
        if k == PAIRS - 1:
            last.then_inc(self.made, 1)

    def add(self, dve, n):
        c, m = divmod(n, DT)
        if n == 0:
            dve.wait_ge(self.bias_in, 16)
        dve.wait_ge(self.made, n + 1)
        part = self.resid[:, m, c * CH:(c + 1) * CH]
        dve.scalar_tensor_tensor(part, self.ps[:, n % self.banks, :], self.bias[:, m:m + 1], part,
                                 ALU.add, ALU.add).then_inc(self.added, 1)


def output_phase(nc, tag, o_dram, wo, bo, resid, dst, ones_mean, eps, for_layers):
    with Scope(nc, tag) as s:
        constants = Constants(s, *for_layers)
        out = Output(s, o_dram, wo, bo, resid, 4)
        norm = Norm(s, resid, dst, ones_mean, eps, 2, (out.added, lambda c: DT * (c + 1)))
        block = s.block()

        @block.sync
        def _(sp):
            for c in range(NCH):
                out.load_chunk(sp, c)
            constants.load(sp)

        @block.tensor
        def _(pe):
            per_chunk = DT * PAIRS
            for c in range(NCH + 1):
                for i in range(per_chunk):
                    if c < NCH:
                        out.product(pe, c * per_chunk + i)
                    if c and i == PAIRS:
                        norm.mean(pe, c - 1)
                if c:
                    norm.variance(pe, c - 1)

        @block.scalar
        def _(act):
            for c in range(NCH):
                norm.square(act, c)
                norm.root(act, c)

        @block.vector
        def _(dve):
            for c in range(NCH + 1):
                for m in range(DT):
                    if c < NCH:
                        out.add(dve, DT * c + m)
                    if m == 0 and c:
                        norm.centre(dve, c - 1)
                if c:
                    norm.invert(dve, c - 1)
            constants.convert_sel(dve)

        @block.gpsimd
        def _(pool):
            constants.convert_masks(pool)
            norm.scale_all(pool)



def fold_items():
    across = range(WITHIN, STAGES)
    items = [("across", 1, st, t) for st in reversed(across) for t in range(HT0)]
    for i in range(WITHIN):
        items += [("within", d, st, t) for d, st in ((1, WITHIN - 1 - i), (0, i)) for t in range(HT0)]
    return items + [("across", 0, st, t) for st in across for t in range(HT0)]


def butterfly_phase(nc, a, ident, w_up, b_up, w_down, b_out, *attended):
    up_w, down_w = a["L0_ffn_up_weights"], a["L0_ffn_down_weights"]
    WD = D + 1
    ROWS = WITHIN * HT0
    with Scope(nc, "fold") as s:
        exp = s.sb("exp", [P, DT, HID0])
        x = [[s.sb(f"x{d}{i}", [P, HT0, WD if d == 0 else D]) for i in range(2)] for d in range(2)]
        perm = s.sb("perm", [P, WITHIN, P])
        pick = s.sb("pick", [P, WITHIN, P])
        rows = s.sb("rows", [ROWS, 2, P // 2, 4])
        sorted_w = s.sb("sorted", [ROWS, 4, 2, P // 2])
        sides = s.sb("sides", [P, WITHIN, 4, HT0])
        factor = s.sb("factor", [P, WITHIN, 4, HT0])
        big = s.sb("big", [P, 2, (STAGES - WITHIN) * 4, 4])
        tmp = s.sb("tmp", [P, 4, WD])
        biases = s.sb("biases", [P, DT, 2])
        upb = s.sb("upb", [P, HT0])
        ring = s.ps("ring", [P, 4, CH])
        turned_w = s.ps("turned_w", [P, 4, ROWS])
        picked = s.ps("picked", [P, WITHIN, 4, HT0])
        con_in, big_in, exp_in, rows_in, const_in, bias_in = [s.sem(n) for n in ("con_in", "big_in", "exp_in", "rows_in", "const_in", "bias_in")]
        ring_full, ring_read, kept, combined = s.sem("ring_full"), s.sem("ring_read"), s.sem("kept"), s.sem("combined")
        sorted_done, turned_done, sides_done, picked_done, factor_done = [
            s.sem(n) for n in ("sorted_done", "turned_done", "sides_done", "picked_done", "factor_done")]
        out_done = s.sem("out_done")
        out = Output(s, *attended, 2)
        block = s.block()

        items = fold_items()
        number = {item: n for n, item in enumerate(items)}
        within = [item for item in items if item[0] == "within"]
        FIRST = items.index(within[0])
        IN = 4
        PIECES = NCH * DT * PAIRS
        LATER = 8
        AHEAD = 16

        def pieces_after(n):
            return AHEAD + (n + 1) * (PIECES - AHEAD - LATER) // len(within)

        def done_before(item):
            kind, d, st, t = item
            prev = st - 1 if d == 0 else st + 1
            if not 0 <= prev < STAGES:
                return 0
            return number[("within" if prev < WITHIN else "across", d, prev, t)] + 1

        def source(item):
            kind, d, st, t = item
            if kind == "within":
                return x[d][1], (w_down if d == 1 and st == 0 else x[d][1])
            i = (st - WITHIN) % 2
            return (x[0][1 - i], x[0][i]) if d == 0 else (x[1][i], x[1][1 - i])

        def factors(item):
            kind, d, st, t = item
            if kind == "within":
                return [factor[:, st, 2 * d + i, t:t + 1] for i in range(2)]
            b = st - WITHIN
            side, pair = (t >> b) & 1, ((t >> (b + 1)) << b) + t % (1 << b)
            own, other = (side, side), ((side, 1 - side) if d == 0 else (1 - side, side))
            return [big[:, d, 4 * b + pair, 2 * i + j:2 * i + j + 1] for i, j in (own, other)]

        @block.sync
        def _(sp):
            slow = dict(allow_slow_non_contiguous=True)
            out.load_chunk(sp, 0)
            for d, w in enumerate((up_w, down_w)):
                sp.dma_start(rows[:, d, :, :], w[0:WITHIN].rearrange("s (t k) i j -> (s t) k (i j)", t=HT0)).then_inc(rows_in, 16)
            sp.dma_start(x[1][0][:, :, :], a["L0_ffn_W_con"].rearrange("(t p) d -> p t d", p=P)).then_inc(con_in, 16)
            for d, w in ((1, down_w), (0, up_w)):
                sp.dma_start(big[:, d, :, :], w[WITHIN:].rearrange("s (k p) i j -> (s k) p (i j)", p=P).rearrange("n p e -> p n e"),
                             **slow).then_inc(big_in, 16)
            sp.dma_start(exp[:, :, :], a["L0_ffn_W_exp"].rearrange("(k p) h -> p k h", p=P)).then_inc(exp_in, 16)
            sp.dma_start(pick[:, :, :], a["c_pick"]).then_inc(const_in, 16)
            out.load_chunk(sp, 1)
            sp.dma_start(perm[:, :, :], a["c_perm"]).then_inc(const_in, 16)
            sp.dma_start(x[0][1][:, :, D:WD], a["L0_ffn_b_exp"].rearrange("(t p a) -> p t a", p=P, a=1), **slow).then_inc(bias_in, 16)
            sp.dma_start(upb[:, :], a["L0_ffn_up_bias"].rearrange("(t p) -> p t", p=P), **slow).then_inc(bias_in, 16)
            for i, n in enumerate(("L0_ffn_b_con", "L0_ffn_down_bias")):
                sp.dma_start(biases[:, :, i], a[n].rearrange("(t p) -> p t", p=P), **slow).then_inc(bias_in, 16)
            for c in range(2, NCH):
                out.load_chunk(sp, c)

        @block.tensor
        def _(pe):
            for i in range(AHEAD // 2):
                out.product(pe, i)
            pe.wait_ge(exp_in, 16)
            for n in range(IN):
                for j in range(4):
                    t, k = 2 * n + j // 2, j % 2
                    last = pe.transpose(ring[:, n, j * P:(j + 1) * P], exp[:, k, t * P:(t + 1) * P], ident[:, :])
                last.then_inc(ring_full, 1)
            pe.wait_ge(sorted_done, 6)
            for i in range(4):
                last = pe.transpose(turned_w[:, i, :], sorted_w[:, i, :, :].rearrange("r s k -> r (s k)"), ident[0:ROWS, 0:ROWS])
            last.then_inc(turned_done, 1)
            pe.wait_ge(const_in, 32)
            pe.wait_ge(sides_done, 4)
            for st in range(WITHIN):
                last = pe.matmul(picked[:, st, :, :].rearrange("p i t -> p (i t)"), pick[:, st, :],
                                 sides[:, st, :, :].rearrange("p i t -> p (i t)"), start=True, stop=True)
            last.then_inc(picked_done, 1)
            for i in range(AHEAD // 2, AHEAD):
                out.product(pe, i)
            done = AHEAD
            for n, item in enumerate(within):
                _, d, st, t = item
                r = IN + n
                if n < 4:
                    pe.wait_ge(ring_read, n + 1)
                else:
                    pe.wait_ge(combined, FIRST + n - 3)
                if done_before(item):
                    pe.wait_ge(combined, done_before(item))
                else:
                    pe.wait_ge(ring_read, IN)
                    pe.wait_ge(bias_in, 64)
                src, _ = source(item)
                wd = WD if d == 0 else D
                pe.matmul(ring[:, r % 4, 0:wd], perm[:, st, :], src[:, t, :], start=True, stop=True).then_inc(ring_full, 1)
                for i in range(done, pieces_after(n)):
                    out.product(pe, i)
                done = pieces_after(n)
            for i in range(done, PIECES):
                out.product(pe, i)
            for n in range(IN):
                k, half = divmod(n, 2)
                pe.wait_ge(combined, len(items) if half else len(items) - 4)
                for j in range(4):
                    t = 4 * half + j
                    last = pe.transpose(ring[:, n, j * P:(j + 1) * P], x[0][0][:, t, k * P:(k + 1) * P], ident[:, :])
                last.then_inc(out_done, 1)

        @block.scalar
        def _(act):
            for m, item in enumerate(items):
                kind, d, st, t = item
                if m >= 4:
                    act.wait_ge(combined, m - 3)
                if m == 0:
                    act.wait_ge(con_in, 16)
                    act.wait_ge(big_in, 32)
                if kind == "within" and m == FIRST:
                    act.wait_ge(factor_done, 1)
                if done_before(item):
                    act.wait_ge(combined, done_before(item))
                elif d == 0:
                    act.wait_ge(ring_read, IN)
                    act.wait_ge(bias_in, 64)
                src, _ = source(item)
                wd = WD if d == 0 else D
                act.activation(tmp[:, m % 4, 0:wd], src[:, t, :], ACT.Copy, scale=factors(item)[0]).then_inc(kept, 1)

        @block.vector
        def _(dve):
            def combine(m, item):
                kind, d, st, t = item
                src, dst = source(item)
                wd = WD if d == 0 else D
                dve.wait_ge(kept, m + 1)
                if kind == "within":
                    n = m - FIRST
                    dve.wait_ge(ring_full, IN + n + 1)
                    partner = ring[:, (IN + n) % 4, 0:wd]
                else:
                    if m == 0:
                        dve.wait_ge(con_in, 16)
                        dve.wait_ge(big_in, 32)
                    last_stage = ("across" if d or st > WITHIN else "within", d, st + (1 if d else -1), HT0 - 1)
                    if last_stage in number:
                        dve.wait_ge(combined, number[last_stage] + 1)
                    partner = src[:, t ^ (1 << (st - WITHIN)), :]
                dve.scalar_tensor_tensor(dst[:, t, :], partner, factors(item)[1], tmp[:, m % 4, 0:wd],
                                         ALU.mult, ALU.add).then_inc(combined, 1)

            def sort_weights():
                dve.wait_ge(rows_in, 32)
                for d in range(2):
                    v = rows[:, d, :, :].rearrange("r k e -> r e k")
                    own, other = sorted_w[:, 2 * d, :, :], sorted_w[:, 2 * d + 1, :, :]
                    dve.tensor_copy(own, v[:, 0:4:3, :]).then_inc(sorted_done, 1)
                    for side in range(2):
                        e = 1 + (side ^ d)
                        dve.tensor_copy(other[:, side, :], v[:, e, :]).then_inc(sorted_done, 1)

            sort_weights()
            for n in range(AHEAD // 2 // PAIRS):
                out.add(dve, n)
            for m, item in enumerate(items):
                if m == 8:
                    for n in range(IN):
                        dve.wait_ge(ring_full, n + 1)
                        dve.tensor_copy(x[0][1][:, 2 * n:2 * n + 2, 0:D], ring[:, n, :].rearrange("p (t d) -> p t d", t=2)).then_inc(ring_read, 1)
                if m == 12:
                    dve.wait_ge(turned_done, 1)
                    for i in range(4):
                        dve.tensor_copy(sides[:, :, i, :], turned_w[:, i, :].rearrange("p (s t) -> p s t", t=HT0)).then_inc(sides_done, 1)
                if m == 20:
                    dve.wait_ge(picked_done, 1)
                    dve.tensor_copy(factor[:, :, :, :], picked[:, :, :, :]).then_inc(factor_done, 1)
                if m == FIRST:
                    for n in range(2, AHEAD // PAIRS):
                        out.add(dve, n)
                    dve.wait_ge(factor_done, 1)
                combine(m, item)
                if m >= FIRST + 2:
                    before = pieces_after(min(m - FIRST - 3, len(within) - 1)) // PAIRS
                    now = pieces_after(min(m - FIRST - 2, len(within) - 1)) // PAIRS
                    if m == len(items) - 1:
                        now = NCH * DT
                    for n in range(before, now):
                        out.add(dve, n)
            dve.wait_ge(combined, len(items))
            dve.tensor_tensor(b_up[:, :], x[0][0][:, :, D], upb[:, :], ALU.add)
            dve.tensor_tensor(b_out[:, :], biases[:, :, 0], biases[:, :, 1], ALU.add)
            for n in range(IN):
                k, half = divmod(n, 2)
                dve.wait_ge(out_done, n + 1)
                dve.tensor_copy(w_up[:, k, half * CH:(half + 1) * CH], ring[:, n, :])


def butterfly_ffn_phase(nc, hn, w_up, b_up, w_down, b_out, resid, ones_mean, eps):
    STAGED = 4
    with Scope(nc, "ffn0") as s:
        parts = lambda name, shape: [s.sb(f"{name}_{n}", shape, F32R) for n in ("hi", "lo")]
        up_w = parts("up_w", [P, DT, HID0])
        down_w = parts("down_w", [P, HT0, D])
        x = parts("x", [P, 2, DT, CH])
        g = parts("g", [P, 2, HT0, CH])
        gel = s.sb("gel", [P, STAGED, CH])
        hid = s.ps("hid", [P, 4, CH])
        ps = s.ps("ps", [P, 2, CH])
        made = s.sem("made")
        gelued = s.sem("gelued")
        out_done = s.sem("out_done")
        added = s.sem("added")
        leading = s.sem("leading")
        w_split, x_split, g_split = s.sem("w_split"), s.sem("x_split"), s.sem("g_split")
        norm = Norm(s, resid, hn, ones_mean, eps, 1, (added, lambda c: DT * (c + 1)))
        block = s.block()
        TERMS = ((0, 0), (1, 0), (0, 1))

        @block.tensor
        def _(pe):
            def up(c):
                pe.wait_ge(x_split, c + 1)
                for j in range(HT0):
                    if j == 2 and c >= 2:
                        norm.mean(pe, c - 2)
                    n = c * HT0 + j
                    if n >= 4:
                        pe.wait_ge(gelued, n - 3)
                    if c == 0 and j % 4 == 0:
                        pe.wait_ge(w_split, j // 4 + 1)
                    products = [(k, term) for k in range(DT) for term in TERMS]
                    for i, (k, (a, b)) in enumerate(products):
                        last = pe.matmul(hid[:, n % 4, :], up_w[a][:, k, j * P:(j + 1) * P], x[b][:, c % 2, k, :],
                                         start=i == 0, stop=i == len(products) - 1)
                    last.then_inc(made, 1)

            def down(c):
                for m in range(DT):
                    if m == 1 and c >= 1:
                        norm.variance(pe, c - 1)
                    n = c * DT + m
                    if n >= 2:
                        pe.wait_ge(added, n - 1)
                    if n == 0:
                        pe.wait_ge(w_split, 4)
                    products = [(j, term) for j in range(HT0) for term in TERMS]
                    for i, (j, (a, b)) in enumerate(products):
                        if m == 0 and i % len(TERMS) == 0:
                            pe.wait_ge(g_split, c * HT0 + j + 1)
                        last = pe.matmul(ps[:, m, :], down_w[a][:, j, m * P:(m + 1) * P], g[b][:, c % 2, j, :],
                                         start=i == 0, stop=i == len(products) - 1)
                    last.then_inc(out_done, 1)

            up(0)
            for c in range(1, NCH):
                up(c)
                down(c - 1)
            norm.mean(pe, NCH - 2)
            down(NCH - 1)
            norm.mean(pe, NCH - 1)
            norm.variance(pe, NCH - 1)

        @block.scalar
        def _(act):
            for n in range(NCH * HT0):
                c, j = divmod(n, HT0)
                act.wait_ge(made, n + 1)
                if n >= STAGED:
                    act.wait_ge(g_split, n - STAGED + 1)
                act.activation(gel[:, n % STAGED, :], hid[:, n % 4, :], ACT.Gelu, bias=b_up[:, j:j + 1]).then_inc(gelued, 1)
                if c >= 2 and j == HT0 // 2:
                    norm.square(act, c - 2)
                if c >= 2 and j == HT0 - 1:
                    norm.root(act, c - 2)
            for c in range(NCH - 2, NCH):
                norm.square(act, c)
                norm.root(act, c)

        @block.vector
        def _(dve):
            count = 0

            def split(dst, at, src, done):
                nonlocal count
                count += 1
                dve.tensor_copy(dst[0][at], src).then_inc(leading, 1)
                dve.wait_ge(leading, count)
                dve.tensor_tensor(dst[1][at], src, dst[0][at].bitcast(F32), ALU.subtract).then_inc(done, 1)

            def split_x(c):
                if c >= 2:
                    dve.wait_ge(made, (c - 1) * HT0)
                split(x, (slice(None), c % 2), hn[:, :, c * CH:(c + 1) * CH], x_split)

            def add(n):
                c, m = divmod(n, DT)
                dve.wait_ge(out_done, n + 1)
                part = resid[:, m, c * CH:(c + 1) * CH]
                dve.scalar_tensor_tensor(part, ps[:, m, :], b_out[:, m:m + 1], part, ALU.add, ALU.add).then_inc(added, 1)

            split_x(0)
            for i in range(2):
                half = (slice(None), slice(None), slice(i * CH, (i + 1) * CH))
                split(up_w, half, w_up[half], w_split)
            for c in range(NCH + 1):
                if c + 1 < NCH:
                    split_x(c + 1)
                for j in range(HT0):
                    if c < NCH:
                        n = c * HT0 + j
                        dve.wait_ge(gelued, n + 1)
                        if c >= 2:
                            dve.wait_ge(out_done, DT * (c - 1))
                        split(g, (slice(None), c % 2, j), gel[:, n % STAGED, :], g_split)
                    if c == 0 and j in (3, 6):
                        half = (slice(None), slice(j // 6 * HT0 // 2, (j // 6 + 1) * HT0 // 2))
                        split(down_w, half, w_down[half], w_split)
                    if c >= 2 and j == 3:
                        norm.centre(dve, c - 2)
                if c:
                    for m in range(DT):
                        add(DT * (c - 1) + m)
                if c >= 2:
                    norm.invert(dve, c - 2)
            norm.centre(dve, NCH - 1)
            norm.invert(dve, NCH - 1)

        @block.gpsimd
        def _(pool):
            norm.scale_all(pool)



UNITS = 2 * PAIRS
QK_SCALE = 8.0
LAYERS = 2
HALF = DH // 2
INV_LOW = 32
INV_ROWS = INV_LOW + 2 * UNITS
NLOADS = 23
WPC = CH // WIN
SLOTS = WPC * PAIRS
CONTRACT_AT = (1, SLOTS + 1)
KW = CH + WIN
MIDDLE = [("V", 0), ("V", 1), ("V", 2), ("V", 3), ("B", 0), ("E", 0), ("B", 1), ("E", 1), ("B", 2), ("E", 2), ("B", 3), ("B", 4), ("E", 3), ("B", 5), ("E", 4), ("B", 6), ("E", 5), ("B", 7)]
RING_USES = [("P", j) for j in range(UNITS)] + [step for step in MIDDLE if step[0] != "E"] + [("O", m) for m in range(DT)]
RING = len(RING_USES)
BACK_AG = 2
BACK_Y = BACK_AG + 2 * HT1
BACK = BACK_Y + DT


def layer_phase(nc, tag, a, l, wqkv, y, y_mid, cst, ident, ones_mean, eps):
    with Scope(nc, tag) as s:
        PB = 3
        wo = s.sb("wo", [P, PAIRS, D])
        w1 = s.sb("w1", [P, DT, 2 * HID1])
        w2 = s.sb("w2", [P, HT1, D])
        b1 = s.sb("b1", [P, 2, HT1])
        b2 = s.sb("b2", [P, DT])
        ln_g = s.sb("ln_g", [P, DT])
        ln_b = s.sb("ln_b", [P, DT])
        scales = s.sb("scales", [P, 2, 2])
        table = s.sb("table", [P, 4, CH])
        raw = s.sb("raw", [P, UNITS, CH])
        sq = s.sb("sq", [P, 2, CH])
        norm = sq[0:2 * UNITS, 0, :]
        inv_parts = s.sb("inv_parts", [INV_ROWS, CH], F32R)
        t_cos = s.sb("t_cos", [P, 2, CH])
        t_sin = s.sb("t_sin", [P, 2, CH])
        qr = s.sb("qr", [P, PAIRS, 2, CH])
        kr = s.sb("kr", [P, PAIRS, KW])
        v = s.sb("v", [P, WPC + 1, INNER])
        mx = s.sb("mx", [P, 4, 2])
        neg = s.sb("neg", [P, 4, 2])
        den = s.sb("den", [P, 4, 2])
        rden = s.sb("rden", [P, 4, 2])
        probs = s.sb("probs", [P, PB, 2, 2 * WIN])
        probs_t = s.sb("probs_t", [P, PB, 4, WIN])
        o = s.sb("o", [P, PAIRS, CH])
        hn = s.sb("hn", [P, DT, CH])
        std = s.sb("std", [P, CH])
        gel = s.sb("gel", [P, 2, CH])
        hid = s.sb("hid", [P, HT1, CH])
        y_stage = hid[:, HT1 - DT:HT1, :]
        ring = s.ps("ring", [P, 2, CH])
        st = s.ps("st", [P, 2, 2, 2 * WIN])
        tp = s.ps("tp", [P, 4, WIN])
        ov = s.ps("ov", [P, PAIRS, WIN])
        back = s.ps("back", [P, 2, CH])
        sem = s.sem
        w_in, v_zero, table_in = sem("w_in"), sem("v_zero"), sem("table_in")
        ring_full, st_full, tp_full, av_done = sem("ring_full"), sem("st_full"), sem("tp_full"), sem("av_done")
        n2_part = sem("n2_part")
        raw_copied, squared, v_copied, norm_done = sem("raw_copied"), sem("squared"), sem("v_copied"), sem("norm_done")
        exped, pt_copied, o_copied = sem("exped"), sem("pt_copied"), sem("o_copied")
        clipped, rnormed, sin_done, qk_done = sem("clipped"), sem("rnormed"), sem("sin_done"), sem("qk_done")
        maxed, negged, inverted, p_normed, mid_done = sem("maxed"), sem("negged"), sem("inverted"), sem("p_normed"), sem("mid_done")
        turned_in = [sem(f"turned_in{i}") for i in range(2)]
        qkv_in = sem("qkv_in")
        inv_split, inv_zero = sem("inv_split"), sem("inv_zero")
        cos_done, rotated, kv_moved, staged, table_scaled = sem("cos_done"), sem("rotated"), sem("kv_moved"), sem("staged"), sem("table_scaled")
        back_full, hsquared, std_done, gelued = sem("back_full"), sem("hsquared"), sem("std_done"), sem("gelued")
        centred, inv_std, scaled, affined, gated, y_done = sem("centred"), sem("inv_std"), sem("scaled"), sem("affined"), sem("gated"), sem("y_done")
        block = s.block()

        def iterations(eng, body):
            body(0, None)
            with eng.Fori(1, NCH) as c:
                body(c, c - 1)
            body(None, NCH - 1)

        def ring_free(pe, c, pos):
            if pos < 2:
                if isinstance(c, int) and c == 0:
                    return
                pe.wait_ge(mid_done, DT * c + pos - 1)
            else:
                kind, n = RING_USES[pos - 2]
                sem, count = {"P": (squared, UNITS), "V": (v_copied, WPC), "B": (qk_done, UNITS)}[kind]
                pe.wait_ge(sem, count * c + n + 1)

        def back_free(pe, c, pos):
            if pos < 2:
                pe.wait_ge(y_done, DT * c + pos + 1)
            elif pos == 2:
                pe.wait_ge(centred, DT * (c + 1))
            elif pos == 3:
                pe.wait_ge(std_done, c + 1)
            else:
                j, i = divmod(pos - 2 - BACK_AG, 2)
                pe.wait_ge(gated if i else gelued, HT1 * c + j + 1)

        def toks(c, shifted):
            return bass.ds(c * CH + (0 if shifted else 1), CH)

        @block.sync
        def _(sp):
            slow = dict(allow_slow_non_contiguous=True)
            loads = [(wo[:, :, :], a["L1_ffn_wo"][l].rearrange("(k p) n -> p k n", p=P), {}),
                     (w1[:, :, :], a["L1_ffn_w1"][l].rearrange("(k p) n -> p k n", p=P), {}),
                     (w2[:, 0:HT1 - 1, :], a["L1_ffn_w2"][l, 0:(HT1 - 1) * P, :].rearrange("(k p) n -> p k n", p=P), {}),
                     (w2[0:LASTH, HT1 - 1, :], a["L1_ffn_w2"][l, (HT1 - 1) * P:HID1, :], {})]
            for i in range(2):
                bv = a["L1_ffn_b1"][l, i * HID1:(i + 1) * HID1]
                loads += [(b1[:, i, 0:HT1 - 1], bv[0:(HT1 - 1) * P].rearrange("(k p) -> p k", p=P), slow),
                          (b1[0:LASTH, i, HT1 - 1:HT1], bv[(HT1 - 1) * P:HID1].rearrange("(p a) -> p a", a=1), {})]
            for t, n in ((b2, "b2"), (ln_g, "ln_g"), (ln_b, "ln_b")):
                loads.append((t[:, :], a["L1_ffn_" + n][l].rearrange("(k p) -> p k", p=P), slow))
            for i, n in enumerate(("L1_ffn_q_scale", "L1_ffn_k_scale")):
                sv = a[n][l].rearrange("(p a) -> p a", a=1)
                for h in range(2):
                    r = h * DH
                    loads += [(scales[r:r + DH, i, 0:1], sv, {}),
                              (scales[r:r + DH // 2, i, 1:2], sv[DH // 2:DH], {}),
                              (scales[r + DH // 2:r + DH, i, 1:2], sv[0:DH // 2], {})]
            for dst, src, kw in loads:
                sp.dma_start(dst, src, **kw).then_inc(w_in, 16)
            assert len(loads) == NLOADS
            for c in range(NCH):
                if c:
                    sp.wait_ge(qk_done, UNITS * c)
                sp.dma_start(table[:, :, :], cst["tables"][:, :, c * CH:(c + 1) * CH]).then_inc(table_in, 16)
                for j in range(UNITS):
                    sp.wait_ge(raw_copied, UNITS * c + j + 1)
                    if j >= 2 or c:
                        sp.wait_ge(rotated, UNITS * c + j - 1)
                    for r in range(0, P, HALF):
                        src = r + HALF if r % DH == 0 else r - HALF
                        sp.dma_start(t_sin[r:r + HALF, j % 2, :], raw[src:src + HALF, j, :]).then_inc(turned_in[j % 2], 16)
            if l + 1 < LAYERS:
                sp.wait_ge(v_copied, WPC * NCH)
                sp.dma_start(wqkv[:, :, :], a["L1_ffn_wqkv"][l + 1].rearrange("(k p) n -> p k n", p=P)).then_inc(qkv_in, 16)
                sp.wait_ge(qkv_in, 16)


        @block.tensor
        def _(pe):
            def project(c, j):
                ring_free(pe, c, j)
                for k in range(DT):
                    last = pe.matmul(ring[:, j % 2, :], wqkv[:, k, j * P:(j + 1) * P], y[:, k, toks(c, k)],
                                     start=k == 0, stop=k == DT - 1)
                last.then_inc(ring_full, 1)

            def norm_sum(c, j):
                pe.wait_ge(squared, UNITS * c + j + 1)
                if j == 0 and not (isinstance(c, int) and c == 0):
                    pe.wait_ge(o_copied, WPC * c)
                last = pe.matmul(ov[0:2 * UNITS, :, :].rearrange("p m q -> p (m q)"), cst["sel"][:, j, :], sq[:, j % 2, :],
                                 start=j == 0, stop=j == UNITS - 1)
                last.then_inc(n2_part, 1)

            def values(c, t):
                pos = RING_USES.index(("V", t))
                ring_free(pe, c, pos)
                for k in range(DT):
                    pe_in = y_stage[:, k, t * P:(t + 1) * P]
                    last = pe.matmul(ring[:, pos % 2, :], pe_in, wqkv[:, k, 2 * INNER:3 * INNER],
                                     start=k == 0, stop=k == DT - 1)
                last.then_inc(ring_full, 1)

            def spread_inverse(c, j):
                pos = RING_USES.index(("B", j))
                ring_free(pe, c, pos)
                if j == 0:
                    pe.wait_ge(inv_split, 2 * (c + 1))
                pe.matmul(ring[:, pos % 2, :], cst["sel_t"][:, j, :], inv_parts[:, :], start=True, stop=True).then_inc(ring_full, 1)

            def scores(c, u):
                w, m = divmod(u, PAIRS)
                first = isinstance(c, int) and c == 0
                if w == 0:
                    pe.wait_ge(qk_done, UNITS * c + PAIRS + m + 1)
                if u >= 2 or not first:
                    pe.wait_ge(exped, SLOTS * c + u - 1)
                mask = cst["mask_first"] if first and w == 0 else cst["mask"]
                bank = st[:, u % 2, :, :]
                pe.matmul(bank.rearrange("p h k -> p (h k)"), cst["ident_b"][:, :], mask[:, :], start=True, stop=True)
                for h in range(2):
                    last = pe.matmul(bank[:, h, :], qr[:, m, h, w * WIN:(w + 1) * WIN], kr[:, m, w * WIN:(w + 2) * WIN],
                                     start=False, stop=True, skip_group_check=True)
                last.then_inc(st_full, 1)

            def turn(c, u):
                pe.wait_ge(p_normed, SLOTS * c + u + 1)
                if u or not (isinstance(c, int) and c == 0):
                    pe.wait_ge(pt_copied, SLOTS * c + u)
                for i in range(4):
                    last = pe.transpose(tp[:, i, :], probs[:, u % PB, i // 2, (i % 2) * WIN:(i % 2 + 1) * WIN], ident[:, :])
                last.then_inc(tp_full, 1)

            def weigh(c, u):
                w, m = divmod(u, PAIRS)
                pe.wait_ge(pt_copied, SLOTS * c + u + 1)
                if u == 0:
                    pe.wait_ge(v_copied, WPC * (c + 1))
                    pe.wait_ge(norm_done, c + 1)
                elif m == 0:
                    pe.wait_ge(o_copied, WPC * c + w)
                for h in range(2):
                    for i in range(2):
                        last = pe.matmul(ov[h * DH:(h + 1) * DH, m, :], v[:, w + i, (2 * m + h) * DH:(2 * m + h + 1) * DH],
                                         probs_t[:, u % PB, 2 * h + i, :], start=i == 0, stop=i == 1)
                last.then_inc(av_done, 1)

            def output(c, m):
                if isinstance(c, int) and m == 0:
                    pe.wait_ge(w_in, 16 * NLOADS)
                pos = RING_USES.index(("O", m))
                ring_free(pe, c, pos)
                pe.wait_ge(o_copied, WPC * (c + 1))
                for k in range(PAIRS):
                    last = pe.matmul(ring[:, pos % 2, :], wo[:, k, m * P:(m + 1) * P], o[:, k, :], start=k == 0, stop=k == PAIRS - 1)
                last.then_inc(ring_full, 1)

            def mean(c):
                pe.wait_ge(mid_done, DT * (c + 1))
                back_free(pe, c, 0)
                for k in range(DT):
                    last = pe.matmul(back[:, 0, :], ones_mean[:, :], y_mid[:, k, toks(c, k)], start=k == 0, stop=k == DT - 1)
                last.then_inc(back_full, 1)

            def variance(c):
                pe.wait_ge(hsquared, c + 1)
                back_free(pe, c, 1)
                for k in range(DT):
                    last = pe.matmul(back[:, 1, :], ones_mean[:, :], gel[:, k, :], start=k == 0, stop=k == DT - 1)
                last.then_inc(back_full, 1)

            def expand(c, j):
                n = hid_rows(j)
                if j == 0:
                    pe.wait_ge(affined, DT * (c + 1))
                for i in range(2):
                    back_free(pe, c, BACK_AG + 2 * j + i)
                    col = (1 - i) * HID1 + j * P
                    for k in range(DT):
                        last = pe.matmul(back[0:n, i, :], w1[:, k, col:col + n], hn[:, k, :], start=k == 0, stop=k == DT - 1)
                    last.then_inc(back_full, 1)

            def contract(c, m):
                back_free(pe, c, BACK_Y + m)
                pe.wait_ge(gated, HT1 * (c + 1))
                for j in range(HT1):
                    n = hid_rows(j)
                    last = pe.matmul(back[:, m, :], w2[0:n, j, m * P:(m + 1) * P], hid[0:n, j, :], start=j == 0, stop=j == HT1 - 1)
                last.then_inc(back_full, 1)

            def body(f, b):
                if f is None:
                    mean(b)
                if f is not None:
                    for j in range(UNITS):
                        project(f, j)
                        if j:
                            norm_sum(f, j - 1)
                        if j == 0 and b is not None:
                            mean(b)
                        if j == 3 and b is not None:
                            variance(b)
                    norm_sum(f, UNITS - 1)
                    pe.wait_ge(staged, DT * (f + 1))
                if f is None:
                    variance(b)
                for kind, n in MIDDLE:
                    if kind == "E" and b is not None:
                        expand(b, n)
                    if kind == "V" and f is not None:
                        values(f, n)
                    if kind == "B" and f is not None:
                        spread_inverse(f, n)
                if f is not None:
                    for u in range(SLOTS + 4):
                        if u < SLOTS:
                            scores(f, u)
                        if u >= 4:
                            weigh(f, u - 4)
                        if 2 <= u <= SLOTS + 1:
                            turn(f, u - 2)
                        if b is not None and u in CONTRACT_AT:
                            contract(b, CONTRACT_AT.index(u))
                    for m in range(DT):
                        output(f, m)
                else:
                    for m in range(DT):
                        contract(b, m)

            iterations(pe, body)

        @block.scalar
        def _(act):
            def scale_table(c):
                act.wait_ge(table_in, 16 * (c + 1))
                for i in range(2):
                    act.activation(table[:, 2 * i, :], table[:, 2 * i, :], ACT.Copy, scale=scales[:, i, 0:1]).then_inc(table_scaled, 1)

            def root_variance(c):
                act.wait_ge(back_full, BACK * c + 2)
                act.activation(std[:, :], back[:, 1, :], ACT.Sqrt, bias=eps[:, 0:1]).then_inc(std_done, 1)

            def body(f, b):
                if f is not None:
                    if b is not None:
                        scale_table(f)
                    for j in range(UNITS):
                        act.wait_ge(ring_full, RING * f + j + 1)
                        if j == 0 and not (isinstance(f, int) and f == 0):
                            act.wait_ge(qk_done, UNITS * f)
                        act.activation(raw[:, j, :], ring[:, j % 2, :], ACT.Copy).then_inc(raw_copied, 1)
                        if j >= 2:
                            act.wait_ge(n2_part, UNITS * f + j - 1)
                        act.activation(sq[:, j % 2, :], ring[:, j % 2, :], ACT.Square).then_inc(squared, 1)
                        if b is not None and j == 4:
                            root_variance(b)
                        if b is not None and j == 2:
                            act.wait_ge(centred, DT * (b + 1))
                            act.activation(gel[:, :, :], hn[:, :, :], ACT.Square).then_inc(hsquared, 1)
                    if b is None:
                        act.wait_ge(w_in, 16 * NLOADS)
                        scale_table(f)
                    act.wait_ge(n2_part, UNITS * (f + 1))
                    act.activation(norm, ov[0:2 * UNITS, :, :].rearrange("p m q -> p (m q)"), ACT.Sqrt).then_inc(norm_done, 1)
                else:
                    act.wait_ge(centred, DT * (b + 1))
                    act.activation(gel[:, :, :], hn[:, :, :], ACT.Square).then_inc(hsquared, 1)
                    root_variance(b)
                for kind, n in MIDDLE:
                    if kind == "V" and f is not None:
                        pos = RING_USES.index(("V", n))
                        act.wait_ge(ring_full, RING * f + pos + 1)
                        if n == 0 and not (isinstance(f, int) and f == 0):
                            act.wait_ge(kv_moved, 2 * f)
                        act.activation(v[:, n + 1, :], ring[:, pos % 2, :], ACT.Copy).then_inc(v_copied, 1)
                    if kind == "E" and b is not None:
                        rows = hid_rows(n)
                        act.wait_ge(back_full, BACK * b + BACK_AG + 2 * n + 1)
                        if n >= 2:
                            act.wait_ge(gated, HT1 * b + n - 1)
                        act.activation(gel[0:rows, n % 2, :], back[0:rows, 0, :], ACT.Gelu, bias=b1[0:rows, 1, n:n + 1]).then_inc(gelued, 1)
                if f is not None:
                    first = isinstance(f, int) and f == 0
                    for u in range(SLOTS + 4):
                        if u < SLOTS:
                            act.wait_ge(negged, SLOTS * f + u + 1)
                            if u >= PB or not first:
                                act.wait_ge(tp_full, SLOTS * f + max(u - PB + 1, 0))
                            if u >= 4 or not first:
                                act.wait_ge(inverted, SLOTS * f + u - 3)
                            for h in range(2):
                                last = act.activation(probs[:, u % PB, h, :], st[:, u % 2, h, :], ACT.Exp, scale=QK_SCALE,
                                                      bias=neg[:, u % 4, h:h + 1], accum_out=den[:, u % 4, h:h + 1])
                            last.then_inc(exped, 1)
                        if u >= 4 and (u - 4) % PAIRS == PAIRS - 1:
                            w = (u - 4) // PAIRS
                            act.wait_ge(av_done, SLOTS * f + u - 3)
                            act.activation(o[:, :, w * WIN:(w + 1) * WIN], ov[:, :, :], ACT.Copy).then_inc(o_copied, 1)
                        if 2 <= u <= SLOTS + 1:
                            t = u - 2
                            act.wait_ge(tp_full, SLOTS * f + t + 1)
                            if t >= PB or not first:
                                act.wait_ge(av_done, SLOTS * f + max(t - PB + 1, 0))
                            act.activation(probs_t[:, t % PB, :, :], tp[:, :, :], ACT.Copy).then_inc(pt_copied, 1)
                    act.activation(kr[:, :, 0:WIN], kr[:, :, CH:KW], ACT.Copy).then_inc(kv_moved, 1)
                    act.activation(v[:, 0, :], v[:, WPC, :], ACT.Copy).then_inc(kv_moved, 1)

            iterations(act, body)

        @block.vector
        def _(dve):
            def sine(c, j):
                i = j // PAIRS
                dve.wait_ge(turned_in[j % 2], 64 * (UNITS // 2 * c + j // 2 + 1))
                dve.scalar_tensor_tensor(t_sin[:, j % 2, :], t_sin[:, j % 2, :], scales[:, i, 1:2],
                                         table[:, 2 * i + 1, :], ALU.mult, ALU.mult).then_inc(sin_done, 1)

            def body(f, b):
                if b is not None:
                    dve.wait_ge(back_full, BACK * b + 1)
                    for k in range(DT):
                        dve.tensor_tensor(hn[:, k, :], y_mid[:, k, toks(b, k)], back[:, 0, :], ALU.subtract).then_inc(centred, 1)
                if b is not None:
                    dve.wait_ge(std_done, b + 1)
                    dve.reciprocal(std[:, :], std[:, :]).then_inc(inv_std, 1)
                    dve.wait_ge(inv_std, b + 1)
                    dve.wait_ge(hsquared, b + 1)
                    for k in range(DT):
                        dve.scalar_tensor_tensor(hn[:, k, :], hn[:, k, :], ln_g[:, k:k + 1], std[:, :], ALU.mult, ALU.mult).then_inc(scaled, 1)
                    for k in range(DT):
                        dve.wait_ge(scaled, DT * b + k + 1)
                        dve.tensor_scalar(hn[:, k, :], hn[:, k, :], ln_b[:, k:k + 1], None, ALU.add).then_inc(affined, 1)
                if f is not None:
                    dve.wait_ge(norm_done, f + 1)
                    dve.tensor_scalar(norm, norm, 1e-12, None, ALU.max).then_inc(clipped, 1)
                    dve.wait_ge(clipped, f + 1)
                    dve.reciprocal(norm, norm).then_inc(rnormed, 1)
                    dve.wait_ge(rnormed, f + 1)
                    head = inv_parts[0:2 * UNITS, :]
                    dve.tensor_copy(head, norm).then_inc(inv_split, 1)
                    dve.wait_ge(inv_split, 2 * f + 1)
                    dve.tensor_tensor(inv_parts[INV_LOW:INV_ROWS, :], norm, head.bitcast(F32), ALU.subtract).then_inc(inv_split, 1)
                for kind, j in MIDDLE:
                    if kind == "B" and f is not None:
                        if j == 0:
                            dve.wait_ge(table_in, 16 * (f + 1))
                            if not (isinstance(f, int) and f == 0):
                                dve.wait_ge(kv_moved, 2 * f)
                            sine(f, 0)
                        if j + 1 < UNITS:
                            sine(f, j + 1)
                        pos = RING_USES.index(("B", j))
                        dve.wait_ge(ring_full, RING * f + pos + 1)
                        dve.wait_ge(rotated, UNITS * f + j + 1)
                        if j < PAIRS:
                            for h in range(2):
                                rows = slice(h * DH, (h + 1) * DH)
                                last = dve.tensor_tensor(qr[rows, j, h, :], t_cos[rows, j % 2, :], ring[rows, pos % 2, :], ALU.mult)
                        else:
                            last = dve.tensor_tensor(kr[:, j - PAIRS, WIN:KW], t_cos[:, j % 2, :], ring[:, pos % 2, :], ALU.mult)
                        last.then_inc(qk_done, 1)
                    if kind == "E" and b is not None:
                        n = hid_rows(j)
                        dve.wait_ge(gelued, HT1 * b + j + 1)
                        dve.wait_ge(back_full, BACK * b + BACK_AG + 2 * j + 2)
                        dve.scalar_tensor_tensor(hid[0:n, j, :], back[0:n, 1, :], b1[0:n, 0, j:j + 1], gel[0:n, j % 2, :],
                                                 ALU.add, ALU.mult).then_inc(gated, 1)

                def finish(m):
                    dve.wait_ge(back_full, BACK * b + BACK_Y + m + 1)
                    dve.scalar_tensor_tensor(y[:, m, toks(b, 0)], back[:, m, :], b2[:, m:m + 1], y_mid[:, m, toks(b, 0)],
                                             ALU.add, ALU.add).then_inc(y_done, 1)
                if f is not None:
                    for u in range(SLOTS + 4):
                        if u < SLOTS:
                            dve.wait_ge(st_full, SLOTS * f + u + 1)
                            dve.reduce_max(mx[:, u % 4, :], st[:, u % 2, :, :], AX.X).then_inc(maxed, 1)
                            dve.wait_ge(maxed, SLOTS * f + u + 1)
                            dve.tensor_scalar(neg[:, u % 4, :], mx[:, u % 4, :], -QK_SCALE, None, ALU.mult).then_inc(negged, 1)
                        if 1 <= u <= SLOTS:
                            t = u - 1
                            dve.wait_ge(exped, SLOTS * f + t + 1)
                            dve.reciprocal(rden[:, t % 4, :], den[:, t % 4, :]).then_inc(inverted, 1)
                            dve.wait_ge(inverted, SLOTS * f + t + 1)
                            dve.tensor_tensor(probs[:, t % PB, :, :], probs[:, t % PB, :, :],
                                              rden[:, t % 4, :].unsqueeze(2).broadcast_to([P, 2, 2 * WIN]), ALU.mult).then_inc(p_normed, 1)
                        if b is not None and u - 2 in CONTRACT_AT:
                            finish(CONTRACT_AT.index(u - 2))
                    for m in range(DT):
                        dve.wait_ge(ring_full, RING * f + RING_USES.index(("O", m)) + 1)
                        dve.tensor_tensor(y_mid[:, m, toks(f, 0)], ring[:, RING_USES.index(("O", m)) % 2, :], y[:, m, toks(f, 0)],
                                          ALU.add).then_inc(mid_done, 1)
                else:
                    for m in range(DT):
                        finish(m)

            dve.sem_inc(y_done, DT)
            for h in range(2):
                other = slice((1 - h) * DH, (2 - h) * DH)
                dve.memset(qr[other, :, h, :], 0.0)
            dve.memset(inv_parts[:, :].bitcast(F32), 0.0).then_inc(inv_zero, 1)
            dve.wait_ge(inv_zero, 1)
            dve.wait_ge(w_in, 16 * NLOADS)
            iterations(dve, body)

        @block.gpsimd
        def _(pool):
            def body(f, b):
                if f is None:
                    return
                first = isinstance(f, int) and f == 0
                if not first:
                    pool.wait_ge(y_done, DT * f)
                for k in range(DT):
                    pool.tensor_copy(y_stage[:, k, :], y[:, k, toks(f, k)]).then_inc(staged, 1)
                pool.wait_ge(table_scaled, 2 * (f + 1))
                for j in range(UNITS):
                    i = j // PAIRS
                    pool.wait_ge(raw_copied, UNITS * f + j + 1)
                    if j >= 2 or not first:
                        pool.wait_ge(qk_done, UNITS * f + j - 1)
                    pool.tensor_tensor(t_cos[:, j % 2, :], raw[:, j, :], table[:, 2 * i, :], ALU.mult).then_inc(cos_done, 1)
                    pool.wait_ge(cos_done, UNITS * f + j + 1)
                    pool.wait_ge(sin_done, UNITS * f + j + 1)
                    pool.tensor_tensor(t_cos[:, j % 2, :], t_cos[:, j % 2, :], t_sin[:, j % 2, :], ALU.add).then_inc(rotated, 1)

            pool.memset(kr[:, :, 0:WIN], 0.0).then_inc(v_zero, 1)
            pool.memset(v[:, 0, :], 0.0).then_inc(v_zero, 1)
            pool.wait_ge(v_zero, 2)
            iterations(pool, body)


def tables():
    t = np.arange(NQ, dtype=np.float32)
    half = np.arange(0, DH, 2, dtype=np.float32)
    freqs = t[:, None] * (np.float32(1.0) / np.float32(10000.0) ** (half / np.float32(DH)))[None, :]
    base = (half + np.float32(0.4 * DH)) / np.float32(1.4 * DH)
    power = (t - NQ // 2) / np.float32(WIN // 2)
    xpos = base[None, :] ** power[:, None]
    four = [np.cos(freqs) * xpos, np.sin(freqs) * xpos, np.cos(freqs) / xpos, np.sin(freqs) / xpos]
    rotary = np.stack([np.tile(m.T, (4, 1)) for m in four], axis=1).astype(np.float32)
    rotary[np.arange(P) % DH < HALF, 1::2] *= -1.0
    i, j = np.arange(WIN)[:, None], np.arange(2 * WIN)[None, :] - WIN
    band = np.where((i < j) | (i > j + WIN), NEG, 0.0).astype(np.float32)
    first = np.where((i < j) | (j < 0), NEG, 0.0).astype(np.float32)
    masks = np.stack([np.tile(band, (1, 2)), np.tile(first, (1, 2))], axis=1)
    p = np.arange(P)
    sel = np.zeros((P, UNITS, 2 * UNITS), np.float32)
    for u in range(UNITS):
        sel[p, u, 2 * u + p // DH] = 1.0
    sel_t = np.zeros((INV_ROWS, UNITS, P), np.float32)
    sel_t[0:2 * UNITS] = sel_t[INV_LOW:] = sel.transpose(2, 1, 0)
    perm = np.zeros((P, WITHIN, P), np.float32)
    pick = np.zeros((P, WITHIN, P), np.float32)
    for st in range(WITHIN):
        perm[p, st, p ^ (1 << st)] = 1.0
        pick[((p >> st) & 1) * (P // 2) + ((p >> (st + 1)) << st) + p % (1 << st), st, p] = 1.0
    return {"c_perm": perm, "c_pick": pick, "c_rotary": rotary, "c_masks": masks, "c_sel": sel, "c_sel_t": sel_t}


class Constants:

    def __init__(self, s, a, cst, y, y_mid, wqkv):
        self.a, self.cst, self.y, self.y_mid, self.wqkv = a, cst, y, y_mid, wqkv
        self.masks = s.sb("masks", [P, 2, 4 * WIN])
        self.sel_t = s.sb("sel_t", [INV_ROWS, UNITS, P])
        self.loaded, self.masks_in, self.sel_in, self.converted = [s.sem(n) for n in ("loaded", "masks_in", "sel_in", "converted")]

    def load(self, sp):
        sp.dma_start(self.sel_t[:, :, :], self.a["c_sel_t"]).then_inc(self.sel_in, 16)
        sp.dma_start(self.masks[:, :, :], self.a["c_masks"]).then_inc(self.masks_in, 16)
        sp.dma_start(self.cst["sel"][:, :, :], self.a["c_sel"]).then_inc(self.loaded, 16)
        sp.dma_start(self.wqkv[:, :, :], self.a["L1_ffn_wqkv"][0].rearrange("(k p) n -> p k n", p=P)).then_inc(self.loaded, 16)
        sp.wait_ge(self.loaded, 32)

    def convert_masks(self, pool):
        pool.memset(self.y[:, :, 0:1], 0.0).then_inc(self.converted, 1)
        pool.memset(self.y_mid[:, :, 0:1], 0.0).then_inc(self.converted, 1)
        pool.tensor_copy(self.cst["ident_b"][:, :], self.cst["ident"][:, :]).then_inc(self.converted, 1)
        pool.wait_ge(self.masks_in, 16)
        pool.tensor_copy(self.cst["mask"][:, :], self.masks[:, 0, :]).then_inc(self.converted, 1)
        pool.tensor_copy(self.cst["mask_first"][:, :], self.masks[:, 1, :]).then_inc(self.converted, 1)

    def convert_sel(self, dve):
        dve.wait_ge(self.sel_in, 16)
        dve.tensor_copy(self.cst["sel_t"][:, :, :], self.sel_t[:, :, :]).then_inc(self.converted, 1)


def gated_layers(nc, s, a, o_dram, resid, ident, ones_mean, eps):
    y = s.sb("y", [P, DT, NQ + 1])
    y_mid = s.sb("y_mid", [P, DT, NQ + 1])
    cst = {"sel": s.sb("sel", [P, UNITS, 2 * UNITS]),
           "sel_t": s.sb("sel_t", [INV_ROWS, UNITS, P], F32R), "mask": s.sb("mask", [P, 4 * WIN], BF16),
           "mask_first": s.sb("mask_first", [P, 4 * WIN], BF16), "ident_b": s.sb("ident_b", [P, P], BF16),
           "ident": ident, "tables": a["c_rotary"]}
    wqkv = s.sb("wqkv", [P, DT, 3 * INNER])
    output_phase(nc, "out1", o_dram, a["L1_xattn_Wout"], a["L1_xattn_bout"], resid, y[:, :, 1:NQ + 1], ones_mean, eps,
                 (a, cst, y, y_mid, wqkv))
    for l in range(LAYERS):
        layer_phase(nc, f"l{l}", a, l, wqkv, y, y_mid, cst, ident, ones_mean, eps)
    return y[:, :, 1:NQ + 1]


def store_phase(nc, a, b, ident, out):
    TX = NQ // P
    with Scope(nc, "store") as s:
        y = s.sb("y", [P, DT, NQ])
        o = s.sb("o", [P, TX, D])
        tp = s.ps("tp", [P, 8, 2, DT, P])
        summed = s.sem("summed")
        turned = s.sem("turned")
        copied = s.sem("copied")
        stored = s.sem("stored")
        block = s.block()

        @block.gpsimd
        def _(pool):
            for c in range(NCH):
                part = slice(c * CH, (c + 1) * CH)
                pool.tensor_tensor(y[:, :, part], a[:, :, part], b[:, :, part], ALU.add).then_inc(summed, 1)

        @block.tensor
        def _(pe):
            for n in range(TX // 2):
                pe.wait_ge(summed, n // 2 + 1)
                for j in range(2):
                    for k in range(DT):
                        t = 2 * n + j
                        last = pe.transpose(tp[:, n, j, k, :], y[:, k, t * P:(t + 1) * P], ident[:, :])
                last.then_inc(turned, 1)

        @block.vector
        def _(dve):
            for n in range(TX // 2):
                dve.wait_ge(turned, n + 1)
                dve.tensor_copy(o[:, 2 * n:2 * n + 2, :].rearrange("p j d -> p (j d)"),
                                tp[:, n, :, :, :].rearrange("p j k q -> p (j k q)")).then_inc(copied, 1)

        @block.sync
        def _(sp):
            ov = out.rearrange("b (t p) d -> p (b t) d", p=P)
            for n in range(4):
                sp.wait_ge(copied, 2 * (n + 1))
                sp.dma_start(ov[:, 4 * n:4 * n + 4, :], o[:, 4 * n:4 * n + 4, :]).then_inc(stored, 16)
            sp.wait_ge(stored, 64)


def transformer_kernel(nc, a, out):
    with Scope(nc, "all") as s:
        ident = s.sb("ident", [P, P])
        ones_mean = s.sb("ones_mean", [P, P])
        ones64 = s.sb("ones64", [P, DH])
        eps = s.sb("eps", [P, 1])
        resid = s.sb("resid", [P, DT, NQ])
        v_dram = nc.dram_tensor("v_scratch", (NC_, INNER // 2), F32, kind="Internal").ap()
        o_dram = nc.dram_tensor("o_scratch", (INNER, NQ), F32, kind="Internal").ap()

        with Scope(nc, "ctx") as s1:
            ctx_t = s1.sb("ctx_t", [P, 2, NC_ + 1])
            hn = s1.sb("hn", [P, DT, NQ])
            load_phase(nc, a["x"], a["ctx_768"], ident, ones_mean, ones64, eps, resid, ctx_t, hn)
            attention_phase(nc, "att0", hn, ctx_t, a["L0_xattn_Wq"], a["L0_xattn_Wk"], a["L0_xattn_Wv"], v_dram, o_dram, ident, ones64)
            with Scope(nc, "bf") as s2:
                w_up = s2.sb("w_up", [P, DT, HID0])
                w_down = s2.sb("w_down", [P, HT0, D])
                b_up = s2.sb("b_up", [P, HT0])
                b_out = s2.sb("b_out", [P, DT])
                butterfly_phase(nc, a, ident, w_up, b_up, w_down, b_out, o_dram, a["L0_xattn_Wo"], a["L0_xattn_bo"], resid)
                norm_phase(nc, "ln1", resid, hn, ones_mean, eps)
                butterfly_ffn_phase(nc, hn, w_up, b_up, w_down, b_out, resid, ones_mean, eps)
            attention_phase(nc, "att1", hn, ctx_t, a["L1_xattn_Wq"], a["L1_xattn_Wk"], a["L1_xattn_Wv"], v_dram, o_dram, ident, ones64)
        y = gated_layers(nc, s, a, o_dram, resid, ident, ones_mean, eps)
        store_phase(nc, resid, y, ident, out)


_INS = ["x", "ctx_768", "L0_xattn_Wq", "L0_xattn_Wk", "L0_xattn_Wv", "L0_xattn_Wo", "L0_xattn_bo",
        "L0_ffn_W_exp", "L0_ffn_b_exp", "L0_ffn_up_weights", "L0_ffn_up_bias", "L0_ffn_down_weights",
        "L0_ffn_W_con", "L0_ffn_b_con", "L0_ffn_down_bias",
        "L1_xattn_Wq", "L1_xattn_Wk", "L1_xattn_Wv", "L1_xattn_Wout", "L1_xattn_bout",
        "L1_ffn_wqkv", "L1_ffn_q_scale", "L1_ffn_k_scale", "L1_ffn_wo", "L1_ffn_ln_g", "L1_ffn_ln_b",
        "L1_ffn_w1", "L1_ffn_b1", "L1_ffn_w2", "L1_ffn_b2"]


def kernel(**inputs):
    import numpy as _np
    import concourse.bacc as _bacc
    from concourse import mybir as _mybir
    from concourse.bass_utils import run_bass_kernel_spmd as _run

    nc = _bacc.Bacc("TRN2", target_bir_lowering=False, num_devices=1)
    arrays, args = {}, {}
    given = {name: _np.ascontiguousarray(inputs[name]) for name in _INS}
    for name, value in {**given, **tables()}.items():
        arrays[f"in_{name}_dram"] = value
        args[name] = nc.dram_tensor(f"in_{name}_dram", value.shape, _mybir.dt.from_np(value.dtype), kind="ExternalInput").ap()
    out = nc.dram_tensor("out_dram", (1, NQ, D), _mybir.dt.float32, kind="ExternalOutput").ap()
    transformer_kernel(nc, args, out)
    return _run(nc, [arrays], core_ids=[0]).results[0]["out_dram"]
```
